# Optimizing a Trainium2 kernel written in Bass

```python
import numpy as np
import jax
import jax.numpy as jnp

def _softmax(x, axis=-1):
    return jax.nn.softmax(x, axis=axis)

def _gelu(x):
    return jax.nn.gelu(x, approximate=True)

def _silu(x):
    return jax.nn.silu(x)

def _sigmoid(x):
    return jax.nn.sigmoid(x)

def _layernorm(x, axis=-1, eps=1e-05):
    m = jnp.mean(x, axis=axis, keepdims=True)
    v = jnp.var(x, axis=axis, keepdims=True)
    return (x - m) / jnp.sqrt(v + eps)

def _scatter_add(tgt, idx, src, axis=0):
    return tgt.at[idx].add(src)

def _segment_sum(src, seg, n):
    return jax.ops.segment_sum(src, seg, n)
kernel_name = 'mk_gnn_resnorm_d4_gnn_r32_c24c62'

def setup_inputs(seed: int=0):
    np.random.seed(seed)
    _w = jnp.asarray

    def _rec_inputs():
        import jax
        import jax.numpy as jnp
        _gk = jax.random.key(seed)
        x = -0.0003713 + 1 * jax.random.normal(jax.random.fold_in(_gk, 1), (50000, 128), jnp.float32)
        src = jax.random.randint(jax.random.fold_in(_gk, 2), (25000,), 0, 50000, jnp.int32)
        dst = jnp.minimum((50000 * jax.random.uniform(jax.random.fold_in(_gk, 3), (25000,)) ** 2.0).astype(jnp.int32), 49999)
        _o = jnp.argsort(dst, stable=True)
        src = src[_o]
        dst = dst[_o]
        edge_weight1 = -0.000152433 + 0.999798 * jax.random.normal(jax.random.fold_in(_gk, 13), (25000, 1), jnp.float32)
        node_vec = jax.random.uniform(jax.random.fold_in(_gk, 14), (50000,), jnp.float32, 0.0, 0.999991)
        return (x, src, dst, edge_weight1, node_vec)
    x, src, dst, edge_weight1, node_vec = _rec_inputs()

    def _L0_gnn_setup():
        import jax, jax.numpy as jnp
        import numpy as np
        N = 3125
        E = 50000
        IN = 128
        HEADS = 8
        HID = 16
        NEG_SLOPE = 0.2
        key = jax.random.key(seed)
        k1, k2, k3, k4, k5 = jax.random.split(key, 5)
        x = jax.random.normal(k1, (N, IN), dtype=jnp.float32)
        edge_index = jax.random.randint(k2, (2, E), 0, N, dtype=jnp.int32)
        pos = jax.random.uniform(k3, (N,), dtype=jnp.float32)
        W = jax.random.normal(k4, (HEADS * HID, IN), dtype=jnp.float32) * 0.1
        att = jax.random.normal(k5, (1, HEADS, 2 * HID), dtype=jnp.float32) * 0.1
        return {'x': x, 'edge_index': edge_index, 'pos': pos, 'W': W, 'att': att}
    _L0_gnn_all = _L0_gnn_setup()
    _L0_gnn_in = {k: v for k, v in _L0_gnn_all.items() if k in ('W', 'att')}
    del _L0_gnn_all

    def _L1_gnn_setup():
        import jax, jax.numpy as jnp
        import numpy as np
        N, D, E = (50000, 128, 20000)

        def _spect_conv(x, edge_index, edge_attr, w, b):
            src, dst = (edge_index[0], edge_index[1])
            msg = edge_attr[:, 0:1] * x[src]
            h = jax.ops.segment_sum(msg, dst, num_segments=x.shape[0])
            return h @ w + b

        def _lin(x, w, b):
            return x @ w + b
        key = jax.random.key(seed)
        ks = jax.random.split(key, 24)
        inp = {'x': jax.random.normal(ks[0], (N, D), jnp.float32), 'edge_index': jax.random.randint(ks[1], (2, E), 0, N, dtype=jnp.int32), 'edge_attr': jax.random.normal(ks[2], (E, 1), jnp.float32)}
        names = ['fc11', 'fc12', 'fc13', 'conv1', 'fc21', 'fc22', 'fc23', 'conv2']
        for i, n in enumerate(names):
            inp[n + '_w'] = jax.random.normal(ks[3 + 2 * i], (D, D), jnp.float32) * 0.05
            inp[n + '_b'] = jax.random.normal(ks[4 + 2 * i], (D,), jnp.float32) * 0.01
        return inp
    _L1_gnn_all = _L1_gnn_setup()
    _L1_gnn_in = {k: v for k, v in _L1_gnn_all.items() if k in ('fc11_w', 'fc11_b', 'fc12_w', 'fc12_b', 'fc13_w', 'fc13_b', 'conv1_w', 'conv1_b', 'fc21_w', 'fc21_b', 'fc22_w', 'fc22_b', 'fc23_w', 'fc23_b', 'conv2_w', 'conv2_b')}
    del _L1_gnn_all

    def _L2_gnn_setup():
        import math
        import jax, jax.numpy as jnp
        import numpy as np
        N = 50000
        C = 128
        H = 8
        D = C // H
        E = 25000

        def _layernorm(x, g, b, eps=1e-05):
            mu = jnp.mean(x, axis=-1, keepdims=True)
            var = jnp.var(x, axis=-1, keepdims=True)
            return (x - mu) * jax.lax.rsqrt(var + eps) * g + b
        key = jax.random.key(seed)
        ks = jax.random.split(key, 12)
        s = 1.0 / math.sqrt(C)
        s4 = 1.0 / math.sqrt(4 * C)
        return {'x': jax.random.normal(ks[0], (N, C), dtype=jnp.float32), 'edge_index': jax.random.randint(ks[1], (2, E), 0, N, dtype=jnp.int64), 'Wq': jax.random.normal(ks[2], (C, C), dtype=jnp.float32) * s, 'Wk': jax.random.normal(ks[3], (C, C), dtype=jnp.float32) * s, 'Wv': jax.random.normal(ks[4], (C, C), dtype=jnp.float32) * s, 'Wo': jax.random.normal(ks[5], (C, C), dtype=jnp.float32) * s, 'bo': jnp.zeros((C,), dtype=jnp.float32), 'Wf1': jax.random.normal(ks[6], (C, 4 * C), dtype=jnp.float32) * s, 'bf1': jnp.zeros((4 * C,), dtype=jnp.float32), 'Wf2': jax.random.normal(ks[7], (4 * C, C), dtype=jnp.float32) * s4, 'bf2': jnp.zeros((C,), dtype=jnp.float32), 'g1': jnp.ones((C,), dtype=jnp.float32), 'b1': jnp.zeros((C,), dtype=jnp.float32), 'g2': jnp.ones((C,), dtype=jnp.float32), 'b2': jnp.zeros((C,), dtype=jnp.float32)}
    _L2_gnn_all = _L2_gnn_setup()
    _L2_gnn_in = {k: v for k, v in _L2_gnn_all.items() if k in ('Wq', 'Wk', 'Wv', 'Wo', 'bo', 'Wf1', 'bf1', 'Wf2', 'bf2', 'g1', 'b1', 'g2', 'b2')}
    del _L2_gnn_all

    def _L3_gnn_setup():
        import jax, jax.numpy as jnp
        import numpy as np
        N_NODES = 3125
        N_EDGES = 50000
        D_IN = 128
        D_H = 128
        D_OUT = 128

        def _sage_conv(h, src, dst, Ws, Wn, b):
            n = h.shape[0]
            msg = h[src]
            summed = jax.ops.segment_sum(msg, dst, num_segments=n)
            deg = jax.ops.segment_sum(jnp.ones(src.shape, h.dtype), dst, num_segments=n)
            neigh = summed / jnp.maximum(deg, 1.0)[:, None]
            return h @ Ws.T + neigh @ Wn.T + b
        key = jax.random.key(seed)
        ks = jax.random.split(key, 12)
        x = jax.random.normal(ks[0], (N_NODES, D_IN), dtype=jnp.float32)
        src = jax.random.randint(ks[1], (N_EDGES,), 0, N_NODES, dtype=jnp.int32)
        dst = jax.random.randint(ks[2], (N_EDGES,), 0, N_NODES, dtype=jnp.int32)

        def lin(k, dout, din):
            s = 1.0 / np.sqrt(din)
            return jax.random.uniform(k, (dout, din), jnp.float32, -s, s)
        Ws0 = lin(ks[3], D_H, D_IN)
        Wn0 = lin(ks[4], D_H, D_IN)
        b0 = jnp.zeros((D_H,), jnp.float32)
        Ws1 = lin(ks[5], D_H, D_H)
        Wn1 = lin(ks[6], D_H, D_H)
        b1 = jnp.zeros((D_H,), jnp.float32)
        Ws2 = lin(ks[7], D_OUT, D_H)
        Wn2 = lin(ks[8], D_OUT, D_H)
        b2 = jnp.zeros((D_OUT,), jnp.float32)
        return {'x': x, 'Ws0': Ws0, 'Wn0': Wn0, 'b0': b0, 'Ws1': Ws1, 'Wn1': Wn1, 'b1': b1, 'Ws2': Ws2, 'Wn2': Wn2, 'b2': b2, 'src': src, 'dst': dst}
    _L3_gnn_all = _L3_gnn_setup()
    _L3_gnn_in = {k: v for k, v in _L3_gnn_all.items() if k in ('Ws0', 'Wn0', 'b0', 'Ws1', 'Wn1', 'b1', 'Ws2', 'Wn2', 'b2')}
    del _L3_gnn_all
    return {'x': x, 'src': src, 'dst': dst, 'edge_weight1': edge_weight1, 'node_vec': node_vec, 'L0_gnn_W': _L0_gnn_in['W'], 'L0_gnn_att': _L0_gnn_in['att'], 'L1_gnn_fc11_w': _L1_gnn_in['fc11_w'], 'L1_gnn_fc11_b': _L1_gnn_in['fc11_b'], 'L1_gnn_fc12_w': _L1_gnn_in['fc12_w'], 'L1_gnn_fc12_b': _L1_gnn_in['fc12_b'], 'L1_gnn_fc13_w': _L1_gnn_in['fc13_w'], 'L1_gnn_fc13_b': _L1_gnn_in['fc13_b'], 'L1_gnn_conv1_w': _L1_gnn_in['conv1_w'], 'L1_gnn_conv1_b': _L1_gnn_in['conv1_b'], 'L1_gnn_fc21_w': _L1_gnn_in['fc21_w'], 'L1_gnn_fc21_b': _L1_gnn_in['fc21_b'], 'L1_gnn_fc22_w': _L1_gnn_in['fc22_w'], 'L1_gnn_fc22_b': _L1_gnn_in['fc22_b'], 'L1_gnn_fc23_w': _L1_gnn_in['fc23_w'], 'L1_gnn_fc23_b': _L1_gnn_in['fc23_b'], 'L1_gnn_conv2_w': _L1_gnn_in['conv2_w'], 'L1_gnn_conv2_b': _L1_gnn_in['conv2_b'], 'L2_gnn_Wq': _L2_gnn_in['Wq'], 'L2_gnn_Wk': _L2_gnn_in['Wk'], 'L2_gnn_Wv': _L2_gnn_in['Wv'], 'L2_gnn_Wo': _L2_gnn_in['Wo'], 'L2_gnn_bo': _L2_gnn_in['bo'], 'L2_gnn_Wf1': _L2_gnn_in['Wf1'], 'L2_gnn_bf1': _L2_gnn_in['bf1'], 'L2_gnn_Wf2': _L2_gnn_in['Wf2'], 'L2_gnn_bf2': _L2_gnn_in['bf2'], 'L2_gnn_g1': _L2_gnn_in['g1'], 'L2_gnn_b1': _L2_gnn_in['b1'], 'L2_gnn_g2': _L2_gnn_in['g2'], 'L2_gnn_b2': _L2_gnn_in['b2'], 'L3_gnn_Ws0': _L3_gnn_in['Ws0'], 'L3_gnn_Wn0': _L3_gnn_in['Wn0'], 'L3_gnn_b0': _L3_gnn_in['b0'], 'L3_gnn_Ws1': _L3_gnn_in['Ws1'], 'L3_gnn_Wn1': _L3_gnn_in['Wn1'], 'L3_gnn_b1': _L3_gnn_in['b1'], 'L3_gnn_Ws2': _L3_gnn_in['Ws2'], 'L3_gnn_Wn2': _L3_gnn_in['Wn2'], 'L3_gnn_b2': _L3_gnn_in['b2']}

def reference(x, src, dst, edge_weight1, node_vec, L0_gnn_W, L0_gnn_att, L1_gnn_fc11_w, L1_gnn_fc11_b, L1_gnn_fc12_w, L1_gnn_fc12_b, L1_gnn_fc13_w, L1_gnn_fc13_b, L1_gnn_conv1_w, L1_gnn_conv1_b, L1_gnn_fc21_w, L1_gnn_fc21_b, L1_gnn_fc22_w, L1_gnn_fc22_b, L1_gnn_fc23_w, L1_gnn_fc23_b, L1_gnn_conv2_w, L1_gnn_conv2_b, L2_gnn_Wq, L2_gnn_Wk, L2_gnn_Wv, L2_gnn_Wo, L2_gnn_bo, L2_gnn_Wf1, L2_gnn_bf1, L2_gnn_Wf2, L2_gnn_bf2, L2_gnn_g1, L2_gnn_b1, L2_gnn_g2, L2_gnn_b2, L3_gnn_Ws0, L3_gnn_Wn0, L3_gnn_b0, L3_gnn_Ws1, L3_gnn_Wn1, L3_gnn_b1, L3_gnn_Ws2, L3_gnn_Wn2, L3_gnn_b2):
    import jax
    import jax.numpy as jnp

    def _L0_gnn_ref(x, edge_index, pos, W, att):
        import jax, jax.numpy as jnp
        import numpy as np
        N = 3125
        E = 50000
        IN = 128
        HEADS = 8
        HID = 16
        NEG_SLOPE = 0.2
        n = x.shape[0]
        hid = att.shape[-1] // 2
        heads = att.shape[1]
        h = (x @ W.T).reshape(n, heads, hid)
        row, col = (edge_index[0], edge_index[1])
        att_l = att[0, :, :hid]
        att_r = att[0, :, hid:]
        al = jnp.einsum('nhd,hd->nh', h, att_l)
        ar = jnp.einsum('nhd,hd->nh', h, att_r)
        alpha = al[row] + ar[col]
        alpha = jnp.where(alpha >= 0, alpha, NEG_SLOPE * alpha)
        alpha = jnp.exp(alpha) * pos[col][:, None]
        rowsum = jax.ops.segment_sum(alpha, row, num_segments=n)
        inv = 1.0 / rowsum + 1e-16
        alpha = alpha * inv[row]
        out = jax.ops.segment_sum(alpha[:, :, None] * h[col], row, num_segments=n)
        return out.reshape(n, heads * hid)

    def _L1_gnn_ref(x, edge_index, edge_attr, fc11_w, fc11_b, fc12_w, fc12_b, fc13_w, fc13_b, conv1_w, conv1_b, fc21_w, fc21_b, fc22_w, fc22_b, fc23_w, fc23_b, conv2_w, conv2_b):
        import jax, jax.numpy as jnp
        import numpy as np
        N, D, E = (50000, 128, 20000)

        def _spect_conv(x, edge_index, edge_attr, w, b):
            src, dst = (edge_index[0], edge_index[1])
            msg = edge_attr[:, 0:1] * x[src]
            h = jax.ops.segment_sum(msg, dst, num_segments=x.shape[0])
            return h @ w + b

        def _lin(x, w, b):
            return x @ w + b
        h = jax.nn.relu(_lin(x, fc11_w, fc11_b) + _spect_conv(x, edge_index, edge_attr, conv1_w, conv1_b) + _lin(x, fc12_w, fc12_b) * _lin(x, fc13_w, fc13_b))
        out = jax.nn.relu(_lin(h, fc21_w, fc21_b) + _spect_conv(h, edge_index, edge_attr, conv2_w, conv2_b) + _lin(h, fc22_w, fc22_b) * _lin(h, fc23_w, fc23_b))
        return out

    def _L2_gnn_ref(x, edge_index, Wq, Wk, Wv, Wo, bo, Wf1, bf1, Wf2, bf2, g1, b1, g2, b2):
        import math
        import jax, jax.numpy as jnp
        import numpy as np
        N = 50000
        C = 128
        H = 8
        D = C // H
        E = 25000

        def _layernorm(x, g, b, eps=1e-05):
            mu = jnp.mean(x, axis=-1, keepdims=True)
            var = jnp.var(x, axis=-1, keepdims=True)
            return (x - mu) * jax.lax.rsqrt(var + eps) * g + b
        n = x.shape[0]
        loops = jnp.arange(n, dtype=edge_index.dtype)
        row = jnp.concatenate([edge_index[0], loops])
        col = jnp.concatenate([edge_index[1], loops])
        q = (x @ Wq).reshape(n, H, D)
        k = (x @ Wk).reshape(n, H, D)
        v = (x @ Wv).reshape(n, H, D)
        scores = jnp.einsum('ehd,ehd->eh', q[row], k[col]) / math.sqrt(D)
        smax = jax.ops.segment_max(scores, col, num_segments=n)
        exp = jnp.exp(scores - smax[col])
        ssum = jax.ops.segment_sum(exp, col, num_segments=n)
        alpha = exp / (ssum[col] + 1e-08)
        out = jax.ops.segment_sum(v[row] * alpha[..., None], col, num_segments=n)
        attn = out.reshape(n, C) @ Wo + bo
        residual = x
        x1 = _layernorm(residual + attn, g1, b1)
        ffn = jax.nn.gelu(x1 @ Wf1 + bf1, approximate=False) @ Wf2 + bf2
        return _layernorm(x1 + ffn, g2, b2)

    def _L3_gnn_ref(x, Ws0, Wn0, b0, Ws1, Wn1, b1, Ws2, Wn2, b2, src, dst):
        import jax, jax.numpy as jnp
        import numpy as np
        N_NODES = 3125
        N_EDGES = 50000
        D_IN = 128
        D_H = 128
        D_OUT = 128

        def _sage_conv(h, src, dst, Ws, Wn, b):
            n = h.shape[0]
            msg = h[src]
            summed = jax.ops.segment_sum(msg, dst, num_segments=n)
            deg = jax.ops.segment_sum(jnp.ones(src.shape, h.dtype), dst, num_segments=n)
            neigh = summed / jnp.maximum(deg, 1.0)[:, None]
            return h @ Ws.T + neigh @ Wn.T + b
        h = jax.nn.relu(_sage_conv(x, src, dst, Ws0, Wn0, b0))
        prev = h
        h = _sage_conv(h, src, dst, Ws1, Wn1, b1)
        h = jax.nn.relu(h + prev)
        return _sage_conv(h, src, dst, Ws2, Wn2, b2)
    edge_index = jnp.stack([src, dst])
    x = _layernorm(x + _L0_gnn_ref(x, edge_index, node_vec, L0_gnn_W, L0_gnn_att), axis=-1)
    x = _layernorm(x + _L1_gnn_ref(x, edge_index, edge_weight1, L1_gnn_fc11_w, L1_gnn_fc11_b, L1_gnn_fc12_w, L1_gnn_fc12_b, L1_gnn_fc13_w, L1_gnn_fc13_b, L1_gnn_conv1_w, L1_gnn_conv1_b, L1_gnn_fc21_w, L1_gnn_fc21_b, L1_gnn_fc22_w, L1_gnn_fc22_b, L1_gnn_fc23_w, L1_gnn_fc23_b, L1_gnn_conv2_w, L1_gnn_conv2_b), axis=-1)
    x = _layernorm(x + _L2_gnn_ref(x, edge_index, L2_gnn_Wq, L2_gnn_Wk, L2_gnn_Wv, L2_gnn_Wo, L2_gnn_bo, L2_gnn_Wf1, L2_gnn_bf1, L2_gnn_Wf2, L2_gnn_bf2, L2_gnn_g1, L2_gnn_b1, L2_gnn_g2, L2_gnn_b2), axis=-1)
    x = _layernorm(x + _L3_gnn_ref(x, L3_gnn_Ws0, L3_gnn_Wn0, L3_gnn_b0, L3_gnn_Ws1, L3_gnn_Wn1, L3_gnn_b1, L3_gnn_Ws2, L3_gnn_Wn2, L3_gnn_b2, src, dst), axis=-1)
    return x

_drawn_inputs = setup_inputs


def setup_inputs(seed=0):
    import zlib

    import numpy as np

    out = dict(_drawn_inputs(seed))
    spreads = {'L2_gnn_bo': (0.0, 0.1),
     'L2_gnn_bf1': (0.0, 0.272),
     'L2_gnn_bf2': (0.0, 0.1),
     'L2_gnn_g1': (1.0, 0.2),
     'L2_gnn_b1': (0.0, 0.1),
     'L2_gnn_g2': (1.0, 0.2),
     'L2_gnn_b2': (0.0, 0.1),
     'L3_gnn_b0': (0.0, 0.1),
     'L3_gnn_b1': (0.0, 0.1),
     'L3_gnn_b2': (0.0, 0.1)}
    factors = {'L1_gnn_fc11_b': 8.0,
     'L1_gnn_fc12_b': 27.407,
     'L1_gnn_fc13_b': 28.009,
     'L1_gnn_conv1_b': 8.0,
     'L1_gnn_fc21_b': 8.0,
     'L1_gnn_fc22_b': 25.341,
     'L1_gnn_fc23_b': 25.362,
     'L1_gnn_conv2_b': 8.0}
    for name, (base, spread) in spreads.items():
        noise = np.random.default_rng([zlib.crc32(name.encode()), seed]).standard_normal(out[name].shape)
        drawn = base * np.exp(spread * noise) if base else spread * noise
        out[name] = jnp.asarray(drawn.astype(out[name].dtype))
    for name, factor in factors.items():
        out[name] = (out[name] * factor).astype(out[name].dtype)
    return out
```

```python
from contextlib import ExitStack, contextmanager

import concourse.bass as bass
from concourse import mybir

ALU = mybir.AluOpType
ACT = mybir.ActivationFunctionType
F32 = mybir.dt.float32
F16 = mybir.dt.float16
I32 = mybir.dt.int32

P = 128
D = 128
N = 50000
E = 25000
TB = 4
BLK = TB * P
NODE_BLOCKS = -(-N // BLK)
NPAD = NODE_BLOCKS * BLK
TILES = -(-E // BLK) * TB
EDGE_BLOCKS = TILES // TB
EPAD = TILES * P
HALF = TILES // 2
ROWS = NPAD + EPAD
NCOL = -(-N // P)
PAD_KEY = NCOL * P - 1
HEADS, HID = 8, 16
EPS = 1e-5
BIG = 1e30
assert PAD_KEY >= N and PAD_KEY < NPAD and TILES % 2 == 0 and HALF <= P


class Kit:
    pass


@contextmanager
def phase(nc, title):
    with ExitStack() as ctx:
        sems = []

        def sb(name, shape, dt=F32):
            return ctx.enter_context(nc.sbuf_tensor(f"{title}_{name}", shape, dt))

        def ps(name, shape, dt=F32):
            return ctx.enter_context(nc.psum_tensor(f"{title}_{name}", shape, dt))

        def sem(name):
            sems.append(nc.alloc_semaphore(f"{title}_{name}"))
            return sems[-1]

        yield sb, ps, sem
        nc.clear_and_free_semaphores(sems)
        nc.all_engine_barrier()


def run_blocks(eng, blocks, body, first=4):
    for b in range(first):
        body(b, b % 2, b // 2)
    pairs = (blocks - first) // 2
    with eng.Fori(0, pairs) as i:
        for s in range(2):
            body(i * 2 + (first + s), s, i + first // 2)
    if (blocks - first) % 2:
        body(blocks - 1, (blocks - 1) % 2, (blocks - 1) // 2)


def later(b, lag=2):
    return not isinstance(b, int) or b >= lag


def block_rows(table, b):
    return table[bass.ds(b * BLK, BLK), :].rearrange("(p j) c -> p j c", j=TB)


def as_row(v):
    return v.rearrange("(a c) -> a c", a=1)


def setup(nc, k, x, src, dst, edge_w, node_vec, w):
    R = len(k.vec_names)
    with phase(nc, "setup") as (sb, ps, sem):
        rc = sb("rc", [P, 2, P], I32)
        rcs = sb("rcs", [P, 2, P], I32)
        head = sb("head", [P, P])
        vec_rows = sb("vec_rows", [P, D])
        raw = sb("raw", [P, 9, D])
        attx = sb("attx", [P, 2, D])
        zeros = sb("zeros", [P, 12544])
        pads = sb("pads", [1, 2, P], I32)
        guard = sb("guard", [1, 2, 4])
        by_tile = sb("by_tile", [HALF, 4, 2, P], I32)
        by_tile_f = sb("by_tile_f", [HALF, 5, 2, P])
        dst_i = sb("dst_i", [P, TILES], I32)
        dst_stage = sb("dst_stage", [P, 2, TB], I32)
        nv = sb("nv", [P, 2, TB])
        pt = ps("pt", [P, 2, 512])
        pw = ps("pw", [P, 512])
        pads_set, iota_done, shifted, masks = sem("pads_set"), sem("iota_done"), sem("shifted"), sem("masks")
        weights_in, padded, lists_in, converted = sem("weights_in"), sem("padded"), sem("lists_in"), sem("converted")
        tables_in, pe_turn, copied = sem("tables_in"), sem("pe_turn"), sem("copied")
        attx_done, sums = sem("attx_done"), sem("sums")
        staged, nv_in = sem("staged"), [sem("nv_in0"), sem("nv_in1")]
        nv_kept = sem("nv_kept")
        block = nc.Block()
        block.__enter__()

        lists = [(src, k.key_dram[0]), (dst, k.key_dram[1]), (src, k.oth_dram[0]), (dst, k.oth_dram[1])]
        direct = ["fc11", "fc12", "fc13", "conv1", "fc21", "fc22", "fc23", "conv2", "Wq", "Wk", "Wv", "Wo"]
        turned = ["W0", "Ws0", "Wn0", "Ws1", "Wn1", "Ws2", "Wn2", "Wv"]
        n_in = [0]

        @block.sync
        def _(sp):
            sp.wait_ge(pads_set, 5)
            n = 0
            for a, out in lists:
                sp.dma_start(out[0:E].rearrange("(p c) -> p c", p=8), a.rearrange("(p c) -> p c", p=8)).then_inc(padded, 16)
                sp.dma_start(as_row(out[E:EPAD]), pads[0:1, 0 if n < 2 else 1, 0:EPAD - E]).then_inc(padded, 16)
                n += 1
            sp.dma_start(k.w_dram[0:E].rearrange("(p c) -> p c", p=8), edge_w.rearrange("(p c) o -> p (c o)", p=8)).then_inc(padded, 16)
            sp.dma_start(as_row(k.w_dram[E:EPAD]), zeros[0:1, 0:EPAD - E]).then_inc(padded, 16)
            for s in range(2):
                sp.dma_start(k.sorted_dram[s][0:1, :], guard[0:1, 0, :]).then_inc(tables_in, 16)
                sp.dma_start(k.sorted_dram[s][EPAD + 1:EPAD + 2, :], guard[0:1, 1, :]).then_inc(tables_in, 16)
            sp.wait_ge(padded, 16 * 10)
            for i, a in enumerate([k.key_dram[0], k.key_dram[1], k.oth_dram[0], k.oth_dram[1]]):
                sp.dma_start(by_tile[:, i, :, :], a.rearrange("(h t p) -> t h p", h=2, p=P)).then_inc(lists_in, 16)
            sp.dma_start(by_tile_f[:, 4, :, :], k.w_dram.rearrange("(h t p) -> t h p", h=2, p=P)).then_inc(lists_in, 16)
            for c in range(5):
                rows = slice(c * (N // 5), (c + 1) * (N // 5))
                sp.dma_start(k.table[0][rows, :].rearrange("(p r) c -> p (r c)", p=16),
                             x[rows, :].rearrange("(p r) c -> p (r c)", p=16)).then_inc(tables_in, 16)
            sp.dma_start(k.table[0][N:NPAD, :].rearrange("(p r) c -> p (r c)", p=16),
                         zeros[0:16, 0:(NPAD - N) // 16 * D]).then_inc(tables_in, 16)
            for s in range(2):
                for h in range(2):
                    rows = slice(NPAD + h * (EPAD // 2), NPAD + (h + 1) * (EPAD // 2))
                    sp.dma_start(k.table[s][rows, :].rearrange("(p r) c -> p (r c)", p=P), zeros[:, :]).then_inc(tables_in, 16)
            sp.wait_ge(tables_in, 16 * 14)

        @block.scalar
        def _(act):
            for name in direct:
                act.dma_start(k.W[name], w[name]).then_inc(weights_in, 16)
            for i, name in enumerate(turned):
                act.dma_start(raw[:, i, :], w[name]).then_inc(weights_in, 16)
            act.dma_start(k.W["Wf1"], w["Wf1"]).then_inc(weights_in, 16)
            act.dma_start(k.W["Wf2"], w["Wf2"].rearrange("(c p) n -> p c n", p=P)).then_inc(weights_in, 16)
            for r, name in enumerate(k.vec_names):
                v = w[name]
                if name in ("attL", "attR"):
                    act.dma_start(vec_rows[r:r + 1, :].rearrange("a (h d) -> a h d", h=HEADS), v).then_inc(weights_in, 16)
                else:
                    act.dma_start(vec_rows[r:r + 1, :], as_row(v)).then_inc(weights_in, 16)
            for out, v in ((k.g2, w["g2"]), (k.b2, w["b2"])):
                act.dma_start(out[:, :], as_row(v).to_broadcast([P, D])).then_inc(weights_in, 16)
            n_in[0] = len(direct) + len(turned) + 2 + R + 2
            act.wait_ge(weights_in, 16 * n_in[0])

        @block.gpsimd
        def _(pool):
            pool.memset(pads[:, 0, :], PAD_KEY).then_inc(pads_set, 1)
            pool.memset(pads[:, 1, :], 0).then_inc(pads_set, 1)
            pool.memset(guard[:, 0, :], -1.0).then_inc(pads_set, 1)
            pool.memset(guard[:, 1, :], -2.0).then_inc(pads_set, 1)
            pool.iota(rc[:, 0, :], [[0, P]], base=0, channel_multiplier=1).then_inc(iota_done, 1)
            pool.iota(rc[:, 1, :], [[1, P]], base=0, channel_multiplier=0).then_inc(iota_done, 1)
            pool.iota(k.col_iota[:, :], [[1, NCOL]], base=0, channel_multiplier=0, allow_small_or_imprecise_dtypes=True).then_inc(iota_done, 1)
            pool.memset(k.neg_half[:, :], -0.5).then_inc(iota_done, 1)
            pool.memset(k.eps[:, :], EPS).then_inc(iota_done, 1)
            pool.memset(k.ones[:, :], 1.0).then_inc(iota_done, 1)

            def gather_nv(b, s, turn):
                pool.wait_ge(staged, b + 1)
                pool.nop(nofuse=True)
                for j in range(TB):
                    pool.indirect_dma_start(out=nv[:, s, j:j + 1], out_offset=None, in_=node_vec.rearrange("(n a) -> n a", a=1),
                                            in_offset=bass.IndirectOffsetOnAxis(ap=dst_stage[:, s, j:j + 1], axis=0)).then_inc(nv_in[s], 16)

            run_blocks(pool, EDGE_BLOCKS, gather_nv)

        @block.tensor
        def _(pe):
            n = 0

            def turn(out, in_, width):
                nonlocal n
                if n >= 2:
                    pe.wait_ge(copied, n - 1)
                pe.transpose(pt[0:in_.shape[1], n % 2, 0:width], in_, k.ident[0:width, 0:width]).then_inc(pe_turn, 1)
                n += 1

            pe.wait_ge(masks, 6)
            pe.wait_ge(converted, 1)
            pe.wait_ge(lists_in, 16 * 5)
            for i in range(5):
                for h in range(2):
                    turn(None, by_tile_f[:, i, h, :], HALF)
            pe.wait_ge(weights_in, 16 * n_in[0])
            for i in range(len(turned)):
                turn(None, raw[:, i, :], P)
            turn(None, vec_rows[0:R, :], R)
            pe.wait_ge(attx_done, 2)
            for s in range(2):
                pe.matmul(pw[:, s * D:(s + 1) * D], raw[:, 0, :], attx[:, s, :], start=True, stop=True)
            pe.matmul(pw[:, 2 * D:3 * D], k.W["WvT"], k.W["Wo"], start=True, stop=True).then_inc(pe_turn, 1)

        @block.vector
        def _(dve):
            dve.memset(zeros[:, :], 0.0).then_inc(pads_set, 1)
            dve.wait_ge(iota_done, 6)
            dve.tensor_scalar(rcs[:, :, :], rc[:, :, :], 4, None, ALU.logical_shift_right).then_inc(shifted, 1)
            dve.tensor_copy(k.part_iota[:, :], rc[:, 0, 0:1]).then_inc(masks, 1)
            dve.tensor_tensor(k.ident[:, :], rc[:, 0, :], rc[:, 1, :], ALU.is_equal).then_inc(masks, 1)
            dve.tensor_tensor(k.before[:, :], rc[:, 1, :], rc[:, 0, :], ALU.is_lt).then_inc(masks, 1)
            dve.tensor_tensor(k.above[:, :], rc[:, 0, :], rc[:, 1, :], ALU.is_lt).then_inc(masks, 1)
            dve.tensor_copy(k.row_iota[:, :], rc[:, 1, :]).then_inc(masks, 1)
            dve.wait_ge(shifted, 1)
            dve.tensor_tensor(head[:, :], rcs[:, 0, :], rcs[:, 1, :], ALU.is_equal).then_inc(masks, 1)
            dve.wait_ge(masks, 6)
            dve.tensor_copy(k.ident16[:, :], k.ident[:, :]).then_inc(masks, 1)
            dve.tensor_copy(k.head[:, :], head[:, :]).then_inc(masks, 1)
            dve.wait_ge(lists_in, 16 * 5)
            dve.tensor_copy(by_tile_f[:, 0:4, :, :].rearrange("t i h p -> t (i h p)"),
                            by_tile[:, :, :, :].rearrange("t i h p -> t (i h p)")).then_inc(converted, 1)
            n = 0

            def take(out, width=P, rows=P):
                nonlocal n
                dve.wait_ge(pe_turn, n + 1)
                dve.tensor_copy(out, pt[0:rows, n % 2, 0:width]).then_inc(copied, 1)
                n += 1

            slot = [(k.payload[0], 0), (k.payload[1], 0), (k.payload[1], 1), (k.payload[0], 1)]
            for i in range(5):
                for h in range(2):
                    half = slice(h * HALF, (h + 1) * HALF)
                    if i < 4:
                        take(slot[i][0][:, half, slot[i][1]], HALF)
                    else:
                        take(k.payload[0][:, half, 2], HALF)
            for name in turned:
                take(k.W[name + "T"])
            take(k.vec[:, 0:R], R)
            dve.wait_ge(copied, n)
            al, ar = k.vec_names.index("attL"), k.vec_names.index("attR")
            dve.tensor_scalar(attx[:, 0, :], head[:, :], k.vec[:, al:al + 1], None, ALU.mult).then_inc(attx_done, 1)
            dve.tensor_scalar(attx[:, 1, :], head[:, :], k.vec[:, ar:ar + 1], None, ALU.mult).then_inc(attx_done, 1)
            for i, (a, b) in enumerate((("fc11_b", "conv1_b"), ("fc21_b", "conv2_b"))):
                a, b = k.vec_names.index(a), k.vec_names.index(b)
                dve.tensor_tensor(k.bsum[:, i:i + 1], k.vec[:, a:a + 1], k.vec[:, b:b + 1], ALU.add).then_inc(sums, 1)
            dve.tensor_copy(k.payload[1][:, :, 2], k.payload[0][:, :, 2]).then_inc(sums, 1)
            dve.tensor_copy(dst_i[:, :], k.payload[0][:, :, 1]).then_inc(sums, 1)
            dve.wait_ge(pe_turn, n + 1)
            for i, name in enumerate(("attLW", "attRW", "Wvo")):
                dve.tensor_copy(k.W[name], pw[:, i * D:(i + 1) * D]).then_inc(sums, 1)
            dve.wait_ge(sums, 4)

            def keep_nv(b, s, turn):
                if later(b):
                    dve.wait_ge(nv_in[s], turn * (16 * TB))
                    store_nv(b - 2, s)
                dve.tensor_copy(dst_stage[:, s, :], dst_i[:, bass.ds(b * TB, TB)]).then_inc(staged, 1)

            def store_nv(b, s):
                for pay in k.payload:
                    dve.tensor_copy(pay[:, bass.ds(b * TB, TB), 3], nv[:, s, :]).then_inc(nv_kept, 1)

            def keep(b, s, turn):
                keep_nv(b, s, turn)

            run_blocks(dve, EDGE_BLOCKS, keep)
            for b in (EDGE_BLOCKS - 2, EDGE_BLOCKS - 1):
                dve.wait_ge(nv_in[b % 2], (b // 2 + 1) * 16 * TB)
                store_nv(b, b % 2)

        block.__exit__(None, None, None)


def sort_edges(nc, k, which):
    pay, key_dram, out = k.payload[which], k.key_dram[which], k.sorted_dram[which]
    with phase(nc, f"sort{which}") as (sb, ps, sem):
        key_i = sb("key_i", [P, TILES], I32)
        bits = sb("bits", [P, 2, TILES], I32)
        kpart = sb("kpart", [P, TILES])
        kcol = sb("kcol", [P, TILES])
        oh_part = sb("oh_part", [P, 2, TB, P], F16)
        oh_col = sb("oh_col", [P, 2, TB, NCOL], F16)
        oh_turned = sb("oh_turned", [P, 2, P])
        counts = sb("counts", [P, NCOL])
        col_sum = sb("col_sum", [P, NCOL + 1])
        start = sb("start", [P, NCOL])
        base = sb("base", [P, 2, NCOL])
        key_row = sb("key_row", [P, 2, BLK], I32)
        junk = sb("junk", [P, TB, NCOL])
        junk2 = sb("junk2", [P, TB, P])
        found = sb("found", [P, 2, TB])
        rank = sb("rank", [P, 2, TB])
        place = sb("place", [P, 2, TB], I32)
        cargo = sb("cargo", [P, 2, TB, 4])
        key_now = sb("key_now", [P, 2, TB])
        total = ps("total", [P, 512])
        sums = ps("sums", [P, 2, 512])
        look = ps("look", [P, 2, 512])
        turned = ps("turned", [P, 2, 1024], F16)
        key_split, onehots, counted, step = sem("key_split"), sem("onehots"), sem("counted"), sem("step")
        onehots2, turned_ok, turned_kept = sem("onehots2"), sem("turned_ok"), sem("turned_kept")
        added, base_ready, looked, found_ok = sem("added"), sem("base_ready"), sem("looked"), sem("found_ok")
        rows_in = [sem("rows_in0"), sem("rows_in1")]
        keys_staged, ranked, cargo_ready = sem("keys_staged"), sem("ranked"), sem("cargo_ready")
        sent = [sem("sent0"), sem("sent1")]
        block = nc.Block()
        block.__enter__()

        @block.sync
        def _(sp):
            def load_rows(b, s, turn):
                if later(b):
                    sp.wait_ge(ranked, b * TB - TB)
                sp.dma_start(key_row[:, s, :], as_row(key_dram[bass.ds(b * BLK, BLK)]).to_broadcast([P, BLK])).then_inc(rows_in[s], 16)

            run_blocks(sp, EDGE_BLOCKS, load_rows)

        def make_onehots(dve, b, s, done):
            for j in range(TB):
                at = bass.ds(b * TB + j, 1)
                dve.tensor_scalar(oh_part[:, s, j, :], k.row_iota[:, :], kpart[:, at], None, ALU.is_equal).then_inc(done, 1)
                dve.tensor_scalar(oh_col[:, s, j, :], k.col_iota[:, :], kcol[:, at], None, ALU.is_equal).then_inc(done, 1)

        @block.vector
        def _(dve):
            dve.tensor_copy(key_i[:, :], pay[:, :, 0]).then_inc(key_split, 1)
            dve.wait_ge(key_split, 1)
            dve.tensor_scalar(bits[:, 0, :], key_i[:, :], P - 1, None, ALU.bitwise_and).then_inc(key_split, 1)
            dve.tensor_scalar(bits[:, 1, :], key_i[:, :], 7, None, ALU.logical_shift_right).then_inc(key_split, 1)
            dve.wait_ge(key_split, 3)
            dve.tensor_copy(kpart[:, :], bits[:, 0, :]).then_inc(key_split, 1)
            dve.tensor_copy(kcol[:, :], bits[:, 1, :]).then_inc(key_split, 1)
            dve.wait_ge(key_split, 5)

            def count(b, s, turn):
                if later(b):
                    dve.wait_ge(counted, b * TB - TB)
                make_onehots(dve, b, s, onehots)

            run_blocks(dve, EDGE_BLOCKS, count)
            dve.wait_ge(counted, TILES)
            dve.tensor_copy(counts[:, :], total[:, 0:NCOL]).then_inc(step, 1)
            dve.memset(col_sum[:, 0:1], 0.0).then_inc(step, 1)
            dve.wait_ge(counted, TILES + 1)
            dve.wait_ge(step, 2)
            dve.tensor_tensor_scan(col_sum[:, 1:NCOL + 1], k.ones[:, 0:NCOL], sums[:, 0, 0:NCOL], 0.0, ALU.mult, ALU.add).then_inc(step, 1)
            dve.wait_ge(step, 3)
            dve.tensor_tensor(start[:, :], sums[:, 1, 0:NCOL], col_sum[:, 0:NCOL], ALU.add).then_inc(step, 1)

            def stage(b, s):
                dve.tensor_copy(key_now[:, s, :], pay[:, bass.ds(b * TB, TB), 0]).then_inc(keys_staged, 1)

            def place_block(b, s, turn):
                if later(b):
                    dve.wait_ge(looked, b * TB - TB)
                    dve.wait_ge(found_ok, b * TB - TB)
                make_onehots(dve, b, s, onehots2)
                stage(b, s)
                dve.wait_ge(keys_staged, b + 1)
                dve.wait_ge(rows_in[s], turn * 16 + 16)
                if later(b, 1):
                    dve.wait_ge(ranked, b * TB)
                    dve.wait_ge(found_ok, b * TB)
                for j in range(TB):
                    dve.scalar_tensor_tensor(junk2[:, j, :], key_row[:, s, j * P:(j + 1) * P], key_now[:, s, j:j + 1], k.before[:, :],
                                             ALU.is_equal, ALU.mult, accum_out=rank[:, s, j:j + 1]).then_inc(ranked, 1)
                for j in range(TB):
                    dve.wait_ge(looked, b * TB + (j + 1))
                    dve.scalar_tensor_tensor(junk[:, j, :], look[:, j % 2, 0:NCOL], 1.0, oh_col[:, s, j, :],
                                             ALU.mult, ALU.mult, accum_out=found[:, s, j:j + 1]).then_inc(found_ok, 1)
                if later(b):
                    dve.wait_ge(sent[s], turn * (16 * TB))
                dve.wait_ge(found_ok, b * TB + TB)
                dve.wait_ge(ranked, b * TB + TB)
                dve.scalar_tensor_tensor(place[:, s, :], found[:, s, :], 1.0, rank[:, s, :], ALU.add, ALU.add).then_inc(cargo_ready, 1)
                dve.tensor_copy(cargo[:, s, :, :], pay[:, bass.ds(b * TB, TB), :]).then_inc(cargo_ready, 1)

            run_blocks(dve, EDGE_BLOCKS, place_block)

        @block.tensor
        def _(pe):
            def count(b, s, turn):
                for j in range(TB):
                    pe.wait_ge(onehots, b * (2 * TB) + 2 * (j + 1))
                    pe.matmul(total[:, 0:NCOL], oh_part[:, s, j, :], oh_col[:, s, j, :],
                              start=isinstance(b, int) and b == 0 and j == 0, stop=False, skip_group_check=True).then_inc(counted, 1)

            run_blocks(pe, EDGE_BLOCKS, count)
            pe.wait_ge(step, 1)
            pe.matmul(sums[:, 0, 0:NCOL], k.ones[:, 0:P], counts[:, :], start=True, stop=True)
            pe.matmul(sums[:, 1, 0:NCOL], k.above[:, :], counts[:, :], start=True, stop=True).then_inc(counted, 1)
            pe.wait_ge(step, 4)
            pe.matmul(total[:, 0:NCOL], k.ident[:, :], start[:, :], start=True, stop=False, skip_group_check=True).then_inc(added, 1)

            def place_block(b, s, turn):
                for j in range(TB):
                    pe.wait_ge(onehots2, b * (2 * TB) + 2 * (j + 1))
                    if j >= 2 or later(b, 1):
                        pe.wait_ge(turned_kept, b * TB + (j - 1))
                    pe.transpose(turned[:, j % 2, 0:P], oh_part[:, s, j, :], k.ident16[:, :]).then_inc(turned_ok, 1)
                    pe.wait_ge(base_ready, b * TB + (j + 1))
                    pe.matmul(total[:, 0:NCOL], oh_part[:, s, j, :], oh_col[:, s, j, :], start=False, stop=False,
                              skip_group_check=True).then_inc(added, 1)
                    pe.wait_ge(turned_kept, b * TB + (j + 1))
                    if j >= 2 or later(b, 1):
                        pe.wait_ge(found_ok, b * TB + (j - 1))
                    pe.matmul(look[:, j % 2, 0:NCOL], oh_turned[:, j % 2, :], base[:, j % 2, :], start=True, stop=True).then_inc(looked, 1)

            run_blocks(pe, EDGE_BLOCKS, place_block)


        @block.scalar
        def _(act):
            def keep(b, s, turn):
                for j in range(TB):
                    act.wait_ge(added, b * TB + (j + 1))
                    if j >= 2 or later(b, 1):
                        act.wait_ge(looked, b * TB + (j - 1))
                    act.copy(base[:, j % 2, :], total[:, 0:NCOL]).then_inc(base_ready, 1)
                    act.wait_ge(turned_ok, b * TB + (j + 1))
                    act.copy(oh_turned[:, j % 2, :], turned[:, j % 2, 0:P]).then_inc(turned_kept, 1)

            run_blocks(act, EDGE_BLOCKS, keep)

        @block.gpsimd
        def _(pool):
            def send(b, s, turn):
                pool.wait_ge(cargo_ready, b * 2 + 2)
                pool.nop(nofuse=True)
                for j in range(TB):
                    pool.indirect_dma_start(out=out[:, :], out_offset=bass.IndirectOffsetOnAxis(ap=place[:, s, j:j + 1], axis=0),
                                            in_=cargo[:, s, j, :], in_offset=None).then_inc(sent[s], 16)

            run_blocks(pool, EDGE_BLOCKS, send)
            for s in range(2):
                pool.wait_ge(sent[s], 16 * TB * len(range(s, EDGE_BLOCKS, 2)))

        block.__exit__(None, None, None)


def sorted_lists(nc, k, which):
    table = k.sorted_dram[which]
    with phase(nc, f"lists{which}") as (sb, ps, sem):
        words = sb("words", [HALF, 3, 2, P, 4])
        same = sb("same", [HALF, 2, P])
        is_end = sb("is_end", [HALF, 2, P])
        spare = sb("spare", [HALF, 2, P])
        diff = sb("diff", [HALF, 2, P])
        idx = sb("idx", [HALF, 3, 2, P])
        pt = ps("pt", [P, 2, 512])
        loaded, spare_set, step, ready = sem("loaded"), sem("spare_set"), sem("step"), sem("ready")
        stored, pe_turn, copied = sem("stored"), sem("pe_turn"), sem("copied")
        block = nc.Block()
        block.__enter__()

        @block.sync
        def _(sp):
            for i in range(3):
                first = (1, 0, 2)[i]
                sp.dma_start(words[:, i, :, :, :].rearrange("t h p w -> t h (p w)"),
                             table[first:first + EPAD, :].rearrange("(h t p) w -> t h (p w)", h=2, p=P)).then_inc(loaded, 16)
            sp.wait_ge(ready, 3)
            for a, src in ((k.same_dram[which], same), (k.weight_dram[which], idx[:, 0]), (k.nv_dram[which], idx[:, 1])):
                sp.dma_start(a.rearrange("(h t p) -> t h p", h=2, p=P), src[:, :, :] if src is same else src).then_inc(stored, 16)
            sp.wait_ge(stored, 16 * 3)

        @block.gpsimd
        def _(pool):
            pool.iota(spare[:, :, :], [[HALF * P, 2], [1, P]], base=NPAD, channel_multiplier=P,
                      allow_small_or_imprecise_dtypes=True).then_inc(spare_set, 1)

        @block.vector
        def _(dve):
            dve.wait_ge(loaded, 16 * 3)
            key = words[:, 0, :, :, 0]
            dve.tensor_tensor(same[:, :, :], key, words[:, 1, :, :, 0], ALU.is_equal).then_inc(ready, 1)
            dve.tensor_copy(idx[:, 0], words[:, 0, :, :, 2]).then_inc(ready, 1)
            dve.tensor_copy(idx[:, 1], words[:, 0, :, :, 3]).then_inc(ready, 1)
            dve.tensor_tensor(is_end[:, :, :], key, words[:, 2, :, :, 0], ALU.not_equal).then_inc(step, 1)
            dve.wait_ge(spare_set, 1)
            dve.tensor_tensor(diff[:, :, :], key, spare[:, :, :], ALU.subtract).then_inc(step, 1)
            dve.wait_ge(step, 2)
            dve.tensor_tensor(diff[:, :, :], diff[:, :, :], is_end[:, :, :], ALU.mult).then_inc(step, 1)
            dve.wait_ge(step, 3)
            dve.wait_ge(stored, 16 * 3)
            dve.tensor_tensor(idx[:, 2], diff[:, :, :], spare[:, :, :], ALU.add).then_inc(step, 1)
            dve.tensor_copy(idx[:, 1], words[:, 0, :, :, 1]).then_inc(step, 1)
            dve.tensor_scalar(idx[:, 0], key, float(N - 1), None, ALU.min).then_inc(step, 1)
            n = 0
            for out in (k.at_key[which], k.at_other[which], k.at_end[which]):
                for h in range(2):
                    dve.wait_ge(pe_turn, n + 1)
                    dve.tensor_copy(out[:, h * HALF:(h + 1) * HALF], pt[:, n % 2, 0:HALF]).then_inc(copied, 1)
                    n += 1

        @block.tensor
        def _(pe):
            pe.wait_ge(step, 6)
            n = 0
            for i in range(3):
                for h in range(2):
                    if n >= 2:
                        pe.wait_ge(copied, n - 1)
                    pe.transpose(pt[:, n % 2, 0:HALF], idx[:, i, h, :], k.ident[0:HALF, 0:HALF]).then_inc(pe_turn, 1)
                    n += 1

        block.__exit__(None, None, None)


def gather_rows(pool, source, rows, index, done):
    for j in range(TB):
        pool.indirect_dma_start(out=rows[:, j * D:(j + 1) * D], out_offset=None, in_=source,
                                in_offset=bass.IndirectOffsetOnAxis(ap=index[:, j:j + 1], axis=0)).then_inc(done, 16)


def scatter_add_rows(pool, target, rows, index, done):
    for j in range(TB):
        pool.indirect_dma_start(out=target, out_offset=bass.IndirectOffsetOnAxis(ap=index[:, j:j + 1], axis=0),
                                in_=rows[:, j * D:(j + 1) * D], in_offset=None, bounds_check=ROWS - 1, oob_is_err=True,
                                compute_op=ALU.add).then_inc(done, 16)


def edge_pool_program(pool, gathers, end_index, target, y, stage, sems):
    index_ready, rows_used, rows_in, y_ready, sent = sems
    END = len(gathers)

    def gather(b, s, count):
        if later(b):
            pool.wait_ge(rows_used, b - 1)
        for i, (_, index, _) in enumerate(gathers):
            ins = pool.tensor_copy(stage[:, s, i, :], index[:, bass.ds(b * TB, TB)])
        ins.then_inc(index_ready, 1)
        pool.wait_ge(index_ready, count)
        pool.nop(nofuse=True)
        for i, (source, _, rows) in enumerate(gathers):
            gather_rows(pool, source, rows[:, s, :], stage[:, s, i, :], rows_in[s])

    def scatter(b, s, turn, count):
        if later(b):
            pool.wait_ge(sent[s], turn * (16 * TB))
        pool.tensor_copy(stage[:, s, END, :], end_index[:, bass.ds(b * TB, TB)]).then_inc(index_ready, 1)
        pool.wait_ge(y_ready, b + 1)
        pool.wait_ge(index_ready, count)
        pool.nop(nofuse=True)
        scatter_add_rows(pool, target, y[:, s, :], stage[:, s, END, :], sent[s])

    gather(0, 0, 1)
    gather(1, 1, 2)

    def both(b, s, turn):
        gather(b, s, b * 2 - 1)
        scatter(b - 2, s, turn - 1, b * 2)

    both(2, 0, 1)
    both(3, 1, 1)
    pairs = (EDGE_BLOCKS - 4) // 2
    with pool.Fori(0, pairs) as i:
        for s in range(2):
            both(i * 2 + (4 + s), s, i + 2)
    for b in range(4 + 2 * pairs, EDGE_BLOCKS):
        both(b, b % 2, b // 2)
    n = 2 * EDGE_BLOCKS - 2
    for b in (EDGE_BLOCKS - 2, EDGE_BLOCKS - 1):
        n += 1
        scatter(b, b % 2, b // 2, n)
    for s in range(2):
        pool.wait_ge(sent[s], 16 * TB * len(range(s, EDGE_BLOCKS, 2)))


def attend_layer0(nc, k, x):
    target = k.table[0]
    with phase(nc, "layer0") as (sb, ps, sem):
        xs_rows, xd_rows = sb("xs_rows", [P, 2, BLK]), sb("xd_rows", [P, 2, BLK])
        stage = sb("stage", [P, 2, 3, TB], I32)
        xs, xd = sb("xs", [P, 2, BLK]), sb("xd", [P, 2, BLK])
        same, nv = sb("same", [P, 2, BLK]), sb("nv", [P, 2, BLK])
        small, leaky, ex = sb("small", [P, BLK]), sb("leaky", [P, BLK]), sb("ex", [P, BLK])
        alpha, msg = sb("alpha", [P, BLK]), sb("msg", [P, BLK])
        asum, osum = sb("asum", [P, 2, BLK]), sb("osum", [P, 2, BLK])
        inv, out = sb("inv", [P, BLK]), sb("out", [P, 2, BLK])
        y = sb("y", [P, 2, BLK])
        p_s, p_d, p_z, p_h, p_o = ps("p_s", [P, 512]), ps("p_d", [P, 512]), ps("p_z", [P, 512]), ps("p_h", [P, 512]), ps("p_o", [P, 512])
        index_ready, rows_used, y_ready = sem("index_ready"), sem("rows_used"), sem("y_ready")
        rows_in, sent, lines_in = ([sem(f"{n}{s}") for s in range(2)] for n in ("rows_in", "sent", "lines_in"))
        x_ready, z_done, h_done, small_done, leaky_done = sem("x_ready"), sem("z_done"), sem("h_done"), sem("small_done"), sem("leaky_done")
        ex_done, alpha_done, msg_done, asum_done, osum_done = sem("ex_done"), sem("alpha_done"), sem("msg_done"), sem("asum_done"), sem("osum_done")
        inv_done, out_done, turned_out = sem("inv_done"), sem("out_done"), sem("turned_out")
        block = nc.Block()
        block.__enter__()

        @block.gpsimd
        def _(pool):
            edge_pool_program(pool, [(x, k.at_key[0], xs_rows), (x, k.at_other[0], xd_rows)], k.at_end[0], target, y, stage,
                              (index_ready, rows_used, rows_in, y_ready, sent))

        @block.sync
        def _(sp):
            def load(b, s, turn):
                if later(b):
                    sp.wait_ge(osum_done, b - 1)
                cols = bass.ds(b * BLK, BLK)
                sp.dma_start(same[:, s, :], as_row(k.same_dram[0][cols]).to_broadcast([P, BLK])).then_inc(lines_in[s], 16)
                sp.dma_start(nv[:, s, :], as_row(k.nv_dram[0][cols]).to_broadcast([P, BLK])).then_inc(lines_in[s], 16)

            run_blocks(sp, EDGE_BLOCKS, load)

        @block.tensor
        def _(pe):
            def products(b, s, turn):
                pe.wait_ge(rows_in[s], turn * (32 * TB) + 32 * TB)
                if later(b, 1):
                    pe.wait_ge(x_ready, b)
                for rows, out_ in ((xs_rows, p_s), (xd_rows, p_d)):
                    for j in range(TB):
                        ins = pe.transpose(out_[:, j * P:(j + 1) * P], rows[:, s, j * D:(j + 1) * D], k.ident[:, :])
                ins.then_inc(rows_used, 1)
                pe.wait_ge(x_ready, b + 1)
                if later(b, 1):
                    pe.wait_ge(leaky_done, b)
                pe.matmul(p_z[:, :], k.W["attLW"], xs[:, s, :], start=True, stop=False)
                pe.matmul(p_z[:, :], k.W["attRW"], xd[:, s, :], start=False, stop=True).then_inc(z_done, 1)
                if later(b, 1):
                    pe.wait_ge(msg_done, b)
                pe.matmul(p_h[:, :], k.W["W0T"], xd[:, s, :], start=True, stop=True).then_inc(h_done, 1)

            def turn_out(b, s):
                pe.wait_ge(out_done, b + 1)
                if later(b, 1):
                    pe.wait_ge(y_ready, b)
                for j in range(TB):
                    ins = pe.transpose(p_o[:, j * P:(j + 1) * P], out[:, s, j * P:(j + 1) * P], k.ident[:, :])
                ins.then_inc(turned_out, 1)

            def both(b, s, turn):
                products(b, s, turn)
                if later(b, 1):
                    turn_out(b - 1, 1 - s)

            run_blocks(pe, EDGE_BLOCKS, both)
            turn_out(EDGE_BLOCKS - 1, (EDGE_BLOCKS - 1) % 2)

        @block.scalar
        def _(act):
            def keep_y(b, s, turn):
                act.wait_ge(turned_out, b + 1)
                if later(b):
                    act.wait_ge(sent[s], turn * (16 * TB))
                act.copy(y[:, s, :], p_o[:, :]).then_inc(y_ready, 1)

            def body(b, s, turn):
                act.wait_ge(rows_used, b + 1)
                if later(b):
                    act.wait_ge(h_done, b - 1)
                act.copy(xs[:, s, :], p_s[:, :])
                act.copy(xd[:, s, :], p_d[:, :]).then_inc(x_ready, 1)
                act.wait_ge(leaky_done, b + 1)
                if later(b, 1):
                    act.wait_ge(alpha_done, b)
                act.activation(ex[:, :], leaky[:, :], ACT.Exp).then_inc(ex_done, 1)
                if later(b, 1):
                    keep_y(b - 1, 1 - s, turn if s else turn - 1)

            run_blocks(act, EDGE_BLOCKS, body)
            keep_y(EDGE_BLOCKS - 1, (EDGE_BLOCKS - 1) % 2, (EDGE_BLOCKS - 1) // 2)

        @block.vector
        def _(dve):
            def body(b, s, turn):
                more = later(b, 1)
                dve.wait_ge(z_done, b + 1)
                if more:
                    dve.wait_ge(leaky_done, b)
                dve.tensor_scalar(small[:, :], p_z[:, :], 0.2, None, ALU.mult).then_inc(small_done, 1)
                dve.wait_ge(small_done, b + 1)
                if more:
                    dve.wait_ge(ex_done, b)
                dve.tensor_tensor(leaky[:, :], p_z[:, :], small[:, :], ALU.max).then_inc(leaky_done, 1)
                dve.wait_ge(lines_in[s], turn * 32 + 32)
                dve.wait_ge(ex_done, b + 1)
                if more:
                    dve.wait_ge(osum_done, b)
                dve.tensor_tensor(alpha[:, :], ex[:, :], nv[:, s, :], ALU.mult).then_inc(alpha_done, 1)
                dve.wait_ge(alpha_done, b + 1)
                dve.wait_ge(h_done, b + 1)
                dve.tensor_tensor(msg[:, :], alpha[:, :], p_h[:, :], ALU.mult).then_inc(msg_done, 1)
                first = isinstance(b, int) and b == 0
                dve.tensor_tensor_scan(asum[:, s, :], same[:, s, :], alpha[:, :], 0.0 if first else asum[:, 1 - s, BLK - 1:BLK],
                                       ALU.mult, ALU.add).then_inc(asum_done, 1)
                dve.wait_ge(msg_done, b + 1)
                dve.tensor_tensor_scan(osum[:, s, :], same[:, s, :], msg[:, :], 0.0 if first else osum[:, 1 - s, BLK - 1:BLK],
                                       ALU.mult, ALU.add).then_inc(osum_done, 1)
                dve.wait_ge(asum_done, b + 1)
                if more:
                    dve.wait_ge(out_done, b)
                dve.reciprocal(inv[:, :], asum[:, s, :]).then_inc(inv_done, 1)
                dve.wait_ge(inv_done, b + 1)
                dve.wait_ge(osum_done, b + 1)
                if later(b):
                    dve.wait_ge(turned_out, b - 1)
                dve.scalar_tensor_tensor(out[:, s, :], inv[:, :], 1e-16, osum[:, s, :], ALU.add, ALU.mult).then_inc(out_done, 1)

            run_blocks(dve, EDGE_BLOCKS, body)

        block.__exit__(None, None, None)


def aggregate(nc, k, title, source, target, weight, relu, mean):
    with phase(nc, title) as (sb, ps, sem):
        rows = sb("rows", [P, 2, BLK])
        stage = sb("stage", [P, 2, 2, TB], I32)
        same, wrow = sb("same", [P, 2, BLK]), sb("wrow", [P, 2, BLK])
        ones = sb("ones_block", [P, BLK])
        msg, total = sb("msg", [P, 2, BLK]), sb("total", [P, 2, BLK])
        count, inv, avg = sb("count", [P, 2, BLK]), sb("inv", [P, BLK]), sb("avg", [P, 2, BLK])
        y = sb("y", [P, 2, BLK])
        p_x, p_y = ps("p_x", [P, 2, 512]), ps("p_y", [P, 2, 512])
        index_ready, rows_used, y_ready = sem("index_ready"), sem("rows_used"), sem("y_ready")
        rows_in, sent, lines_in = ([sem(f"{n}{s}") for s in range(2)] for n in ("rows_in", "sent", "lines_in"))
        msg_done, total_done, multiplied = sem("msg_done"), sem("total_done"), sem("multiplied")
        ones_set, count_done, inv_done, avg_done = sem("ones_set"), sem("count_done"), sem("inv_done"), sem("avg_done")
        sums, sums_done = (avg, avg_done) if mean else (total, total_done)
        lines = 1 if mean else 2
        block = nc.Block()
        block.__enter__()

        @block.gpsimd
        def _(pool):
            edge_pool_program(pool, [(source, k.at_other[1], rows)], k.at_end[1], target, y, stage,
                              (index_ready, rows_used, rows_in, y_ready, sent))

        @block.sync
        def _(sp):
            def load(b, s, turn):
                if later(b):
                    sp.wait_ge(sums_done, b - 1)
                cols = bass.ds(b * BLK, BLK)
                sp.dma_start(same[:, s, :], as_row(k.same_dram[1][cols]).to_broadcast([P, BLK])).then_inc(lines_in[s], 16)
                if not mean:
                    sp.dma_start(wrow[:, s, :], as_row(k.weight_dram[1][cols]).to_broadcast([P, BLK])).then_inc(lines_in[s], 16)

            run_blocks(sp, EDGE_BLOCKS, load)

        @block.tensor
        def _(pe):
            def body(b, s, turn):
                pe.wait_ge(rows_in[s], turn * (16 * TB) + 16 * TB)
                if later(b):
                    pe.wait_ge(msg_done, b - 1)
                for j in range(TB):
                    ins = pe.transpose(p_x[:, s, j * P:(j + 1) * P], rows[:, s, j * D:(j + 1) * D], k.ident[:, :])
                ins.then_inc(rows_used, 1)
                pe.wait_ge(sums_done, b + 1)
                if later(b):
                    pe.wait_ge(y_ready, b - 1)
                for j in range(TB):
                    ins = pe.matmul(p_y[:, s, j * D:(j + 1) * D], sums[:, s, j * P:(j + 1) * P], weight, start=True, stop=True)
                ins.then_inc(multiplied, 1)

            run_blocks(pe, EDGE_BLOCKS, body)

        @block.scalar
        def _(act):
            def body(b, s, turn):
                act.wait_ge(multiplied, b + 1)
                if later(b):
                    act.wait_ge(sent[s], turn * (16 * TB))
                act.copy(y[:, s, :], p_y[:, s, :]).then_inc(y_ready, 1)

            run_blocks(act, EDGE_BLOCKS, body)

        @block.vector
        def _(dve):
            if mean:
                dve.memset(ones[:, :], 1.0).then_inc(ones_set, 1)
                dve.wait_ge(ones_set, 1)

            def body(b, s, turn):
                first = isinstance(b, int) and b == 0
                dve.wait_ge(rows_used, b + 1)
                dve.wait_ge(lines_in[s], turn * (16 * lines) + 16 * lines)
                if later(b):
                    dve.wait_ge(total_done, b - 1)
                if mean:
                    if relu:
                        dve.tensor_scalar(msg[:, s, :], p_x[:, s, :], 0.0, None, ALU.max).then_inc(msg_done, 1)
                    else:
                        dve.tensor_copy(msg[:, s, :], p_x[:, s, :]).then_inc(msg_done, 1)
                elif relu:
                    dve.scalar_tensor_tensor(msg[:, s, :], p_x[:, s, :], 0.0, wrow[:, s, :], ALU.max, ALU.mult).then_inc(msg_done, 1)
                else:
                    dve.tensor_tensor(msg[:, s, :], p_x[:, s, :], wrow[:, s, :], ALU.mult).then_inc(msg_done, 1)
                if mean:
                    if later(b, 1):
                        dve.wait_ge(inv_done, b)
                        dve.wait_ge(count_done, b)
                    dve.tensor_tensor_scan(count[:, s, :], same[:, s, :], ones[:, :], 0.0 if first else count[:, 1 - s, BLK - 1:BLK],
                                           ALU.mult, ALU.add).then_inc(count_done, 1)
                dve.wait_ge(msg_done, b + 1)
                if later(b, 1):
                    dve.wait_ge(total_done, b)
                if later(b):
                    dve.wait_ge(multiplied, b - 1)
                dve.tensor_tensor_scan(total[:, s, :], same[:, s, :], msg[:, s, :], 0.0 if first else total[:, 1 - s, BLK - 1:BLK],
                                       ALU.mult, ALU.add).then_inc(total_done, 1)
                if mean:
                    dve.wait_ge(count_done, b + 1)
                    if later(b, 1):
                        dve.wait_ge(avg_done, b)
                    dve.reciprocal(inv[:, :], count[:, s, :]).then_inc(inv_done, 1)
                    dve.wait_ge(inv_done, b + 1)
                    dve.wait_ge(total_done, b + 1)
                    dve.tensor_tensor(avg[:, s, :], total[:, s, :], inv[:, :], ALU.mult).then_inc(avg_done, 1)

            run_blocks(dve, EDGE_BLOCKS, body)

        block.__exit__(None, None, None)


def attend_layer2(nc, k, source, target):
    with phase(nc, "layer2") as (sb, ps, sem):
        def two(name):
            return sb(name, [P, 2, BLK])

        xs_rows, xd_rows, xs, xd, same, y, out = (two(n) for n in ("xs_rows", "xd_rows", "xs", "xd", "same", "y", "out"))
        vs, vd, ssum, osum = (two(n) for n in ("vs", "vd", "ssum", "osum"))
        stage = sb("stage", [P, 2, 3, TB], I32)

        def one(name):
            return sb(name, [P, BLK])

        kd, dot1, dot0, self_score, reset, best = (one(n) for n in ("kd", "dot1", "dot0", "self_score", "reset", "best"))
        neg_self, weights, keep_w, pv, gv, vsum, den, inv, norm = (one(n) for n in ("neg_self", "weights", "keep_w", "pv", "gv", "vsum", "den", "inv", "norm"))
        top = sb("top", [P, 2, BLK + 1])
        gap = sb("gap", [P, 3, BLK])
        ex = sb("ex", [P, 3, BLK])
        p_s, p_d, p_qs, p_kd, p_qd, p_vs, p_vd, p_y = (ps(n, [P, 512]) for n in ("p_s", "p_d", "p_qs", "p_kd", "p_qd", "p_vs", "p_vd", "p_y"))
        index_ready, rows_used, y_ready = sem("index_ready"), sem("rows_used"), sem("y_ready")
        rows_in, sent, lines_in = ([sem(f"{n}{s}") for s in range(2)] for n in ("rows_in", "sent", "lines_in"))
        x_ready, qk_done, v_done, kd_ready, v_ready = sem("x_ready"), sem("qk_done"), sem("v_done"), sem("kd_ready"), sem("v_ready")
        dots_done, scored, self_ready = sem("dots_done"), sem("scored"), sem("self_ready")
        step, out_done, multiplied, gaps_done, ex_done = sem("step"), sem("out_done"), sem("multiplied"), sem("gaps_done"), sem("ex_done")
        block = nc.Block()
        block.__enter__()

        @block.gpsimd
        def _(pool):
            edge_pool_program(pool, [(source, k.at_other[1], xs_rows), (source, k.at_key[1], xd_rows)], k.at_end[1], target, y, stage,
                              (index_ready, rows_used, rows_in, y_ready, sent))

        @block.sync
        def _(sp):
            def load(b, s, turn):
                if later(b):
                    sp.wait_ge(out_done, b - 1)
                sp.dma_start(same[:, s, :], as_row(k.same_dram[1][bass.ds(b * BLK, BLK)]).to_broadcast([P, BLK])).then_inc(lines_in[s], 16)

            run_blocks(sp, EDGE_BLOCKS, load)

        @block.tensor
        def _(pe):
            def products(b, s, turn):
                pe.wait_ge(rows_in[s], turn * (32 * TB) + 32 * TB)
                if later(b, 1):
                    pe.wait_ge(gaps_done, b)
                for rows, out_ in ((xs_rows, p_s), (xd_rows, p_d)):
                    for j in range(TB):
                        ins = pe.transpose(out_[:, j * P:(j + 1) * P], rows[:, s, j * D:(j + 1) * D], k.ident[:, :])
                ins.then_inc(rows_used, 1)
                pe.wait_ge(x_ready, b + 1)
                pe.matmul(p_kd[:, :], k.W["Wk"], xd[:, s, :], start=True, stop=True)
                pe.matmul(p_qs[:, :], k.W["Wq"], xs[:, s, :], start=True, stop=True)
                pe.matmul(p_qd[:, :], k.W["Wq"], xd[:, s, :], start=True, stop=True).then_inc(qk_done, 1)
                if later(b, 1):
                    pe.wait_ge(v_ready, b)
                pe.matmul(p_vs[:, :], k.W["Wv"], xs[:, s, :], start=True, stop=True)
                pe.matmul(p_vd[:, :], k.W["Wv"], xd[:, s, :], start=True, stop=True).then_inc(v_done, 1)
                pe.wait_ge(dots_done, b * 2 + 2)
                pe.matmul(p_s[:, :], k.head[:, :], dot1[:, :], start=True, stop=True)
                pe.matmul(p_d[:, :], k.head[:, :], dot0[:, :], start=True, stop=True).then_inc(scored, 1)

            def project(b, s):
                pe.wait_ge(out_done, b + 1)
                if later(b, 1):
                    pe.wait_ge(y_ready, b)
                for j in range(TB):
                    ins = pe.matmul(p_y[:, j * D:(j + 1) * D], out[:, s, j * P:(j + 1) * P], k.W["Wo"], start=True, stop=True)
                ins.then_inc(multiplied, 1)

            def both(b, s, turn):
                products(b, s, turn)
                if later(b, 1):
                    project(b - 1, 1 - s)

            run_blocks(pe, EDGE_BLOCKS, both)
            project(EDGE_BLOCKS - 1, (EDGE_BLOCKS - 1) % 2)

        @block.scalar
        def _(act):
            def keep_y(b, s, turn):
                act.wait_ge(multiplied, b + 1)
                if later(b):
                    act.wait_ge(sent[s], turn * (16 * TB))
                act.copy(y[:, s, :], p_y[:, :]).then_inc(y_ready, 1)

            def body(b, s, turn):
                act.wait_ge(rows_used, b + 1)
                if later(b):
                    act.wait_ge(v_done, b - 1)
                act.copy(xs[:, s, :], p_s[:, :])
                act.copy(xd[:, s, :], p_d[:, :]).then_inc(x_ready, 1)
                act.wait_ge(qk_done, b + 1)
                if later(b, 1):
                    act.wait_ge(dots_done, b * 2)
                act.copy(kd[:, :], p_kd[:, :]).then_inc(kd_ready, 1)
                act.wait_ge(v_done, b + 1)
                if later(b):
                    act.wait_ge(out_done, b - 1)
                act.copy(vs[:, s, :], p_vs[:, :])
                act.copy(vd[:, s, :], p_vd[:, :]).then_inc(v_ready, 1)
                act.wait_ge(scored, b + 1)
                if later(b, 1):
                    act.wait_ge(gaps_done, b)
                act.mul(self_score[:, :], p_d[:, :], HID ** -0.5).then_inc(self_ready, 1)
                if later(b, 1):
                    keep_y(b - 1, 1 - s, turn if s else turn - 1)
                act.wait_ge(gaps_done, b + 1)
                if later(b, 1):
                    act.wait_ge(out_done, b)
                act.activation(ex[:, :, :].rearrange("p a c -> p (a c)"), gap[:, :, :].rearrange("p a c -> p (a c)"), ACT.Exp).then_inc(ex_done, 1)

            run_blocks(act, EDGE_BLOCKS, body)
            keep_y(EDGE_BLOCKS - 1, (EDGE_BLOCKS - 1) % 2, (EDGE_BLOCKS - 1) // 2)

        @block.vector
        def _(dve):
            STEPS = 18
            dve.memset(top[:, 1, BLK:BLK + 1], 0.0).then_inc(step, 1)

            def body(b, s, turn):
                first = isinstance(b, int) and b == 0
                n = 0

                def did(ins):
                    nonlocal n
                    n += 1
                    ins.then_inc(step, 1)

                def settle():
                    dve.wait_ge(step, b * STEPS + (n + 1))

                settle()
                dve.wait_ge(kd_ready, b + 1)
                if later(b, 1):
                    dve.wait_ge(scored, b)
                dve.tensor_tensor(dot1[:, :], p_qs[:, :], kd[:, :], ALU.mult).then_inc(dots_done, 1)
                dve.tensor_tensor(dot0[:, :], p_qd[:, :], kd[:, :], ALU.mult).then_inc(dots_done, 1)
                dve.wait_ge(lines_in[s], turn * 16 + 16)
                did(dve.tensor_scalar(reset[:, :], same[:, s, :], 1.0, BIG, ALU.subtract, ALU.mult))
                did(dve.tensor_copy(top[:, s, 0:1], top[:, 1 - s, BLK:BLK + 1]))
                dve.wait_ge(self_ready, b + 1)
                did(dve.scalar_tensor_tensor(best[:, :], p_s[:, :], HID ** -0.5, self_score[:, :], ALU.mult, ALU.max))
                settle()
                did(dve.tensor_tensor_scan(top[:, s, 1:BLK + 1], reset[:, :], best[:, :], top[:, s, 0:1], ALU.add, ALU.max))
                settle()
                if later(b, 1):
                    dve.wait_ge(ex_done, b)
                did(dve.tensor_tensor(reset[:, :], top[:, s, 0:BLK], top[:, s, 1:BLK + 1], ALU.subtract))
                settle()
                did(dve.tensor_tensor(gap[:, 2, :], reset[:, :], same[:, s, :], ALU.mult))
                did(dve.scalar_tensor_tensor(gap[:, 0, :], p_s[:, :], HID ** -0.5, top[:, s, 1:BLK + 1], ALU.mult, ALU.subtract))
                settle()
                dve.tensor_tensor(gap[:, 1, :], self_score[:, :], top[:, s, 1:BLK + 1], ALU.subtract).then_inc(gaps_done, 1)
                dve.wait_ge(ex_done, b + 1)
                did(dve.scalar_tensor_tensor(neg_self[:, :], same[:, s, :], 1.0, ex[:, 1, :], ALU.subtract, ALU.mult))
                did(dve.tensor_tensor(keep_w[:, :], ex[:, 2, :], same[:, s, :], ALU.mult))
                dve.wait_ge(v_ready, b + 1)
                did(dve.tensor_tensor(pv[:, :], ex[:, 0, :], vs[:, s, :], ALU.mult))
                settle()
                did(dve.tensor_tensor(gv[:, :], neg_self[:, :], vd[:, s, :], ALU.mult))
                did(dve.tensor_tensor(weights[:, :], ex[:, 0, :], neg_self[:, :], ALU.subtract))
                settle()
                did(dve.tensor_tensor(vsum[:, :], pv[:, :], gv[:, :], ALU.subtract))
                did(dve.tensor_tensor_scan(ssum[:, s, :], keep_w[:, :], weights[:, :], 0.0 if first else ssum[:, 1 - s, BLK - 1:BLK],
                                           ALU.mult, ALU.add))
                settle()
                did(dve.tensor_tensor_scan(osum[:, s, :], keep_w[:, :], vsum[:, :], 0.0 if first else osum[:, 1 - s, BLK - 1:BLK],
                                           ALU.mult, ALU.add))
                did(dve.tensor_scalar(den[:, :], ssum[:, s, :], 1e-8, None, ALU.add))
                return n

            def finish(b, s, n):
                def settle(extra):
                    dve.wait_ge(step, b * STEPS + (n + extra + 1))

                settle(0)
                dve.reciprocal(inv[:, :], den[:, :]).then_inc(step, 1)
                settle(1)
                dve.tensor_tensor(norm[:, :], osum[:, s, :], inv[:, :], ALU.mult).then_inc(step, 1)
                settle(2)
                if later(b):
                    dve.wait_ge(multiplied, b - 1)
                dve.tensor_tensor(out[:, s, :], norm[:, :], vd[:, s, :], ALU.subtract).then_inc(out_done, 1)

            def whole(b, s, turn):
                n = body(b, s, turn)
                assert n + 2 == STEPS, n
                finish(b, s, n)

            run_blocks(dve, EDGE_BLOCKS, whole)

        block.__exit__(None, None, None)


def node_pass(nc, k, title, a_table, u, b_table=None, store=None, dense=None, residual=None, target=None):
    norm = u != "relu"
    b_table = residual if residual is not None else b_table
    gated = dense is not None and dense[0] == "gated"
    with phase(nc, title) as (sb, ps, sem):
        a, bb, v, xn = (sb(n, [P, 2, BLK]) for n in ("a", "b", "v", "xn"))
        stats, mv = sb("stats", [P, 2, TB, 6]), sb("mv", [P, 2, TB, 2])
        shifted, rstd = sb("shifted", [P, 2, TB]), sb("rstd", [P, 2, TB])
        ut, gate, prod, ot, yo = (sb(n, [P, 2, BLK]) for n in ("ut", "gate", "prod", "ot", "yo"))
        p_t = ps("p_t", [P, 2, 512])
        p_m = [ps(f"p_m{i}", [P, 512]) for i in range(3 if gated else 1)]
        p_o = ps("p_o", [P, 2, 512])
        a_in, b_in = ([sem(f"{n}{s}") for s in range(2)] for n in ("a_in", "b_in"))
        v_done, stats_done, aggr_done, shift_done, rstd_done, u_done = (sem(n) for n in ("v_done", "stats_done", "aggr_done", "shift_done", "rstd_done", "u_done"))
        u_stored, y_stored = ([sem(f"{n}{s}") for s in range(2)] for n in ("u_stored", "y_stored"))
        turned, ut_ready, multiplied, gate_ready, prod_done, ot_done, turned_out, y_done = (
            sem(n) for n in ("turned", "ut_ready", "multiplied", "gate_ready", "prod_done", "ot_done", "turned_out", "y_done"))
        v = v if u == "norm_sum" else a
        a_used = {"norm": u_done, "norm_sum": v_done, "relu": turned}[u]
        last = NODE_BLOCKS - 1
        combine_lag = 2 if norm else 1
        full = (N - last * BLK) // TB
        block = nc.Block()
        block.__enter__()

        @block.sync
        def _(sp):
            def load(b, s, turn):
                if later(b):
                    sp.wait_ge(a_used, b - 1)
                sp.dma_start(a[:, s, :].rearrange("p (j c) -> p j c", j=TB), block_rows(a_table, b)).then_inc(a_in[s], 16)
                if b_table is not None:
                    if later(b):
                        sp.wait_ge(y_done if residual is not None else v_done, b - 1)
                    sp.dma_start(bb[:, s, :].rearrange("p (j c) -> p j c", j=TB), block_rows(b_table, b)).then_inc(b_in[s], 16)

            run_blocks(sp, NODE_BLOCKS, load)

        @block.gpsimd
        def _(pool):
            def rstd_of(b, s):
                pool.wait_ge(aggr_done, b * TB + TB)
                if later(b):
                    pool.wait_ge(u_done, b - 1)
                pool.tensor_tensor(shifted[:, s, :], mv[:, s, :, 1], k.eps[:, :], ALU.add).then_inc(shift_done, 1)
                pool.wait_ge(shift_done, b + 1)
                pool.tensor_tensor(rstd[:, s, :], shifted[:, s, :], k.neg_half[:, :], ALU.pow).then_inc(rstd_done, 1)

            def store_block(b, s, table, rows, done):
                if table.shape[0] == N and isinstance(b, int) and b == last:
                    pool.dma_start(table[b * BLK:N, :].rearrange("(p j) c -> p j c", j=TB),
                                   rows[0:full, s, :].rearrange("p (j c) -> p j c", j=TB)).then_inc(done[s], 16)
                else:
                    pool.dma_start(block_rows(table, b), rows[:, s, :].rearrange("p (j c) -> p j c", j=TB)).then_inc(done[s], 16)

            def body(b, s, turn):
                if norm:
                    rstd_of(b, s)
                if store is not None and later(b, 1):
                    pool.wait_ge(u_done, b)
                    pool.nop(nofuse=True)
                    store_block(b - 1, 1 - s, store, xn, u_stored)
                if dense is not None and later(b):
                    pool.wait_ge(y_done, b - 1)
                    pool.nop(nofuse=True)
                    store_block(b - 2, s, target, yo, y_stored)

            run_blocks(pool, last, body)
            if norm:
                rstd_of(last, last % 2)
            if store is not None:
                for b in (last - 1, last):
                    pool.wait_ge(u_done, b + 1)
                    store_block(b, b % 2, store, xn, u_stored)
                for s in range(2):
                    pool.wait_ge(u_stored[s], 16 * len(range(s, NODE_BLOCKS, 2)))
            if dense is not None:
                for b in (last - 2, last - 1, last):
                    pool.wait_ge(y_done, b + 1)
                    store_block(b, b % 2, target, yo, y_stored)
                for s in range(2):
                    pool.wait_ge(y_stored[s], 16 * len(range(s, NODE_BLOCKS, 2)))

        @block.vector
        def _(dve):
            def statistics(b, s, turn):
                dve.wait_ge(a_in[s], turn * 16 + 16)
                if u == "norm_sum":
                    dve.wait_ge(b_in[s], turn * 16 + 16)
                    if later(b):
                        dve.wait_ge(u_done, b - 1)
                    dve.scalar_tensor_tensor(v[:, s, :], a[:, s, :], 0.0, bb[:, s, :], ALU.max, ALU.add).then_inc(v_done, 1)
                    dve.wait_ge(v_done, b + 1)
                if later(b):
                    dve.wait_ge(aggr_done, b * TB - TB)
                for j in range(TB):
                    dve.bn_stats(stats[:, s, j, :], v[:, s, j * D:(j + 1) * D]).then_inc(stats_done, 1)
                if later(b):
                    dve.wait_ge(u_done, b - 1)
                dve.wait_ge(stats_done, b * TB + TB)
                dve.nop(nofuse=True)
                for j in range(TB):
                    dve.bn_aggr(mv[:, s, j, :], stats[:, s, j, :]).then_inc(aggr_done, 1)

            def normalise(b, s, turn):
                dve.wait_ge(rstd_done, b + 1)
                if store is not None and later(b):
                    dve.wait_ge(u_stored[s], turn * 16)
                if dense is not None and later(b):
                    dve.wait_ge(turned, b - 1)
                for j in range(TB):
                    ins = dve.tensor_scalar(xn[:, s, j * D:(j + 1) * D], v[:, s, j * D:(j + 1) * D], mv[:, s, j, 0:1], rstd[:, s, j:j + 1],
                                            ALU.subtract, ALU.mult)
                ins.then_inc(u_done, 1)

            def combine(b, s, turn):
                dve.wait_ge(multiplied, b + 1)
                if later(b):
                    dve.wait_ge(turned_out, b - 1)
                if gated:
                    i = dense[1]
                    dve.wait_ge(gate_ready, b + 1)
                    if later(b):
                        dve.wait_ge(ot_done, b - 1)
                    dve.scalar_tensor_tensor(prod[:, s, :], p_m[2][:, :], k.col_of(f"fc{i}3_b"), gate[:, s, :], ALU.add, ALU.mult).then_inc(prod_done, 1)
                    dve.wait_ge(prod_done, b + 1)
                    dve.scalar_tensor_tensor(ot[:, s, :], p_m[0][:, :], k.bsum[:, i - 1:i], prod[:, s, :], ALU.add, ALU.add).then_inc(ot_done, 1)
                elif dense[3]:
                    dve.scalar_tensor_tensor(ot[:, s, :], p_m[0][:, :], dense[2], ut[:, s, :], ALU.add, ALU.add).then_inc(ot_done, 1)
                else:
                    dve.tensor_scalar(ot[:, s, :], p_m[0][:, :], dense[2], None, ALU.add).then_inc(ot_done, 1)

            def add_residual(b, s, turn):
                dve.wait_ge(turned_out, b + 1)
                dve.wait_ge(b_in[s], turn * 16 + 16)
                if later(b):
                    dve.wait_ge(y_stored[s], turn * 16)
                dve.tensor_tensor(yo[:, s, :], p_o[:, s, :], bb[:, s, :], ALU.add).then_inc(y_done, 1)

            def body(b, s, turn):
                before = (b - 1, 1 - s, turn if s else turn - 1)
                if norm:
                    statistics(b, s, turn)
                    if later(b, 1):
                        normalise(*before)
                if dense is not None and later(b, combine_lag):
                    combine(*(before if combine_lag == 1 else (b - 2, s, turn - 1)))
                if residual is not None and later(b):
                    add_residual(b - 2, s, turn - 1)

            run_blocks(dve, NODE_BLOCKS, body)
            ends = [(b, b % 2, b // 2) for b in (last - 1, last)]
            if norm:
                normalise(*ends[1])
            if dense is not None:
                for e in ends[2 - combine_lag:]:
                    combine(*e)
            if residual is not None:
                for e in ends:
                    add_residual(*e)

        if dense is not None:
            @block.tensor
            def _(pe):
                def turn_in(b, s, turn):
                    if norm:
                        pe.wait_ge(u_done, b + 1)
                    else:
                        pe.wait_ge(a_in[s], turn * 16 + 16)
                    if later(b):
                        pe.wait_ge(ut_ready, b - 1)
                    rows = xn if norm else a
                    for j in range(TB):
                        ins = pe.transpose(p_t[:, s, j * P:(j + 1) * P], rows[:, s, j * D:(j + 1) * D], k.ident[:, :])
                    ins.then_inc(turned, 1)

                def multiply(b, s):
                    pe.wait_ge(ut_ready, b + 1)
                    if later(b, 1):
                        pe.wait_ge(ot_done, b)
                    if gated:
                        for m in (1, 2, 0):
                            ins = pe.matmul(p_m[m][:, :], k.W[f"fc{dense[1]}{m + 1}"], ut[:, s, :], start=True, stop=True)
                    else:
                        ins = pe.matmul(p_m[0][:, :], dense[1], ut[:, s, :], start=True, stop=True)
                    ins.then_inc(multiplied, 1)

                def turn_out(b, s):
                    pe.wait_ge(ot_done, b + 1)
                    if later(b):
                        pe.wait_ge(y_done, b - 1)
                    for j in range(TB):
                        ins = pe.transpose(p_o[:, s, j * D:(j + 1) * D], ot[:, s, j * P:(j + 1) * P], k.ident[:, :])
                    ins.then_inc(turned_out, 1)

                def body(b, s, turn):
                    turn_in(b, s, turn)
                    if later(b, 1):
                        turn_out(b - 1, 1 - s)
                    multiply(b, s)

                run_blocks(pe, NODE_BLOCKS, body)
                turn_out(last, last % 2)

            @block.scalar
            def _(act):
                def body(b, s, turn):
                    act.wait_ge(turned, b + 1)
                    if later(b):
                        act.wait_ge(multiplied, b - 1)
                        act.wait_ge(ot_done, b - 1)
                    if norm:
                        act.copy(ut[:, s, :], p_t[:, s, :]).then_inc(ut_ready, 1)
                    else:
                        act.activation(ut[:, s, :], p_t[:, s, :], ACT.Relu).then_inc(ut_ready, 1)
                    if residual is None and later(b, 1):
                        keep_y(b - 1, 1 - s, turn if s else turn - 1)
                    if gated:
                        act.wait_ge(multiplied, b + 1)
                        if later(b):
                            act.wait_ge(prod_done, b - 1)
                        act.activation(gate[:, s, :], p_m[1][:, :], ACT.Identity, bias=k.col_of(f"fc{dense[1]}2_b")).then_inc(gate_ready, 1)

                def keep_y(b, s, turn):
                    act.wait_ge(turned_out, b + 1)
                    if later(b):
                        act.wait_ge(y_stored[s], turn * 16)
                    act.copy(yo[:, s, :], p_o[:, s, :]).then_inc(y_done, 1)

                run_blocks(act, NODE_BLOCKS, body)
                if residual is None:
                    keep_y(last, last % 2, last // 2)

        block.__exit__(None, None, None)


def ffn_pass(nc, k, sum_table, x_table, store, weight, bias, target):
    with phase(nc, "ffn") as (sb, ps, sem):
        def two(name):
            return sb(name, [P, 2, BLK])

        a, xb, xn, xt, yt, zn, zg, v, x3, ut, ot, yo = (two(n) for n in ("a", "xb", "xn", "xt", "yt", "zn", "zg", "v", "x3", "ut", "ot", "yo"))
        hidden = sb("hidden", [P, 4, BLK])
        xplus = two("xplus")
        g2_block, b2_block = sb("g2_block", [P, BLK]), sb("b2_block", [P, BLK])
        stats = [sb(f"stats{i}", [P, 2, TB, 6]) for i in range(3)]
        mv = [sb(f"mv{i}", [P, 2, TB, 2]) for i in range(3)]
        shifted, rstd = [sb(f"shifted{i}", [P, 2, TB]) for i in range(3)], [sb(f"rstd{i}", [P, 2, TB]) for i in range(3)]
        p_t, p_h, p_f, p_z, p_u = ps("p_t", [P, 512]), ps("p_h", [P, 2, 512]), ps("p_f", [P, 512]), ps("p_z", [P, 2, 512]), ps("p_u", [P, 512])
        p_m = ps("p_m", [P, 512])
        a_in, x_in, u_stored, y_stored = ([sem(f"{n}{s}") for s in range(2)] for n in ("a_in", "x_in", "u_stored", "y_stored"))
        stats_done, aggr_done, shift_done, rstd_done = ([sem(f"{n}{i}") for i in range(3)] for n in ("stats_done", "aggr_done", "shift_done", "rstd_done"))
        tiled, xn_done, turned, xt_ready, h_done, gelu_done, f_done, yt_done = (
            sem(n) for n in ("tiled", "xn_done", "turned", "xt_ready", "h_done", "gelu_done", "f_done", "yt_done"))
        z_turned, zn_done, zg_done, xplus_done, v_done, x3_done, u_turned, ut_ready = (
            sem(n) for n in ("z_turned", "zn_done", "zg_done", "xplus_done", "v_done", "x3_done", "u_turned", "ut_ready"))
        multiplied, ot_done, turned_out, y_done = (sem(n) for n in ("multiplied", "ot_done", "turned_out", "y_done"))
        last = NODE_BLOCKS - 1
        block = nc.Block()
        block.__enter__()

        def steps(eng, stages, total=NODE_BLOCKS):
            def one(b, s, turn):
                for lag, f in stages:
                    if not isinstance(b, int) or 0 <= b - lag < total:
                        f(b - lag, (s - lag) % 2, turn if lag == 0 else (turn - 1 if lag == 2 or s == 0 else turn))

            first = 4
            for b in range(first):
                one(b, b % 2, b // 2)
            pairs = (total - first) // 2
            with eng.Fori(0, pairs) as i:
                for s in range(2):
                    one(i * 2 + (first + s), s, i + first // 2)
            for b in range(first + 2 * pairs, total + 2):
                one(b, b % 2, b // 2)

        @block.sync
        def _(sp):
            def load(b, s, turn):
                if later(b):
                    sp.wait_ge(xn_done, b - 1)
                sp.dma_start(a[:, s, :].rearrange("p (j c) -> p j c", j=TB), block_rows(sum_table, b)).then_inc(a_in[s], 16)
                if later(b):
                    sp.wait_ge(xplus_done, b - 1)
                sp.dma_start(xb[:, s, :].rearrange("p (j c) -> p j c", j=TB), block_rows(x_table, b)).then_inc(x_in[s], 16)

            run_blocks(sp, NODE_BLOCKS, load)

        @block.gpsimd
        def _(pool):
            def rstd_of(i, used):
                def f(b, s, turn):
                    pool.wait_ge(aggr_done[i], b * TB + TB)
                    if later(b):
                        pool.wait_ge(used, b - 1)
                    pool.tensor_tensor(shifted[i][:, s, :], mv[i][:, s, :, 1], k.eps[:, :], ALU.add).then_inc(shift_done[i], 1)
                    pool.wait_ge(shift_done[i], b + 1)
                    pool.tensor_tensor(rstd[i][:, s, :], shifted[i][:, s, :], k.neg_half[:, :], ALU.pow).then_inc(rstd_done[i], 1)
                return f

            def stores(b, s, turn):
                pool.wait_ge(x3_done, b + 1)
                pool.nop(nofuse=True)
                pool.dma_start(block_rows(store, b), x3[:, s, :].rearrange("p (j c) -> p j c", j=TB)).then_inc(u_stored[s], 16)

            def store_y(b, s, turn):
                pool.wait_ge(y_done, b + 1)
                pool.nop(nofuse=True)
                pool.dma_start(block_rows(target, b), yo[:, s, :].rearrange("p (j c) -> p j c", j=TB)).then_inc(y_stored[s], 16)

            steps(pool, [(0, rstd_of(0, xn_done)), (1, rstd_of(1, zn_done)), (1, rstd_of(2, x3_done)), (1, stores), (2, store_y)])
            for s in range(2):
                n = 16 * len(range(s, NODE_BLOCKS, 2))
                pool.wait_ge(u_stored[s], n)
                pool.wait_ge(y_stored[s], n)

        @block.vector
        def _(dve):
            for j in range(TB):
                dve.tensor_copy(g2_block[:, j * D:(j + 1) * D], k.g2[:, :]).then_inc(tiled, 1)
                dve.tensor_copy(b2_block[:, j * D:(j + 1) * D], k.b2[:, :]).then_inc(tiled, 1)
            dve.wait_ge(tiled, 2 * TB)

            def statistics(i, b, s, rows, used):
                if later(b):
                    dve.wait_ge(aggr_done[i], b * TB - TB)
                for j in range(TB):
                    dve.bn_stats(stats[i][:, s, j, :], rows[:, s, j * D:(j + 1) * D]).then_inc(stats_done[i], 1)
                if later(b):
                    dve.wait_ge(used, b - 1)
                dve.wait_ge(stats_done[i], b * TB + TB)
                dve.nop(nofuse=True)
                for j in range(TB):
                    dve.bn_aggr(mv[i][:, s, j, :], stats[i][:, s, j, :]).then_inc(aggr_done[i], 1)

            def normalise(i, b, s, out_, rows, done):
                dve.wait_ge(rstd_done[i], b + 1)
                for j in range(TB):
                    ins = dve.tensor_scalar(out_[:, s, j * D:(j + 1) * D], rows[:, s, j * D:(j + 1) * D], mv[i][:, s, j, 0:1], rstd[i][:, s, j:j + 1],
                                            ALU.subtract, ALU.mult)
                ins.then_inc(done, 1)

            def stage_a1(b, s, turn):
                dve.wait_ge(a_in[s], turn * 16 + 16)
                statistics(0, b, s, a, xn_done)

            def stage_a2(b, s, turn):
                if later(b):
                    dve.wait_ge(turned, b - 1)
                normalise(0, b, s, xn, a, xn_done)

            def stage_a3(b, s, turn):
                dve.wait_ge(f_done, b + 1)
                if later(b):
                    dve.wait_ge(z_turned, b - 1)
                dve.scalar_tensor_tensor(yt[:, s, :], p_f[:, :], k.col_of("bf2"), xt[:, s, :], ALU.add, ALU.add).then_inc(yt_done, 1)

            def stage_b1(b, s, turn):
                dve.wait_ge(z_turned, b + 1)
                statistics(1, b, s, p_z, zn_done)
                dve.wait_ge(x_in[s], turn * 16 + 16)
                if later(b):
                    dve.wait_ge(v_done, b - 1)
                dve.tensor_tensor(xplus[:, s, :], xb[:, s, :], b2_block[:, :], ALU.add).then_inc(xplus_done, 1)

            def stage_b2(b, s, turn):
                if later(b):
                    dve.wait_ge(zg_done, b - 1)
                normalise(1, b, s, zn, p_z, zn_done)
                dve.wait_ge(zn_done, b + 1)
                if later(b):
                    dve.wait_ge(v_done, b - 1)
                dve.tensor_tensor(zg[:, s, :], zn[:, s, :], g2_block[:, :], ALU.mult).then_inc(zg_done, 1)
                dve.wait_ge(zg_done, b + 1)
                dve.wait_ge(xplus_done, b + 1)
                if later(b):
                    dve.wait_ge(x3_done, b - 1)
                dve.tensor_tensor(v[:, s, :], zg[:, s, :], xplus[:, s, :], ALU.add).then_inc(v_done, 1)
                dve.wait_ge(v_done, b + 1)
                statistics(2, b, s, v, x3_done)

            def stage_b3(b, s, turn):
                if later(b):
                    dve.wait_ge(u_stored[s], turn * 16)
                    dve.wait_ge(u_turned, b - 1)
                normalise(2, b, s, x3, v, x3_done)

            def stage_c(b, s, turn):
                dve.wait_ge(multiplied, b + 1)
                if later(b):
                    dve.wait_ge(turned_out, b - 1)
                dve.tensor_scalar(ot[:, s, :], p_m[:, :], bias, None, ALU.add).then_inc(ot_done, 1)

            steps(dve, [(0, stage_a1), (1, stage_b1), (0, stage_a2), (1, stage_b2), (2, stage_c), (0, stage_a3), (1, stage_b3)])

        @block.tensor
        def _(pe):
            def turn_in(b, s, turn):
                pe.wait_ge(xn_done, b + 1)
                if later(b, 1):
                    pe.wait_ge(xt_ready, b)
                for j in range(TB):
                    ins = pe.transpose(p_t[:, j * P:(j + 1) * P], xn[:, s, j * D:(j + 1) * D], k.ident[:, :])
                ins.then_inc(turned, 1)

            def ffn(b, s, turn):
                pe.wait_ge(xt_ready, b + 1)
                for c in range(4):
                    if c >= 2 or later(b, 1):
                        pe.wait_ge(gelu_done, b * 4 + (c - 1))
                    pe.matmul(p_h[:, c % 2, :], k.W["Wf1"][:, c * D:(c + 1) * D], xt[:, s, :], start=True, stop=True).then_inc(h_done, 1)
                    if c >= 1:
                        second(b, c - 1)
                second(b, 3).then_inc(f_done, 1)

            def second(b, c):
                pe.wait_ge(gelu_done, b * 4 + (c + 1))
                if c == 0 and later(b, 1):
                    pe.wait_ge(yt_done, b)
                return pe.matmul(p_f[:, :], k.W["Wf2"][:, c, :], hidden[:, c, :], start=c == 0, stop=c == 3)

            def turn_z(b, s, turn):
                pe.wait_ge(yt_done, b + 1)
                if later(b):
                    pe.wait_ge(zn_done, b - 1)
                for j in range(TB):
                    ins = pe.transpose(p_z[:, s, j * D:(j + 1) * D], yt[:, s, j * P:(j + 1) * P], k.ident[:, :])
                ins.then_inc(z_turned, 1)

            def turn_u(b, s, turn):
                pe.wait_ge(x3_done, b + 1)
                if later(b, 1):
                    pe.wait_ge(y_done, b)
                for j in range(TB):
                    ins = pe.transpose(p_u[:, j * P:(j + 1) * P], x3[:, s, j * D:(j + 1) * D], k.ident[:, :])
                ins.then_inc(u_turned, 1)

            def last_product(b, s, turn):
                pe.wait_ge(ut_ready, b + 1)
                if later(b, 1):
                    pe.wait_ge(ot_done, b)
                pe.matmul(p_m[:, :], weight, ut[:, s, :], start=True, stop=True).then_inc(multiplied, 1)

            def turn_y(b, s, turn):
                pe.wait_ge(ot_done, b + 1)
                for j in range(TB):
                    ins = pe.transpose(p_u[:, j * D:(j + 1) * D], ot[:, s, j * P:(j + 1) * P], k.ident[:, :])
                ins.then_inc(turned_out, 1)

            steps(pe, [(1, turn_z), (0, turn_in), (2, turn_u), (2, last_product), (0, ffn), (2, turn_y)])

        @block.scalar
        def _(act):
            def take_x(b, s, turn):
                act.wait_ge(turned, b + 1)
                if later(b):
                    act.wait_ge(yt_done, b - 1)
                act.activation(xt[:, s, :], p_t[:, :], ACT.Identity, scale=k.col_of("g1"), bias=k.col_of("b1")).then_inc(xt_ready, 1)

            def gelus(b, s, turn):
                for c in range(4):
                    act.wait_ge(h_done, b * 4 + (c + 1))
                    if later(b, 1):
                        act.wait_ge(f_done, b)
                    act.activation(hidden[:, c, :], p_h[:, c % 2, :], ACT.Gelu, bias=k.col_of(f"bf1_{c}")).then_inc(gelu_done, 1)

            def take_u(b, s, turn):
                act.wait_ge(u_turned, b + 1)
                if later(b):
                    act.wait_ge(multiplied, b - 1)
                act.copy(ut[:, s, :], p_u[:, :]).then_inc(ut_ready, 1)

            def keep_y(b, s, turn):
                act.wait_ge(turned_out, b + 1)
                if later(b):
                    act.wait_ge(y_stored[s], turn * 16)
                act.copy(yo[:, s, :], p_u[:, :]).then_inc(y_done, 1)

            steps(act, [(0, take_x), (2, take_u), (0, gelus), (2, keep_y)])

        block.__exit__(None, None, None)


VECTORS = ["fc11_b", "conv1_b", "fc12_b", "fc13_b", "fc21_b", "conv2_b", "fc22_b", "fc23_b", "bo", "bf2", "g1", "b1",
           "b0_3", "b1_3", "b2_3", "bf1_0", "bf1_1", "bf1_2", "bf1_3", "attL", "attR"]


def build(nc, a, out):
    k = Kit()
    w = {
        "fc11": a["L1_gnn_fc11_w"], "fc12": a["L1_gnn_fc12_w"], "fc13": a["L1_gnn_fc13_w"], "conv1": a["L1_gnn_conv1_w"],
        "fc21": a["L1_gnn_fc21_w"], "fc22": a["L1_gnn_fc22_w"], "fc23": a["L1_gnn_fc23_w"], "conv2": a["L1_gnn_conv2_w"],
        "Wq": a["L2_gnn_Wq"], "Wk": a["L2_gnn_Wk"], "Wv": a["L2_gnn_Wv"], "Wo": a["L2_gnn_Wo"], "Wf1": a["L2_gnn_Wf1"],
        "Wf2": a["L2_gnn_Wf2"], "W0": a["L0_gnn_W"],
        "Ws0": a["L3_gnn_Ws0"], "Wn0": a["L3_gnn_Wn0"], "Ws1": a["L3_gnn_Ws1"], "Wn1": a["L3_gnn_Wn1"],
        "Ws2": a["L3_gnn_Ws2"], "Wn2": a["L3_gnn_Wn2"], "g2": a["L2_gnn_g2"], "b2": a["L2_gnn_b2"],
        "fc11_b": a["L1_gnn_fc11_b"], "conv1_b": a["L1_gnn_conv1_b"], "fc12_b": a["L1_gnn_fc12_b"], "fc13_b": a["L1_gnn_fc13_b"],
        "fc21_b": a["L1_gnn_fc21_b"], "conv2_b": a["L1_gnn_conv2_b"], "fc22_b": a["L1_gnn_fc22_b"], "fc23_b": a["L1_gnn_fc23_b"],
        "bo": a["L2_gnn_bo"], "bf2": a["L2_gnn_bf2"], "g1": a["L2_gnn_g1"], "b1": a["L2_gnn_b1"],
        "b0_3": a["L3_gnn_b0"], "b1_3": a["L3_gnn_b1"], "b2_3": a["L3_gnn_b2"],
        "attL": a["L0_gnn_att"][:, :, 0:HID], "attR": a["L0_gnn_att"][:, :, HID:2 * HID],
    }
    for c in range(4):
        w[f"bf1_{c}"] = a["L2_gnn_bf1"][c * D:(c + 1) * D]
    k.vec_names = VECTORS

    def dram(name, shape, dt=F32):
        return nc.dram_tensor(name, shape, dt).ap()

    k.key_dram = [dram(f"keys{i}", (EPAD,), I32) for i in range(2)]
    k.oth_dram = [dram(f"others{i}", (EPAD,), I32) for i in range(2)]
    k.w_dram = dram("edge_weights", (EPAD,))
    k.sorted_dram = [dram(f"sorted{i}", (EPAD + 2, 4)) for i in range(2)]
    k.same_dram = [dram(f"same{i}", (EPAD,)) for i in range(2)]
    k.weight_dram = [dram(f"weight{i}", (EPAD,)) for i in range(2)]
    k.nv_dram = [dram(f"nv{i}", (EPAD,)) for i in range(2)]
    k.table = [dram(f"table{i}", (ROWS, D)) for i in range(2)]
    k.x1, k.x2, k.x3 = (dram(n, (NPAD, D)) for n in ("x1", "x2", "x3"))

    with ExitStack() as ctx:
        def sb(name, shape, dt=F32):
            return ctx.enter_context(nc.sbuf_tensor(name, shape, dt))

        k.W = {}
        squares = ["fc11", "fc12", "fc13", "conv1", "fc21", "fc22", "fc23", "conv2", "Wq", "Wk", "Wv", "Wo", "W0T", "Ws0T", "Wn0T",
                   "Ws1T", "Wn1T", "Ws2T", "Wn2T", "WvT", "attLW", "attRW", "Wvo"]
        all_w = sb("all_w", [P, len(squares), D])
        for i, name in enumerate(squares):
            k.W[name] = all_w[:, i, :]
        k.W["Wf1"] = sb("Wf1", [P, 4 * D])[:, :]
        k.W["Wf2"] = sb("Wf2", [P, 4, D])[:, :, :]
        k.vec = sb("vec", [P, len(VECTORS)])
        k.bsum = sb("bsum", [P, 2])
        k.g2, k.b2 = sb("g2", [P, D]), sb("b2", [P, D])
        k.ident, k.ident16 = sb("ident", [P, P]), sb("ident16", [P, P], F16)
        k.before, k.above, k.head = sb("before", [P, P]), sb("above", [P, P]), sb("head_mask", [P, P])
        k.row_iota, k.col_iota = sb("row_iota", [P, P], F16), sb("col_iota", [P, NCOL], F16)
        k.part_iota = sb("part_iota", [P, 1])
        k.neg_half, k.eps = sb("neg_half", [P, TB]), sb("eps", [P, TB])
        k.ones = sb("ones", [P, NCOL])
        k.at_key = [sb(f"at_key{i}", [P, TILES], I32) for i in range(2)]
        k.at_other = [sb(f"at_other{i}", [P, TILES], I32) for i in range(2)]
        k.at_end = [sb(f"at_end{i}", [P, TILES], I32) for i in range(2)]
        k.payload = [sb(f"payload{i}", [P, TILES, 4]) for i in range(2)]
        k.col_of = lambda name: k.vec[:, VECTORS.index(name):VECTORS.index(name) + 1]

        setup(nc, k, a["x"], a["src"], a["dst"], a["edge_weight1"], a["node_vec"], w)
        for which in range(2):
            sort_edges(nc, k, which)
            sorted_lists(nc, k, which)
        first, second = k.table
        col = k.col_of
        attend_layer0(nc, k, a["x"])
        node_pass(nc, k, "own1", first, "norm", store=k.x1, dense=("gated", 1), target=second)
        aggregate(nc, k, "conv1", k.x1, second, k.W["conv1"], relu=False, mean=False)
        node_pass(nc, k, "own2", second, "relu", dense=("gated", 2), target=first)
        aggregate(nc, k, "conv2", second, first, k.W["conv2"], relu=True, mean=False)
        node_pass(nc, k, "value", first, "norm_sum", b_table=k.x1, store=k.x2, dense=("linear", k.W["Wvo"], col("bo"), True), target=second)
        attend_layer2(nc, k, k.x2, second)
        ffn_pass(nc, k, second, k.x2, k.x3, k.W["Ws0T"], col("b0_3"), first)
        aggregate(nc, k, "sage0", k.x3, first, k.W["Wn0T"], relu=False, mean=True)
        node_pass(nc, k, "own4", first, "relu", dense=("linear", k.W["Ws1T"], col("b1_3"), True), target=second)
        aggregate(nc, k, "sage1", first, second, k.W["Wn1T"], relu=True, mean=True)
        node_pass(nc, k, "own5", second, "relu", dense=("linear", k.W["Ws2T"], col("b2_3"), False), residual=k.x3, target=first)
        aggregate(nc, k, "sage2", second, first, k.W["Wn2T"], relu=True, mean=True)
        node_pass(nc, k, "last", first, "norm", store=out)


_INS = ["x", "src", "dst", "edge_weight1", "node_vec", "L0_gnn_W", "L0_gnn_att"] \
    + [f"L1_gnn_{n}_{t}" for n in ("fc11", "fc12", "fc13", "conv1", "fc21", "fc22", "fc23", "conv2") for t in "wb"] \
    + [f"L2_gnn_{n}" for n in ("Wq", "Wk", "Wv", "Wo", "bo", "Wf1", "bf1", "Wf2", "bf2", "g1", "b1", "g2", "b2")] \
    + [f"L3_gnn_{n}{i}" for i in range(3) for n in ("Ws", "Wn", "b")]


def kernel(**inputs):
    import numpy as _np
    import concourse.bacc as _bacc
    from concourse import mybir as _mybir
    from concourse.bass_utils import run_bass_kernel_spmd as _run

    nc = _bacc.Bacc("TRN2", target_bir_lowering=False, num_devices=1)
    arrays, args = {}, {}
    for name in _INS:
        v = _np.ascontiguousarray(inputs[name])
        arrays[f"in_{name}"] = v
        args[name] = nc.dram_tensor(f"in_{name}", v.shape, _mybir.dt.from_np(v.dtype), kind="ExternalInput").ap()
    out = nc.dram_tensor("out_0", (N, D), _mybir.dt.float32, kind="ExternalOutput").ap()
    build(nc, args, out)
    r = _run(nc, [arrays], core_ids=[0])
    return r.results[0]["out_0"]
```

```python
from contextlib import ExitStack, contextmanager

import concourse.bass as bass
from concourse import mybir

ALU = mybir.AluOpType
ACT = mybir.ActivationFunctionType
F32 = mybir.dt.float32
F16 = mybir.dt.float16
I32 = mybir.dt.int32

P = 128
D = 128
N = 50000
E = 25000
TB = 4
BLK = TB * P
NODE_BLOCKS = -(-N // BLK)
NPAD = NODE_BLOCKS * BLK
TILES = -(-E // BLK) * TB
EDGE_BLOCKS = TILES // TB
EPAD = TILES * P
HALF = TILES // 2
ROWS = NPAD + EPAD
NCOL = -(-N // P)
PAD_KEY = NCOL * P - 1
HEADS, HID = 8, 16
EPS = 1e-5
BIG = 1e30
assert PAD_KEY >= N and PAD_KEY < NPAD and TILES % 2 == 0 and HALF <= P


class Kit:
    pass


@contextmanager
def phase(nc, title):
    with ExitStack() as ctx:
        sems = []

        def sb(name, shape, dt=F32):
            return ctx.enter_context(nc.sbuf_tensor(f"{title}_{name}", shape, dt))

        def ps(name, shape, dt=F32):
            return ctx.enter_context(nc.psum_tensor(f"{title}_{name}", shape, dt))

        def sem(name):
            sems.append(nc.alloc_semaphore(f"{title}_{name}"))
            return sems[-1]

        yield sb, ps, sem
        nc.clear_and_free_semaphores(sems)
        nc.all_engine_barrier()


def run_blocks(eng, blocks, body, unroll=2):
    first = 4
    for b in range(first):
        body(b, b % unroll, b // unroll)
    rounds = (blocks - first) // unroll
    with eng.Fori(0, rounds) as i:
        for s in range(unroll):
            body(i * unroll + (first + s), s, i + first // unroll)
    for b in range(first + rounds * unroll, blocks):
        body(b, b % unroll, b // unroll)


def back(lag, b, s, turn, unroll=4):
    turns_back = (lag - s + unroll - 1) // unroll
    return b - lag, (s - lag) % unroll, turn - turns_back if turns_back > 0 else turn


def later(b, lag=2):
    return not isinstance(b, int) or b >= lag


def block_rows(table, b):
    return table[bass.ds(b * BLK, BLK), :].rearrange("(p j) c -> p j c", j=TB)


def as_row(v):
    return v.rearrange("(a c) -> a c", a=1)


def setup(nc, k, x, src, dst, edge_w, node_vec, w):
    R = len(k.vec_names)
    with phase(nc, "setup") as (sb, ps, sem):
        rc = sb("rc", [P, 2, P], I32)
        rcs = sb("rcs", [P, 2, P], I32)
        head = sb("head", [P, P])
        vec_rows = sb("vec_rows", [P, D])
        raw = sb("raw", [P, 9, D])
        attx = sb("attx", [P, 2, D])
        zeros = sb("zeros", [P, 12544])
        pads = sb("pads", [1, 2, P], I32)
        guard = sb("guard", [1, 2, 4])
        by_tile = sb("by_tile", [HALF, 4, 2, P], I32)
        by_tile_f = sb("by_tile_f", [HALF, 5, 2, P])
        dst_i = sb("dst_i", [P, TILES], I32)
        dst_stage = sb("dst_stage", [P, 2, TB], I32)
        nv = sb("nv", [P, 2, TB])
        pt = ps("pt", [P, 2, 512])
        pw = ps("pw", [P, 512])
        pads_set, iota_done, shifted, masks = sem("pads_set"), sem("iota_done"), sem("shifted"), sem("masks")
        weights_in, padded, lists_in, converted = sem("weights_in"), sem("padded"), sem("lists_in"), sem("converted")
        tables_in, pe_turn, copied = sem("tables_in"), sem("pe_turn"), sem("copied")
        attx_done, sums = sem("attx_done"), sem("sums")
        staged, nv_in = sem("staged"), [sem("nv_in0"), sem("nv_in1")]
        nv_kept = sem("nv_kept")
        block = nc.Block()
        block.__enter__()

        lists = [(src, k.key_dram[0]), (dst, k.key_dram[1]), (src, k.oth_dram[0]), (dst, k.oth_dram[1])]
        direct = ["fc11", "fc12", "fc13", "conv1", "fc21", "fc22", "fc23", "conv2", "Wq", "Wk", "Wv", "Wo"]
        turned = ["W0", "Ws0", "Wn0", "Ws1", "Wn1", "Ws2", "Wn2", "Wv"]
        n_in = [0]

        @block.sync
        def _(sp):
            sp.wait_ge(pads_set, 5)
            n = 0
            for a, out in lists:
                sp.dma_start(out[0:E].rearrange("(p c) -> p c", p=8), a.rearrange("(p c) -> p c", p=8)).then_inc(padded, 16)
                sp.dma_start(as_row(out[E:EPAD]), pads[0:1, 0 if n < 2 else 1, 0:EPAD - E]).then_inc(padded, 16)
                n += 1
            sp.dma_start(k.w_dram[0:E].rearrange("(p c) -> p c", p=8), edge_w.rearrange("(p c) o -> p (c o)", p=8)).then_inc(padded, 16)
            sp.dma_start(as_row(k.w_dram[E:EPAD]), zeros[0:1, 0:EPAD - E]).then_inc(padded, 16)
            for s in range(2):
                sp.dma_start(k.sorted_dram[s][0:1, :], guard[0:1, 0, :]).then_inc(tables_in, 16)
                sp.dma_start(k.sorted_dram[s][EPAD + 1:EPAD + 2, :], guard[0:1, 1, :]).then_inc(tables_in, 16)
            sp.wait_ge(padded, 16 * 10)
            for i, a in enumerate([k.key_dram[0], k.key_dram[1], k.oth_dram[0], k.oth_dram[1]]):
                sp.dma_start(by_tile[:, i, :, :], a.rearrange("(h t p) -> t h p", h=2, p=P)).then_inc(lists_in, 16)
            sp.dma_start(by_tile_f[:, 4, :, :], k.w_dram.rearrange("(h t p) -> t h p", h=2, p=P)).then_inc(lists_in, 16)
            for c in range(5):
                rows = slice(c * (N // 5), (c + 1) * (N // 5))
                sp.dma_start(k.table[0][rows, :].rearrange("(p r) c -> p (r c)", p=16),
                             x[rows, :].rearrange("(p r) c -> p (r c)", p=16)).then_inc(tables_in, 16)
            sp.dma_start(k.table[0][N:NPAD, :].rearrange("(p r) c -> p (r c)", p=16),
                         zeros[0:16, 0:(NPAD - N) // 16 * D]).then_inc(tables_in, 16)
            for s in range(2):
                for h in range(2):
                    rows = slice(NPAD + h * (EPAD // 2), NPAD + (h + 1) * (EPAD // 2))
                    sp.dma_start(k.table[s][rows, :].rearrange("(p r) c -> p (r c)", p=P), zeros[:, :]).then_inc(tables_in, 16)
            sp.wait_ge(tables_in, 16 * 14)

        @block.scalar
        def _(act):
            for name in direct:
                act.dma_start(k.W[name], w[name]).then_inc(weights_in, 16)
            for i, name in enumerate(turned):
                act.dma_start(raw[:, i, :], w[name]).then_inc(weights_in, 16)
            act.dma_start(k.W["Wf1"], w["Wf1"]).then_inc(weights_in, 16)
            act.dma_start(k.W["Wf2"], w["Wf2"].rearrange("(c p) n -> p c n", p=P)).then_inc(weights_in, 16)
            for r, name in enumerate(k.vec_names):
                v = w[name]
                if name in ("attL", "attR"):
                    act.dma_start(vec_rows[r:r + 1, :].rearrange("a (h d) -> a h d", h=HEADS), v).then_inc(weights_in, 16)
                else:
                    act.dma_start(vec_rows[r:r + 1, :], as_row(v)).then_inc(weights_in, 16)
            for out, v in ((k.g2, w["g2"]), (k.b2, w["b2"])):
                act.dma_start(out[:, :], as_row(v).to_broadcast([P, D])).then_inc(weights_in, 16)
            n_in[0] = len(direct) + len(turned) + 2 + R + 2
            act.wait_ge(weights_in, 16 * n_in[0])

        @block.gpsimd
        def _(pool):
            pool.memset(pads[:, 0, :], PAD_KEY).then_inc(pads_set, 1)
            pool.memset(pads[:, 1, :], 0).then_inc(pads_set, 1)
            pool.memset(guard[:, 0, :], -1.0).then_inc(pads_set, 1)
            pool.memset(guard[:, 1, :], -2.0).then_inc(pads_set, 1)
            pool.iota(rc[:, 0, :], [[0, P]], base=0, channel_multiplier=1).then_inc(iota_done, 1)
            pool.iota(rc[:, 1, :], [[1, P]], base=0, channel_multiplier=0).then_inc(iota_done, 1)
            pool.iota(k.col_iota[:, :], [[1, NCOL]], base=0, channel_multiplier=0, allow_small_or_imprecise_dtypes=True).then_inc(iota_done, 1)
            pool.memset(k.neg_half[:, :], -0.5).then_inc(iota_done, 1)
            pool.memset(k.eps[:, :], EPS).then_inc(iota_done, 1)
            pool.memset(k.ones[:, :], 1.0).then_inc(iota_done, 1)

            def gather_nv(b, s, turn):
                pool.wait_ge(staged, b + 1)
                pool.nop(nofuse=True)
                for j in range(TB):
                    pool.indirect_dma_start(out=nv[:, s, j:j + 1], out_offset=None, in_=node_vec.rearrange("(n a) -> n a", a=1),
                                            in_offset=bass.IndirectOffsetOnAxis(ap=dst_stage[:, s, j:j + 1], axis=0)).then_inc(nv_in[s], 16)

            run_blocks(pool, EDGE_BLOCKS, gather_nv)

        @block.tensor
        def _(pe):
            n = 0

            def turn(out, in_, width):
                nonlocal n
                if n >= 2:
                    pe.wait_ge(copied, n - 1)
                pe.transpose(pt[0:in_.shape[1], n % 2, 0:width], in_, k.ident[0:width, 0:width]).then_inc(pe_turn, 1)
                n += 1

            pe.wait_ge(masks, 6)
            pe.wait_ge(converted, 1)
            pe.wait_ge(lists_in, 16 * 5)
            for i in range(5):
                for h in range(2):
                    turn(None, by_tile_f[:, i, h, :], HALF)
            pe.wait_ge(weights_in, 16 * n_in[0])
            for i in range(len(turned)):
                turn(None, raw[:, i, :], P)
            turn(None, vec_rows[0:R, :], R)
            pe.wait_ge(attx_done, 2)
            for s in range(2):
                pe.matmul(pw[:, s * D:(s + 1) * D], raw[:, 0, :], attx[:, s, :], start=True, stop=True)
            pe.matmul(pw[:, 2 * D:3 * D], k.W["WvT"], k.W["Wo"], start=True, stop=True).then_inc(pe_turn, 1)

        @block.vector
        def _(dve):
            dve.memset(zeros[:, :], 0.0).then_inc(pads_set, 1)
            dve.wait_ge(iota_done, 6)
            dve.tensor_scalar(rcs[:, :, :], rc[:, :, :], 4, None, ALU.logical_shift_right).then_inc(shifted, 1)
            dve.tensor_copy(k.part_iota[:, :], rc[:, 0, 0:1]).then_inc(masks, 1)
            dve.tensor_tensor(k.ident[:, :], rc[:, 0, :], rc[:, 1, :], ALU.is_equal).then_inc(masks, 1)
            dve.tensor_tensor(k.before[:, :], rc[:, 1, :], rc[:, 0, :], ALU.is_lt).then_inc(masks, 1)
            dve.tensor_tensor(k.above[:, :], rc[:, 0, :], rc[:, 1, :], ALU.is_lt).then_inc(masks, 1)
            dve.tensor_copy(k.row_iota[:, :], rc[:, 1, :]).then_inc(masks, 1)
            dve.wait_ge(shifted, 1)
            dve.tensor_tensor(head[:, :], rcs[:, 0, :], rcs[:, 1, :], ALU.is_equal).then_inc(masks, 1)
            dve.wait_ge(masks, 6)
            dve.tensor_copy(k.ident16[:, :], k.ident[:, :]).then_inc(masks, 1)
            dve.tensor_copy(k.head[:, :], head[:, :]).then_inc(masks, 1)
            dve.wait_ge(lists_in, 16 * 5)
            dve.tensor_copy(by_tile_f[:, 0:4, :, :].rearrange("t i h p -> t (i h p)"),
                            by_tile[:, :, :, :].rearrange("t i h p -> t (i h p)")).then_inc(converted, 1)
            n = 0

            def take(out, width=P, rows=P):
                nonlocal n
                dve.wait_ge(pe_turn, n + 1)
                dve.tensor_copy(out, pt[0:rows, n % 2, 0:width]).then_inc(copied, 1)
                n += 1

            slot = [(k.payload[0], 0), (k.payload[1], 0), (k.payload[1], 1), (k.payload[0], 1)]
            for i in range(5):
                for h in range(2):
                    half = slice(h * HALF, (h + 1) * HALF)
                    if i < 4:
                        take(slot[i][0][:, half, slot[i][1]], HALF)
                    else:
                        take(k.payload[0][:, half, 2], HALF)
            for name in turned:
                take(k.W[name + "T"])
            take(k.vec[:, 0:R], R)
            dve.wait_ge(copied, n)
            al, ar = k.vec_names.index("attL"), k.vec_names.index("attR")
            dve.tensor_scalar(attx[:, 0, :], head[:, :], k.vec[:, al:al + 1], None, ALU.mult).then_inc(attx_done, 1)
            dve.tensor_scalar(attx[:, 1, :], head[:, :], k.vec[:, ar:ar + 1], None, ALU.mult).then_inc(attx_done, 1)
            for i, (a, b) in enumerate((("fc11_b", "conv1_b"), ("fc21_b", "conv2_b"))):
                a, b = k.vec_names.index(a), k.vec_names.index(b)
                dve.tensor_tensor(k.bsum[:, i:i + 1], k.vec[:, a:a + 1], k.vec[:, b:b + 1], ALU.add).then_inc(sums, 1)
            dve.tensor_copy(k.payload[1][:, :, 2], k.payload[0][:, :, 2]).then_inc(sums, 1)
            dve.tensor_copy(dst_i[:, :], k.payload[0][:, :, 1]).then_inc(sums, 1)
            dve.wait_ge(pe_turn, n + 1)
            for i, name in enumerate(("attLW", "attRW", "Wvo")):
                dve.tensor_copy(k.W[name], pw[:, i * D:(i + 1) * D]).then_inc(sums, 1)
            dve.wait_ge(sums, 4)

            def keep_nv(b, s, turn):
                if later(b):
                    dve.wait_ge(nv_in[s], turn * (16 * TB))
                    store_nv(b - 2, s)
                dve.tensor_copy(dst_stage[:, s, :], dst_i[:, bass.ds(b * TB, TB)]).then_inc(staged, 1)

            def store_nv(b, s):
                for pay in k.payload:
                    dve.tensor_copy(pay[:, bass.ds(b * TB, TB), 3], nv[:, s, :]).then_inc(nv_kept, 1)

            def keep(b, s, turn):
                keep_nv(b, s, turn)

            run_blocks(dve, EDGE_BLOCKS, keep)
            for b in (EDGE_BLOCKS - 2, EDGE_BLOCKS - 1):
                dve.wait_ge(nv_in[b % 2], (b // 2 + 1) * 16 * TB)
                store_nv(b, b % 2)

        block.__exit__(None, None, None)


def sort_edges(nc, k, which):
    pay, key_dram, out = k.payload[which], k.key_dram[which], k.sorted_dram[which]
    with phase(nc, f"sort{which}") as (sb, ps, sem):
        key_i = sb("key_i", [P, TILES], I32)
        bits = sb("bits", [P, 2, TILES], I32)
        kpart = sb("kpart", [P, TILES])
        kcol = sb("kcol", [P, TILES])
        oh_part = sb("oh_part", [P, 2, TB, P], F16)
        oh_col = sb("oh_col", [P, 2, TB, NCOL], F16)
        oh_turned = sb("oh_turned", [P, 2, P])
        counts = sb("counts", [P, NCOL])
        col_sum = sb("col_sum", [P, NCOL + 1])
        start = sb("start", [P, NCOL])
        base = sb("base", [P, 2, NCOL])
        key_row = sb("key_row", [P, 2, BLK], I32)
        junk = sb("junk", [P, TB, NCOL])
        junk2 = sb("junk2", [P, TB, P])
        found = sb("found", [P, 2, TB])
        rank = sb("rank", [P, 2, TB])
        place = sb("place", [P, 2, TB], I32)
        cargo = sb("cargo", [P, 2, TB, 4])
        key_now = sb("key_now", [P, 2, TB])
        total = ps("total", [P, 512])
        sums = ps("sums", [P, 2, 512])
        look = ps("look", [P, 2, 512])
        turned = ps("turned", [P, 2, 1024], F16)
        key_split, onehots, counted, step = sem("key_split"), sem("onehots"), sem("counted"), sem("step")
        onehots2, turned_ok, turned_kept = sem("onehots2"), sem("turned_ok"), sem("turned_kept")
        added, base_ready, looked, found_ok = sem("added"), sem("base_ready"), sem("looked"), sem("found_ok")
        rows_in = [sem("rows_in0"), sem("rows_in1")]
        keys_staged, ranked, cargo_ready = sem("keys_staged"), sem("ranked"), sem("cargo_ready")
        sent = [sem("sent0"), sem("sent1")]
        block = nc.Block()
        block.__enter__()

        @block.sync
        def _(sp):
            def load_rows(b, s, turn):
                if later(b):
                    sp.wait_ge(ranked, b * TB - TB)
                sp.dma_start(key_row[:, s, :], as_row(key_dram[bass.ds(b * BLK, BLK)]).to_broadcast([P, BLK])).then_inc(rows_in[s], 16)

            run_blocks(sp, EDGE_BLOCKS, load_rows)

        def make_onehots(dve, b, s, done):
            for j in range(TB):
                at = bass.ds(b * TB + j, 1)
                dve.tensor_scalar(oh_part[:, s, j, :], k.row_iota[:, :], kpart[:, at], None, ALU.is_equal).then_inc(done, 1)
                dve.tensor_scalar(oh_col[:, s, j, :], k.col_iota[:, :], kcol[:, at], None, ALU.is_equal).then_inc(done, 1)

        @block.vector
        def _(dve):
            dve.tensor_copy(key_i[:, :], pay[:, :, 0]).then_inc(key_split, 1)
            dve.wait_ge(key_split, 1)
            dve.tensor_scalar(bits[:, 0, :], key_i[:, :], P - 1, None, ALU.bitwise_and).then_inc(key_split, 1)
            dve.tensor_scalar(bits[:, 1, :], key_i[:, :], 7, None, ALU.logical_shift_right).then_inc(key_split, 1)
            dve.wait_ge(key_split, 3)
            dve.tensor_copy(kpart[:, :], bits[:, 0, :]).then_inc(key_split, 1)
            dve.tensor_copy(kcol[:, :], bits[:, 1, :]).then_inc(key_split, 1)
            dve.wait_ge(key_split, 5)

            def count(b, s, turn):
                if later(b):
                    dve.wait_ge(counted, b * TB - TB)
                make_onehots(dve, b, s, onehots)

            run_blocks(dve, EDGE_BLOCKS, count)
            dve.wait_ge(counted, TILES)
            dve.tensor_copy(counts[:, :], total[:, 0:NCOL]).then_inc(step, 1)
            dve.memset(col_sum[:, 0:1], 0.0).then_inc(step, 1)
            dve.wait_ge(counted, TILES + 1)
            dve.wait_ge(step, 2)
            dve.tensor_tensor_scan(col_sum[:, 1:NCOL + 1], k.ones[:, 0:NCOL], sums[:, 0, 0:NCOL], 0.0, ALU.mult, ALU.add).then_inc(step, 1)
            dve.wait_ge(step, 3)
            dve.tensor_tensor(start[:, :], sums[:, 1, 0:NCOL], col_sum[:, 0:NCOL], ALU.add).then_inc(step, 1)

            def stage(b, s):
                dve.tensor_copy(key_now[:, s, :], pay[:, bass.ds(b * TB, TB), 0]).then_inc(keys_staged, 1)

            def place_block(b, s, turn):
                if later(b):
                    dve.wait_ge(looked, b * TB - TB)
                    dve.wait_ge(found_ok, b * TB - TB)
                make_onehots(dve, b, s, onehots2)
                stage(b, s)
                dve.wait_ge(keys_staged, b + 1)
                dve.wait_ge(rows_in[s], turn * 16 + 16)
                if later(b, 1):
                    dve.wait_ge(ranked, b * TB)
                    dve.wait_ge(found_ok, b * TB)
                for j in range(TB):
                    dve.scalar_tensor_tensor(junk2[:, j, :], key_row[:, s, j * P:(j + 1) * P], key_now[:, s, j:j + 1], k.before[:, :],
                                             ALU.is_equal, ALU.mult, accum_out=rank[:, s, j:j + 1]).then_inc(ranked, 1)
                for j in range(TB):
                    dve.wait_ge(looked, b * TB + (j + 1))
                    dve.scalar_tensor_tensor(junk[:, j, :], look[:, j % 2, 0:NCOL], 1.0, oh_col[:, s, j, :],
                                             ALU.mult, ALU.mult, accum_out=found[:, s, j:j + 1]).then_inc(found_ok, 1)
                if later(b):
                    dve.wait_ge(sent[s], turn * (16 * TB))
                dve.wait_ge(found_ok, b * TB + TB)
                dve.wait_ge(ranked, b * TB + TB)
                dve.scalar_tensor_tensor(place[:, s, :], found[:, s, :], 1.0, rank[:, s, :], ALU.add, ALU.add).then_inc(cargo_ready, 1)
                dve.tensor_copy(cargo[:, s, :, :], pay[:, bass.ds(b * TB, TB), :]).then_inc(cargo_ready, 1)

            run_blocks(dve, EDGE_BLOCKS, place_block)

        @block.tensor
        def _(pe):
            def count(b, s, turn):
                for j in range(TB):
                    pe.wait_ge(onehots, b * (2 * TB) + 2 * (j + 1))
                    pe.matmul(total[:, 0:NCOL], oh_part[:, s, j, :], oh_col[:, s, j, :],
                              start=isinstance(b, int) and b == 0 and j == 0, stop=False, skip_group_check=True).then_inc(counted, 1)

            run_blocks(pe, EDGE_BLOCKS, count)
            pe.wait_ge(step, 1)
            pe.matmul(sums[:, 0, 0:NCOL], k.ones[:, 0:P], counts[:, :], start=True, stop=True)
            pe.matmul(sums[:, 1, 0:NCOL], k.above[:, :], counts[:, :], start=True, stop=True).then_inc(counted, 1)
            pe.wait_ge(step, 4)
            pe.matmul(total[:, 0:NCOL], k.ident[:, :], start[:, :], start=True, stop=False, skip_group_check=True).then_inc(added, 1)

            def place_block(b, s, turn):
                for j in range(TB):
                    pe.wait_ge(onehots2, b * (2 * TB) + 2 * (j + 1))
                    if j >= 2 or later(b, 1):
                        pe.wait_ge(turned_kept, b * TB + (j - 1))
                    pe.transpose(turned[:, j % 2, 0:P], oh_part[:, s, j, :], k.ident16[:, :]).then_inc(turned_ok, 1)
                    pe.wait_ge(base_ready, b * TB + (j + 1))
                    pe.matmul(total[:, 0:NCOL], oh_part[:, s, j, :], oh_col[:, s, j, :], start=False, stop=False,
                              skip_group_check=True).then_inc(added, 1)
                    pe.wait_ge(turned_kept, b * TB + (j + 1))
                    if j >= 2 or later(b, 1):
                        pe.wait_ge(found_ok, b * TB + (j - 1))
                    pe.matmul(look[:, j % 2, 0:NCOL], oh_turned[:, j % 2, :], base[:, j % 2, :], start=True, stop=True).then_inc(looked, 1)

            run_blocks(pe, EDGE_BLOCKS, place_block)


        @block.scalar
        def _(act):
            def keep(b, s, turn):
                for j in range(TB):
                    act.wait_ge(added, b * TB + (j + 1))
                    if j >= 2 or later(b, 1):
                        act.wait_ge(looked, b * TB + (j - 1))
                    act.copy(base[:, j % 2, :], total[:, 0:NCOL]).then_inc(base_ready, 1)
                    act.wait_ge(turned_ok, b * TB + (j + 1))
                    act.copy(oh_turned[:, j % 2, :], turned[:, j % 2, 0:P]).then_inc(turned_kept, 1)

            run_blocks(act, EDGE_BLOCKS, keep)

        @block.gpsimd
        def _(pool):
            def send(b, s, turn):
                pool.wait_ge(cargo_ready, b * 2 + 2)
                pool.nop(nofuse=True)
                for j in range(TB):
                    pool.indirect_dma_start(out=out[:, :], out_offset=bass.IndirectOffsetOnAxis(ap=place[:, s, j:j + 1], axis=0),
                                            in_=cargo[:, s, j, :], in_offset=None).then_inc(sent[s], 16)

            run_blocks(pool, EDGE_BLOCKS, send)
            for s in range(2):
                pool.wait_ge(sent[s], 16 * TB * len(range(s, EDGE_BLOCKS, 2)))

        block.__exit__(None, None, None)


def sorted_lists(nc, k, which):
    table = k.sorted_dram[which]
    with phase(nc, f"lists{which}") as (sb, ps, sem):
        words = sb("words", [HALF, 3, 2, P, 4])
        same = sb("same", [HALF, 2, P])
        is_end = sb("is_end", [HALF, 2, P])
        spare = sb("spare", [HALF, 2, P])
        diff = sb("diff", [HALF, 2, P])
        idx = sb("idx", [HALF, 3, 2, P])
        pt = ps("pt", [P, 2, 512])
        loaded, spare_set, step, ready = sem("loaded"), sem("spare_set"), sem("step"), sem("ready")
        stored, pe_turn, copied = sem("stored"), sem("pe_turn"), sem("copied")
        block = nc.Block()
        block.__enter__()

        @block.sync
        def _(sp):
            for i in range(3):
                first = (1, 0, 2)[i]
                sp.dma_start(words[:, i, :, :, :].rearrange("t h p w -> t h (p w)"),
                             table[first:first + EPAD, :].rearrange("(h t p) w -> t h (p w)", h=2, p=P)).then_inc(loaded, 16)
            sp.wait_ge(ready, 3)
            for a, src in ((k.same_dram[which], same), (k.weight_dram[which], idx[:, 0]), (k.nv_dram[which], idx[:, 1])):
                sp.dma_start(a.rearrange("(h t p) -> t h p", h=2, p=P), src[:, :, :] if src is same else src).then_inc(stored, 16)
            sp.wait_ge(stored, 16 * 3)

        @block.gpsimd
        def _(pool):
            pool.iota(spare[:, :, :], [[HALF * P, 2], [1, P]], base=NPAD, channel_multiplier=P,
                      allow_small_or_imprecise_dtypes=True).then_inc(spare_set, 1)

        @block.vector
        def _(dve):
            dve.wait_ge(loaded, 16 * 3)
            key = words[:, 0, :, :, 0]
            dve.tensor_tensor(same[:, :, :], key, words[:, 1, :, :, 0], ALU.is_equal).then_inc(ready, 1)
            dve.tensor_copy(idx[:, 0], words[:, 0, :, :, 2]).then_inc(ready, 1)
            dve.tensor_copy(idx[:, 1], words[:, 0, :, :, 3]).then_inc(ready, 1)
            dve.tensor_tensor(is_end[:, :, :], key, words[:, 2, :, :, 0], ALU.not_equal).then_inc(step, 1)
            dve.wait_ge(spare_set, 1)
            dve.tensor_tensor(diff[:, :, :], key, spare[:, :, :], ALU.subtract).then_inc(step, 1)
            dve.wait_ge(step, 2)
            dve.tensor_tensor(diff[:, :, :], diff[:, :, :], is_end[:, :, :], ALU.mult).then_inc(step, 1)
            dve.wait_ge(step, 3)
            dve.wait_ge(stored, 16 * 3)
            dve.tensor_tensor(idx[:, 2], diff[:, :, :], spare[:, :, :], ALU.add).then_inc(step, 1)
            dve.tensor_copy(idx[:, 1], words[:, 0, :, :, 1]).then_inc(step, 1)
            dve.tensor_scalar(idx[:, 0], key, float(N - 1), None, ALU.min).then_inc(step, 1)
            n = 0
            for out in (k.at_key[which], k.at_other[which], k.at_end[which]):
                for h in range(2):
                    dve.wait_ge(pe_turn, n + 1)
                    dve.tensor_copy(out[:, h * HALF:(h + 1) * HALF], pt[:, n % 2, 0:HALF]).then_inc(copied, 1)
                    n += 1

        @block.tensor
        def _(pe):
            pe.wait_ge(step, 6)
            n = 0
            for i in range(3):
                for h in range(2):
                    if n >= 2:
                        pe.wait_ge(copied, n - 1)
                    pe.transpose(pt[:, n % 2, 0:HALF], idx[:, i, h, :], k.ident[0:HALF, 0:HALF]).then_inc(pe_turn, 1)
                    n += 1

        block.__exit__(None, None, None)


def gather_rows(pool, source, rows, index, done):
    for j in range(TB):
        pool.indirect_dma_start(out=rows[:, j * D:(j + 1) * D], out_offset=None, in_=source,
                                in_offset=bass.IndirectOffsetOnAxis(ap=index[:, j:j + 1], axis=0)).then_inc(done, 16)


def scatter_add_rows(pool, target, rows, index, done):
    for j in range(TB):
        pool.indirect_dma_start(out=target, out_offset=bass.IndirectOffsetOnAxis(ap=index[:, j:j + 1], axis=0),
                                in_=rows[:, j * D:(j + 1) * D], in_offset=None, bounds_check=ROWS - 1, oob_is_err=True,
                                compute_op=ALU.add).then_inc(done, 16)


def edge_pool_program(pool, gathers, end_index, target, y, stage, sems):
    index_ready, rows_used, rows_in, y_ready, sent = sems
    END = len(gathers)

    def gather(b, s, count):
        if later(b):
            pool.wait_ge(rows_used, b - 1)
        for i, (_, index, _) in enumerate(gathers):
            ins = pool.tensor_copy(stage[:, s, i, :], index[:, bass.ds(b * TB, TB)])
        ins.then_inc(index_ready, 1)
        pool.wait_ge(index_ready, count)
        pool.nop(nofuse=True)
        for i, (source, _, rows) in enumerate(gathers):
            gather_rows(pool, source, rows[:, s, :], stage[:, s, i, :], rows_in[s])

    def scatter(b, s, turn, count):
        if later(b):
            pool.wait_ge(sent[s], turn * (16 * TB))
        pool.tensor_copy(stage[:, s, END, :], end_index[:, bass.ds(b * TB, TB)]).then_inc(index_ready, 1)
        pool.wait_ge(y_ready, b + 1)
        pool.wait_ge(index_ready, count)
        pool.nop(nofuse=True)
        scatter_add_rows(pool, target, y[:, s, :], stage[:, s, END, :], sent[s])

    gather(0, 0, 1)
    gather(1, 1, 2)

    def both(b, s, turn):
        gather(b, s, b * 2 - 1)
        scatter(b - 2, s, turn - 1, b * 2)

    both(2, 0, 1)
    both(3, 1, 1)
    pairs = (EDGE_BLOCKS - 4) // 2
    with pool.Fori(0, pairs) as i:
        for s in range(2):
            both(i * 2 + (4 + s), s, i + 2)
    for b in range(4 + 2 * pairs, EDGE_BLOCKS):
        both(b, b % 2, b // 2)
    n = 2 * EDGE_BLOCKS - 2
    for b in (EDGE_BLOCKS - 2, EDGE_BLOCKS - 1):
        n += 1
        scatter(b, b % 2, b // 2, n)
    for s in range(2):
        pool.wait_ge(sent[s], 16 * TB * len(range(s, EDGE_BLOCKS, 2)))


def attend_layer0(nc, k, x):
    target = k.table[0]
    with phase(nc, "layer0") as (sb, ps, sem):
        xs_rows, xd_rows = sb("xs_rows", [P, 2, BLK]), sb("xd_rows", [P, 2, BLK])
        stage = sb("stage", [P, 2, 3, TB], I32)
        xs, xd = sb("xs", [P, 2, BLK]), sb("xd", [P, 2, BLK])
        same, nv = sb("same", [P, 2, BLK]), sb("nv", [P, 2, BLK])
        small, leaky, ex = sb("small", [P, BLK]), sb("leaky", [P, BLK]), sb("ex", [P, BLK])
        alpha, msg = sb("alpha", [P, BLK]), sb("msg", [P, BLK])
        asum, osum = sb("asum", [P, 2, BLK]), sb("osum", [P, 2, BLK])
        inv, out = sb("inv", [P, BLK]), sb("out", [P, 2, BLK])
        y = sb("y", [P, 2, BLK])
        p_s, p_d, p_z, p_h, p_o = ps("p_s", [P, 512]), ps("p_d", [P, 512]), ps("p_z", [P, 512]), ps("p_h", [P, 512]), ps("p_o", [P, 512])
        index_ready, rows_used, y_ready = sem("index_ready"), sem("rows_used"), sem("y_ready")
        rows_in, sent, lines_in = ([sem(f"{n}{s}") for s in range(2)] for n in ("rows_in", "sent", "lines_in"))
        x_ready, z_done, h_done, small_done, leaky_done = sem("x_ready"), sem("z_done"), sem("h_done"), sem("small_done"), sem("leaky_done")
        ex_done, alpha_done, msg_done, asum_done, osum_done = sem("ex_done"), sem("alpha_done"), sem("msg_done"), sem("asum_done"), sem("osum_done")
        inv_done, out_done, turned_out = sem("inv_done"), sem("out_done"), sem("turned_out")
        block = nc.Block()
        block.__enter__()

        @block.gpsimd
        def _(pool):
            edge_pool_program(pool, [(x, k.at_key[0], xs_rows), (x, k.at_other[0], xd_rows)], k.at_end[0], target, y, stage,
                              (index_ready, rows_used, rows_in, y_ready, sent))

        @block.sync
        def _(sp):
            def load(b, s, turn):
                if later(b):
                    sp.wait_ge(osum_done, b - 1)
                cols = bass.ds(b * BLK, BLK)
                sp.dma_start(same[:, s, :], as_row(k.same_dram[0][cols]).to_broadcast([P, BLK])).then_inc(lines_in[s], 16)
                sp.dma_start(nv[:, s, :], as_row(k.nv_dram[0][cols]).to_broadcast([P, BLK])).then_inc(lines_in[s], 16)

            run_blocks(sp, EDGE_BLOCKS, load)

        @block.tensor
        def _(pe):
            def products(b, s, turn):
                pe.wait_ge(rows_in[s], turn * (32 * TB) + 32 * TB)
                if later(b, 1):
                    pe.wait_ge(x_ready, b)
                for rows, out_ in ((xs_rows, p_s), (xd_rows, p_d)):
                    for j in range(TB):
                        ins = pe.transpose(out_[:, j * P:(j + 1) * P], rows[:, s, j * D:(j + 1) * D], k.ident[:, :])
                ins.then_inc(rows_used, 1)
                pe.wait_ge(x_ready, b + 1)
                if later(b, 1):
                    pe.wait_ge(leaky_done, b)
                pe.matmul(p_z[:, :], k.W["attLW"], xs[:, s, :], start=True, stop=False)
                pe.matmul(p_z[:, :], k.W["attRW"], xd[:, s, :], start=False, stop=True).then_inc(z_done, 1)
                if later(b, 1):
                    pe.wait_ge(msg_done, b)
                pe.matmul(p_h[:, :], k.W["W0T"], xd[:, s, :], start=True, stop=True).then_inc(h_done, 1)

            def turn_out(b, s):
                pe.wait_ge(out_done, b + 1)
                if later(b, 1):
                    pe.wait_ge(y_ready, b)
                for j in range(TB):
                    ins = pe.transpose(p_o[:, j * P:(j + 1) * P], out[:, s, j * P:(j + 1) * P], k.ident[:, :])
                ins.then_inc(turned_out, 1)

            def both(b, s, turn):
                products(b, s, turn)
                if later(b, 1):
                    turn_out(b - 1, 1 - s)

            run_blocks(pe, EDGE_BLOCKS, both)
            turn_out(EDGE_BLOCKS - 1, (EDGE_BLOCKS - 1) % 2)

        @block.scalar
        def _(act):
            def keep_y(b, s, turn):
                act.wait_ge(turned_out, b + 1)
                if later(b):
                    act.wait_ge(sent[s], turn * (16 * TB))
                act.copy(y[:, s, :], p_o[:, :]).then_inc(y_ready, 1)

            def body(b, s, turn):
                act.wait_ge(rows_used, b + 1)
                if later(b):
                    act.wait_ge(h_done, b - 1)
                act.copy(xs[:, s, :], p_s[:, :])
                act.copy(xd[:, s, :], p_d[:, :]).then_inc(x_ready, 1)
                act.wait_ge(leaky_done, b + 1)
                if later(b, 1):
                    act.wait_ge(alpha_done, b)
                act.activation(ex[:, :], leaky[:, :], ACT.Exp).then_inc(ex_done, 1)
                if later(b, 1):
                    keep_y(b - 1, 1 - s, turn if s else turn - 1)

            run_blocks(act, EDGE_BLOCKS, body)
            keep_y(EDGE_BLOCKS - 1, (EDGE_BLOCKS - 1) % 2, (EDGE_BLOCKS - 1) // 2)

        @block.vector
        def _(dve):
            def body(b, s, turn):
                more = later(b, 1)
                dve.wait_ge(z_done, b + 1)
                if more:
                    dve.wait_ge(leaky_done, b)
                dve.tensor_scalar(small[:, :], p_z[:, :], 0.2, None, ALU.mult).then_inc(small_done, 1)
                dve.wait_ge(small_done, b + 1)
                if more:
                    dve.wait_ge(ex_done, b)
                dve.tensor_tensor(leaky[:, :], p_z[:, :], small[:, :], ALU.max).then_inc(leaky_done, 1)
                dve.wait_ge(lines_in[s], turn * 32 + 32)
                dve.wait_ge(ex_done, b + 1)
                if more:
                    dve.wait_ge(osum_done, b)
                dve.tensor_tensor(alpha[:, :], ex[:, :], nv[:, s, :], ALU.mult).then_inc(alpha_done, 1)
                dve.wait_ge(alpha_done, b + 1)
                dve.wait_ge(h_done, b + 1)
                dve.tensor_tensor(msg[:, :], alpha[:, :], p_h[:, :], ALU.mult).then_inc(msg_done, 1)
                first = isinstance(b, int) and b == 0
                dve.tensor_tensor_scan(asum[:, s, :], same[:, s, :], alpha[:, :], 0.0 if first else asum[:, 1 - s, BLK - 1:BLK],
                                       ALU.mult, ALU.add).then_inc(asum_done, 1)
                dve.wait_ge(msg_done, b + 1)
                dve.tensor_tensor_scan(osum[:, s, :], same[:, s, :], msg[:, :], 0.0 if first else osum[:, 1 - s, BLK - 1:BLK],
                                       ALU.mult, ALU.add).then_inc(osum_done, 1)
                dve.wait_ge(asum_done, b + 1)
                if more:
                    dve.wait_ge(out_done, b)
                dve.reciprocal(inv[:, :], asum[:, s, :]).then_inc(inv_done, 1)
                dve.wait_ge(inv_done, b + 1)
                dve.wait_ge(osum_done, b + 1)
                if later(b):
                    dve.wait_ge(turned_out, b - 1)
                dve.scalar_tensor_tensor(out[:, s, :], inv[:, :], 1e-16, osum[:, s, :], ALU.add, ALU.mult).then_inc(out_done, 1)

            run_blocks(dve, EDGE_BLOCKS, body)

        block.__exit__(None, None, None)


def aggregate(nc, k, title, source, target, weight, relu, mean):
    with phase(nc, title) as (sb, ps, sem):
        rows = sb("rows", [P, 2, BLK])
        stage = sb("stage", [P, 2, 2, TB], I32)
        same, wrow = sb("same", [P, 2, BLK]), sb("wrow", [P, 2, BLK])
        ones = sb("ones_block", [P, BLK])
        msg, total = sb("msg", [P, 2, BLK]), sb("total", [P, 2, BLK])
        count, inv, avg = sb("count", [P, 2, BLK]), sb("inv", [P, BLK]), sb("avg", [P, 2, BLK])
        y = sb("y", [P, 2, BLK])
        p_x, p_y = ps("p_x", [P, 2, 512]), ps("p_y", [P, 2, 512])
        index_ready, rows_used, y_ready = sem("index_ready"), sem("rows_used"), sem("y_ready")
        rows_in, sent, lines_in = ([sem(f"{n}{s}") for s in range(2)] for n in ("rows_in", "sent", "lines_in"))
        msg_done, total_done, multiplied = sem("msg_done"), sem("total_done"), sem("multiplied")
        ones_set, count_done, inv_done, avg_done = sem("ones_set"), sem("count_done"), sem("inv_done"), sem("avg_done")
        sums, sums_done = (avg, avg_done) if mean else (total, total_done)
        lines = 1 if mean else 2
        block = nc.Block()
        block.__enter__()

        @block.gpsimd
        def _(pool):
            edge_pool_program(pool, [(source, k.at_other[1], rows)], k.at_end[1], target, y, stage,
                              (index_ready, rows_used, rows_in, y_ready, sent))

        @block.sync
        def _(sp):
            def load(b, s, turn):
                if later(b):
                    sp.wait_ge(sums_done, b - 1)
                cols = bass.ds(b * BLK, BLK)
                sp.dma_start(same[:, s, :], as_row(k.same_dram[1][cols]).to_broadcast([P, BLK])).then_inc(lines_in[s], 16)
                if not mean:
                    sp.dma_start(wrow[:, s, :], as_row(k.weight_dram[1][cols]).to_broadcast([P, BLK])).then_inc(lines_in[s], 16)

            run_blocks(sp, EDGE_BLOCKS, load)

        @block.tensor
        def _(pe):
            def body(b, s, turn):
                pe.wait_ge(rows_in[s], turn * (16 * TB) + 16 * TB)
                if later(b):
                    pe.wait_ge(msg_done, b - 1)
                for j in range(TB):
                    ins = pe.transpose(p_x[:, s, j * P:(j + 1) * P], rows[:, s, j * D:(j + 1) * D], k.ident[:, :])
                ins.then_inc(rows_used, 1)
                pe.wait_ge(sums_done, b + 1)
                if later(b):
                    pe.wait_ge(y_ready, b - 1)
                for j in range(TB):
                    ins = pe.matmul(p_y[:, s, j * D:(j + 1) * D], sums[:, s, j * P:(j + 1) * P], weight, start=True, stop=True)
                ins.then_inc(multiplied, 1)

            run_blocks(pe, EDGE_BLOCKS, body)

        @block.scalar
        def _(act):
            def body(b, s, turn):
                act.wait_ge(multiplied, b + 1)
                if later(b):
                    act.wait_ge(sent[s], turn * (16 * TB))
                act.copy(y[:, s, :], p_y[:, s, :]).then_inc(y_ready, 1)

            run_blocks(act, EDGE_BLOCKS, body)

        @block.vector
        def _(dve):
            if mean:
                dve.memset(ones[:, :], 1.0).then_inc(ones_set, 1)
                dve.wait_ge(ones_set, 1)

            def body(b, s, turn):
                first = isinstance(b, int) and b == 0
                dve.wait_ge(rows_used, b + 1)
                dve.wait_ge(lines_in[s], turn * (16 * lines) + 16 * lines)
                if later(b):
                    dve.wait_ge(total_done, b - 1)
                if mean:
                    if relu:
                        dve.tensor_scalar(msg[:, s, :], p_x[:, s, :], 0.0, None, ALU.max).then_inc(msg_done, 1)
                    else:
                        dve.tensor_copy(msg[:, s, :], p_x[:, s, :]).then_inc(msg_done, 1)
                elif relu:
                    dve.scalar_tensor_tensor(msg[:, s, :], p_x[:, s, :], 0.0, wrow[:, s, :], ALU.max, ALU.mult).then_inc(msg_done, 1)
                else:
                    dve.tensor_tensor(msg[:, s, :], p_x[:, s, :], wrow[:, s, :], ALU.mult).then_inc(msg_done, 1)
                if mean:
                    if later(b, 1):
                        dve.wait_ge(inv_done, b)
                        dve.wait_ge(count_done, b)
                    dve.tensor_tensor_scan(count[:, s, :], same[:, s, :], ones[:, :], 0.0 if first else count[:, 1 - s, BLK - 1:BLK],
                                           ALU.mult, ALU.add).then_inc(count_done, 1)
                dve.wait_ge(msg_done, b + 1)
                if later(b, 1):
                    dve.wait_ge(total_done, b)
                if later(b):
                    dve.wait_ge(multiplied, b - 1)
                dve.tensor_tensor_scan(total[:, s, :], same[:, s, :], msg[:, s, :], 0.0 if first else total[:, 1 - s, BLK - 1:BLK],
                                       ALU.mult, ALU.add).then_inc(total_done, 1)
                if mean:
                    dve.wait_ge(count_done, b + 1)
                    if later(b, 1):
                        dve.wait_ge(avg_done, b)
                    dve.reciprocal(inv[:, :], count[:, s, :]).then_inc(inv_done, 1)
                    dve.wait_ge(inv_done, b + 1)
                    dve.wait_ge(total_done, b + 1)
                    dve.tensor_tensor(avg[:, s, :], total[:, s, :], inv[:, :], ALU.mult).then_inc(avg_done, 1)

            run_blocks(dve, EDGE_BLOCKS, body)

        block.__exit__(None, None, None)


def steps(eng, stages, total=NODE_BLOCKS):
    drain = max(lag for lag, _ in stages)
    first = -(-(drain + 4) // 4) * 4

    def one(n, s, turn):
        for lag, f in stages:
            if not isinstance(n, int) or 0 <= n - lag < total:
                f(*back(lag, n, s, turn))

    for n in range(first):
        one(n, n % 4, n // 4)
    rounds = (total - first) // 4
    with eng.Fori(0, rounds) as i:
        for s in range(4):
            one(i * 4 + (first + s), s, i + first // 4)
    for n in range(first + 4 * rounds, total + drain):
        one(n, n % 4, n // 4)


def attend_layer2(nc, k, source, target):
    with phase(nc, "layer2") as (sb, ps, sem):
        def two(name):
            return sb(name, [P, 2, BLK])

        xs_rows, xd_rows, xs, xd, same, y, out = (two(n) for n in ("xs_rows", "xd_rows", "xs", "xd", "same", "y", "out"))
        vs, vd, ssum, osum = (two(n) for n in ("vs", "vd", "ssum", "osum"))
        stage = sb("stage", [P, 2, 3, TB], I32)

        def one(name):
            return sb(name, [P, BLK])

        kd, dot1, dot0, self_score, reset, best = (one(n) for n in ("kd", "dot1", "dot0", "self_score", "reset", "best"))
        neg_self, weights, keep_w, pv, gv, vsum, den, inv, norm = (one(n) for n in ("neg_self", "weights", "keep_w", "pv", "gv", "vsum", "den", "inv", "norm"))
        top = sb("top", [P, 2, BLK + 1])
        gap = sb("gap", [P, 3, BLK])
        ex = sb("ex", [P, 3, BLK])
        p_s, p_d, p_qs, p_kd, p_qd, p_vs, p_vd, p_y = (ps(n, [P, 512]) for n in ("p_s", "p_d", "p_qs", "p_kd", "p_qd", "p_vs", "p_vd", "p_y"))
        index_ready, rows_used, y_ready = sem("index_ready"), sem("rows_used"), sem("y_ready")
        rows_in, sent, lines_in = ([sem(f"{n}{s}") for s in range(2)] for n in ("rows_in", "sent", "lines_in"))
        x_ready, qk_done, v_done, kd_ready, v_ready = sem("x_ready"), sem("qk_done"), sem("v_done"), sem("kd_ready"), sem("v_ready")
        dots_done, scored, self_ready = sem("dots_done"), sem("scored"), sem("self_ready")
        den_done, inv_done, norm_done = sem("den_done"), sem("inv_done"), sem("norm_done")
        step, out_done, multiplied, gaps_done, ex_done = sem("step"), sem("out_done"), sem("multiplied"), sem("gaps_done"), sem("ex_done")
        block = nc.Block()
        block.__enter__()

        @block.gpsimd
        def _(pool):
            edge_pool_program(pool, [(source, k.at_other[1], xs_rows), (source, k.at_key[1], xd_rows)], k.at_end[1], target, y, stage,
                              (index_ready, rows_used, rows_in, y_ready, sent))

        @block.sync
        def _(sp):
            def load(b, s, turn):
                if later(b):
                    sp.wait_ge(out_done, b - 1)
                sp.dma_start(same[:, s, :], as_row(k.same_dram[1][bass.ds(b * BLK, BLK)]).to_broadcast([P, BLK])).then_inc(lines_in[s], 16)

            run_blocks(sp, EDGE_BLOCKS, load)

        @block.tensor
        def _(pe):
            def products(b, s, turn):
                pe.wait_ge(rows_in[s], turn * (32 * TB) + 32 * TB)
                if later(b, 1):
                    pe.wait_ge(gaps_done, b)
                for rows, out_ in ((xs_rows, p_s), (xd_rows, p_d)):
                    for j in range(TB):
                        ins = pe.transpose(out_[:, j * P:(j + 1) * P], rows[:, s, j * D:(j + 1) * D], k.ident[:, :])
                ins.then_inc(rows_used, 1)
                pe.wait_ge(x_ready, b + 1)
                pe.matmul(p_kd[:, :], k.W["Wk"], xd[:, s, :], start=True, stop=True)
                pe.matmul(p_qs[:, :], k.W["Wq"], xs[:, s, :], start=True, stop=True)
                pe.matmul(p_qd[:, :], k.W["Wq"], xd[:, s, :], start=True, stop=True).then_inc(qk_done, 1)
                if later(b, 1):
                    pe.wait_ge(v_ready, b)
                pe.matmul(p_vs[:, :], k.W["Wv"], xs[:, s, :], start=True, stop=True)
                pe.matmul(p_vd[:, :], k.W["Wv"], xd[:, s, :], start=True, stop=True).then_inc(v_done, 1)
                pe.wait_ge(dots_done, b * 2 + 2)
                pe.matmul(p_s[:, :], k.head[:, :], dot1[:, :], start=True, stop=True)
                pe.matmul(p_d[:, :], k.head[:, :], dot0[:, :], start=True, stop=True).then_inc(scored, 1)

            def project(b, s):
                pe.wait_ge(out_done, b + 1)
                if later(b, 1):
                    pe.wait_ge(y_ready, b)
                for j in range(TB):
                    ins = pe.matmul(p_y[:, j * D:(j + 1) * D], out[:, s, j * P:(j + 1) * P], k.W["Wo"], start=True, stop=True)
                ins.then_inc(multiplied, 1)

            def both(b, s, turn):
                products(b, s, turn)
                if later(b, 1):
                    project(b - 1, 1 - s)

            run_blocks(pe, EDGE_BLOCKS, both)
            project(EDGE_BLOCKS - 1, (EDGE_BLOCKS - 1) % 2)

        @block.scalar
        def _(act):
            def keep_y(b, s, turn):
                act.wait_ge(multiplied, b + 1)
                if later(b):
                    act.wait_ge(sent[s], turn * (16 * TB))
                act.copy(y[:, s, :], p_y[:, :]).then_inc(y_ready, 1)

            def body(b, s, turn):
                act.wait_ge(rows_used, b + 1)
                if later(b):
                    act.wait_ge(v_done, b - 1)
                act.copy(xs[:, s, :], p_s[:, :])
                act.copy(xd[:, s, :], p_d[:, :]).then_inc(x_ready, 1)
                act.wait_ge(qk_done, b + 1)
                if later(b, 1):
                    act.wait_ge(dots_done, b * 2)
                act.copy(kd[:, :], p_kd[:, :]).then_inc(kd_ready, 1)
                act.wait_ge(v_done, b + 1)
                if later(b):
                    act.wait_ge(out_done, b - 1)
                act.copy(vs[:, s, :], p_vs[:, :])
                act.copy(vd[:, s, :], p_vd[:, :]).then_inc(v_ready, 1)
                act.wait_ge(scored, b + 1)
                if later(b, 1):
                    act.wait_ge(gaps_done, b)
                act.mul(self_score[:, :], p_d[:, :], HID ** -0.5).then_inc(self_ready, 1)
                act.wait_ge(gaps_done, b + 1)
                if later(b, 1):
                    act.wait_ge(den_done, b)
                act.activation(ex[:, :, :].rearrange("p a c -> p (a c)"), gap[:, :, :].rearrange("p a c -> p (a c)"), ACT.Exp).then_inc(ex_done, 1)
                if later(b, 1):
                    keep_y(b - 1, 1 - s, turn if s else turn - 1)

            run_blocks(act, EDGE_BLOCKS, body)
            keep_y(EDGE_BLOCKS - 1, (EDGE_BLOCKS - 1) % 2, (EDGE_BLOCKS - 1) // 2)

        @block.vector
        def _(dve):
            STEPS = 15
            dve.memset(top[:, 1, BLK:BLK + 1], 0.0).then_inc(step, 1)

            def invert(b):
                dve.wait_ge(den_done, b + 1)
                if later(b, 1):
                    dve.wait_ge(norm_done, b)
                dve.reciprocal(inv[:, :], den[:, :]).then_inc(inv_done, 1)

            def finish(b, s):
                dve.wait_ge(inv_done, b + 1)
                if later(b, 1):
                    dve.wait_ge(out_done, b)
                dve.tensor_tensor(norm[:, :], osum[:, s, :], inv[:, :], ALU.mult).then_inc(norm_done, 1)
                dve.wait_ge(norm_done, b + 1)
                if later(b):
                    dve.wait_ge(multiplied, b - 1)
                dve.tensor_tensor(out[:, s, :], norm[:, :], vd[:, s, :], ALU.subtract).then_inc(out_done, 1)

            def body(b, s, turn):
                first = isinstance(b, int) and b == 0
                n = 0

                def did(ins):
                    nonlocal n
                    n += 1
                    ins.then_inc(step, 1)

                def settle():
                    dve.wait_ge(step, b * STEPS + (n + 1))

                settle()
                dve.wait_ge(kd_ready, b + 1)
                if later(b, 1):
                    dve.wait_ge(scored, b)
                dve.tensor_tensor(dot1[:, :], p_qs[:, :], kd[:, :], ALU.mult).then_inc(dots_done, 1)
                dve.tensor_tensor(dot0[:, :], p_qd[:, :], kd[:, :], ALU.mult).then_inc(dots_done, 1)
                dve.wait_ge(lines_in[s], turn * 16 + 16)
                did(dve.tensor_scalar(reset[:, :], same[:, s, :], 1.0, BIG, ALU.subtract, ALU.mult))
                did(dve.tensor_copy(top[:, s, 0:1], top[:, 1 - s, BLK:BLK + 1]))
                if not first:
                    invert(b - 1)
                dve.wait_ge(self_ready, b + 1)
                did(dve.scalar_tensor_tensor(best[:, :], p_s[:, :], HID ** -0.5, self_score[:, :], ALU.mult, ALU.max))
                settle()
                did(dve.tensor_tensor_scan(top[:, s, 1:BLK + 1], reset[:, :], best[:, :], top[:, s, 0:1], ALU.add, ALU.max))
                settle()
                if later(b, 1):
                    dve.wait_ge(ex_done, b)
                did(dve.tensor_tensor(reset[:, :], top[:, s, 0:BLK], top[:, s, 1:BLK + 1], ALU.subtract))
                settle()
                did(dve.tensor_tensor(gap[:, 2, :], reset[:, :], same[:, s, :], ALU.mult))
                did(dve.scalar_tensor_tensor(gap[:, 0, :], p_s[:, :], HID ** -0.5, top[:, s, 1:BLK + 1], ALU.mult, ALU.subtract))
                settle()
                dve.tensor_tensor(gap[:, 1, :], self_score[:, :], top[:, s, 1:BLK + 1], ALU.subtract).then_inc(gaps_done, 1)
                if not first:
                    finish(b - 1, 1 - s)
                dve.wait_ge(ex_done, b + 1)
                did(dve.scalar_tensor_tensor(neg_self[:, :], same[:, s, :], 1.0, ex[:, 1, :], ALU.subtract, ALU.mult))
                did(dve.tensor_tensor(keep_w[:, :], ex[:, 2, :], same[:, s, :], ALU.mult))
                dve.wait_ge(v_ready, b + 1)
                did(dve.tensor_tensor(pv[:, :], ex[:, 0, :], vs[:, s, :], ALU.mult))
                settle()
                did(dve.tensor_tensor(gv[:, :], neg_self[:, :], vd[:, s, :], ALU.mult))
                did(dve.tensor_tensor(weights[:, :], ex[:, 0, :], neg_self[:, :], ALU.subtract))
                settle()
                did(dve.tensor_tensor(vsum[:, :], pv[:, :], gv[:, :], ALU.subtract))
                did(dve.tensor_tensor_scan(ssum[:, s, :], keep_w[:, :], weights[:, :], 0.0 if first else ssum[:, 1 - s, BLK - 1:BLK],
                                           ALU.mult, ALU.add))
                settle()
                did(dve.tensor_tensor_scan(osum[:, s, :], keep_w[:, :], vsum[:, :], 0.0 if first else osum[:, 1 - s, BLK - 1:BLK],
                                           ALU.mult, ALU.add))
                dve.tensor_scalar(den[:, :], ssum[:, s, :], 1e-8, None, ALU.add).then_inc(den_done, 1)
                assert n == STEPS, n
            run_blocks(dve, EDGE_BLOCKS, body)
            last = EDGE_BLOCKS - 1
            invert(last)
            finish(last, last % 2)

        block.__exit__(None, None, None)


def node_pass(nc, k, title, a_table, u, b_table=None, store=None, dense=None, residual=None, target=None):
    norm = u != "relu"
    b_table = residual if residual is not None else b_table
    gated = dense is not None and dense[0] == "gated"
    with phase(nc, title) as (sb, ps, sem):
        a, bb, v, xn, ut, yo = (sb(n, [P, 4, BLK]) for n in ("a", "b", "v", "xn", "ut", "yo"))
        stats, mv = sb("stats", [P, 2, TB, 6]), sb("mv", [P, 2, TB, 2])
        shifted, rstd = sb("shifted", [P, 2, TB]), sb("rstd", [P, 2, TB])
        gate, prod, ot = (sb(n, [P, 2, BLK]) for n in ("gate", "prod", "ot"))
        p_t = ps("p_t", [P, 512])
        p_m = [ps(f"p_m{i}", [P, 2, 512]) for i in range(3 if gated else 1)]
        p_o = ps("p_o", [P, 512])
        a_in, b_in, u_stored, y_stored = ([sem(f"{n}{s}") for s in range(4)] for n in ("a_in", "b_in", "u_stored", "y_stored"))
        v_done, stats_done, aggr_done, shift_done, rstd_done, u_done = (sem(n) for n in ("v_done", "stats_done", "aggr_done", "shift_done", "rstd_done", "u_done"))
        turned, ut_ready, multiplied, gate_ready, prod_done, ot_done, turned_out, y_done = (
            sem(n) for n in ("turned", "ut_ready", "multiplied", "gate_ready", "prod_done", "ot_done", "turned_out", "y_done"))
        v = v if u == "norm_sum" else a
        a_used = {"norm": u_done, "norm_sum": v_done, "relu": turned}[u]
        last = NODE_BLOCKS - 1
        at = 2 if norm else 0
        full = (N - last * BLK) // TB
        block = nc.Block()
        block.__enter__()

        @block.sync
        def _(sp):
            def load_a(b, s, turn):
                if later(b, 4):
                    sp.wait_ge(a_used, b - 3)
                sp.dma_start(a[:, s, :].rearrange("p (j c) -> p j c", j=TB), block_rows(a_table, b)).then_inc(a_in[s], 16)

            def load_b(b, s, turn):
                if later(b, 4):
                    sp.wait_ge(y_done if residual is not None else v_done, b - 3)
                sp.dma_start(bb[:, s, :].rearrange("p (j c) -> p j c", j=TB), block_rows(b_table, b)).then_inc(b_in[s], 16)

            def store_block(b, s, table, rows, done):
                if table.shape[0] == N and isinstance(b, int) and b == last:
                    sp.dma_start(table[b * BLK:N, :].rearrange("(p j) c -> p j c", j=TB),
                                 rows[0:full, s, :].rearrange("p (j c) -> p j c", j=TB)).then_inc(done[s], 16)
                else:
                    sp.dma_start(block_rows(table, b), rows[:, s, :].rearrange("p (j c) -> p j c", j=TB)).then_inc(done[s], 16)

            def store_u(b, s, turn):
                sp.wait_ge(u_done, b + 1)
                store_block(b, s, store, xn, u_stored)

            def store_y(b, s, turn):
                sp.wait_ge(y_done, b + 1)
                store_block(b, s, target, yo, y_stored)

            stages = [(0, load_a)]
            if b_table is not None:
                stages.append((4 if residual is not None else 0, load_b))
            if store is not None:
                stages.append((5, store_u))
            if dense is not None:
                stages.append((at + 8, store_y))
            steps(sp, stages)
            for s in range(4):
                if store is not None:
                    sp.wait_ge(u_stored[s], 16 * len(range(s, NODE_BLOCKS, 4)))
                if dense is not None:
                    sp.wait_ge(y_stored[s], 16 * len(range(s, NODE_BLOCKS, 4)))

        if norm:
            @block.gpsimd
            def _(pool):
                def rstd_of(b, s, turn):
                    h = s % 2
                    pool.wait_ge(aggr_done, b * TB + TB)
                    if later(b):
                        pool.wait_ge(u_done, b - 1)
                    pool.tensor_tensor(shifted[:, h, :], mv[:, h, :, 1], k.eps[:, :], ALU.add).then_inc(shift_done, 1)
                    pool.wait_ge(shift_done, b + 1)
                    pool.tensor_tensor(rstd[:, h, :], shifted[:, h, :], k.neg_half[:, :], ALU.pow).then_inc(rstd_done, 1)

                steps(pool, [(0, rstd_of)])

        @block.vector
        def _(dve):
            def statistics(b, s, turn):
                h = s % 2
                dve.wait_ge(a_in[s], turn * 16 + 16)
                if u == "norm_sum":
                    dve.wait_ge(b_in[s], turn * 16 + 16)
                    if later(b, 4):
                        dve.wait_ge(u_done, b - 3)
                    dve.scalar_tensor_tensor(v[:, s, :], a[:, s, :], 0.0, bb[:, s, :], ALU.max, ALU.add).then_inc(v_done, 1)
                    dve.wait_ge(v_done, b + 1)
                if later(b):
                    dve.wait_ge(aggr_done, b * TB - TB)
                for j in range(TB):
                    dve.bn_stats(stats[:, h, j, :], v[:, s, j * D:(j + 1) * D]).then_inc(stats_done, 1)
                if later(b):
                    dve.wait_ge(u_done, b - 1)
                dve.wait_ge(stats_done, b * TB + TB)
                dve.nop(nofuse=True)
                for j in range(TB):
                    dve.bn_aggr(mv[:, h, j, :], stats[:, h, j, :]).then_inc(aggr_done, 1)

            def normalise(b, s, turn):
                h = s % 2
                dve.wait_ge(rstd_done, b + 1)
                if later(b, 4):
                    if store is not None:
                        dve.wait_ge(u_stored[s], turn * 16)
                    if dense is not None:
                        dve.wait_ge(turned, b - 3)
                for j in range(TB):
                    ins = dve.tensor_scalar(xn[:, s, j * D:(j + 1) * D], v[:, s, j * D:(j + 1) * D], mv[:, h, j, 0:1], rstd[:, h, j:j + 1],
                                            ALU.subtract, ALU.mult)
                ins.then_inc(u_done, 1)

            def combine(b, s, turn):
                h = s % 2
                dve.wait_ge(multiplied, b + 1)
                if later(b):
                    dve.wait_ge(turned_out, b - 1)
                if gated:
                    i = dense[1]
                    dve.wait_ge(gate_ready, b + 1)
                    if later(b):
                        dve.wait_ge(ot_done, b - 1)
                    dve.scalar_tensor_tensor(prod[:, h, :], p_m[2][:, h, :], k.col_of(f"fc{i}3_b"), gate[:, h, :], ALU.add, ALU.mult).then_inc(prod_done, 1)
                    dve.wait_ge(prod_done, b + 1)
                    dve.scalar_tensor_tensor(ot[:, h, :], p_m[0][:, h, :], k.bsum[:, i - 1:i], prod[:, h, :], ALU.add, ALU.add).then_inc(ot_done, 1)
                elif dense[3]:
                    dve.scalar_tensor_tensor(ot[:, h, :], p_m[0][:, h, :], dense[2], ut[:, s, :], ALU.add, ALU.add).then_inc(ot_done, 1)
                else:
                    dve.tensor_scalar(ot[:, h, :], p_m[0][:, h, :], dense[2], None, ALU.add).then_inc(ot_done, 1)

            def add_residual(b, s, turn):
                dve.wait_ge(turned_out, b + 1)
                dve.wait_ge(b_in[s], turn * 16 + 16)
                if later(b, 4):
                    dve.wait_ge(y_stored[s], turn * 16)
                dve.tensor_tensor(yo[:, s, :], p_o[:, :], bb[:, s, :], ALU.add).then_inc(y_done, 1)

            stages = [(0, statistics), (1, normalise)] if norm else []
            if dense is not None:
                stages.insert(1, (at + 2, combine))
            if residual is not None:
                stages.insert(0, (at + 4, add_residual))
            steps(dve, stages)

        if dense is not None:
            @block.tensor
            def _(pe):
                def turn_in(b, s, turn):
                    if norm:
                        pe.wait_ge(u_done, b + 1)
                    else:
                        pe.wait_ge(a_in[s], turn * 16 + 16)
                    if later(b, 1):
                        pe.wait_ge(ut_ready, b)
                    rows = xn if norm else a
                    for j in range(TB):
                        ins = pe.transpose(p_t[:, j * P:(j + 1) * P], rows[:, s, j * D:(j + 1) * D], k.ident[:, :])
                    ins.then_inc(turned, 1)

                def multiply(b, s, turn):
                    h = s % 2
                    pe.wait_ge(ut_ready, b + 1)
                    if later(b):
                        pe.wait_ge(ot_done, b - 1)
                    if gated:
                        for m in (1, 2, 0):
                            ins = pe.matmul(p_m[m][:, h, :], k.W[f"fc{dense[1]}{m + 1}"], ut[:, s, :], start=True, stop=True)
                    else:
                        ins = pe.matmul(p_m[0][:, h, :], dense[1], ut[:, s, :], start=True, stop=True)
                    ins.then_inc(multiplied, 1)

                def turn_out(b, s, turn):
                    h = s % 2
                    pe.wait_ge(ot_done, b + 1)
                    if later(b, 1):
                        pe.wait_ge(y_done, b)
                    for j in range(TB):
                        ins = pe.transpose(p_o[:, j * D:(j + 1) * D], ot[:, h, j * P:(j + 1) * P], k.ident[:, :])
                    ins.then_inc(turned_out, 1)

                steps(pe, [(at, turn_in), (at + 1, multiply), (at + 3, turn_out)])

            @block.scalar
            def _(act):
                def take_u(b, s, turn):
                    act.wait_ge(turned, b + 1)
                    if later(b, 4):
                        act.wait_ge(multiplied, b - 3)
                        act.wait_ge(ot_done, b - 3)
                    if norm:
                        act.copy(ut[:, s, :], p_t[:, :]).then_inc(ut_ready, 1)
                    else:
                        act.activation(ut[:, s, :], p_t[:, :], ACT.Relu).then_inc(ut_ready, 1)

                def keep_gate(b, s, turn):
                    h = s % 2
                    act.wait_ge(multiplied, b + 1)
                    if later(b):
                        act.wait_ge(prod_done, b - 1)
                    act.activation(gate[:, h, :], p_m[1][:, h, :], ACT.Identity, bias=k.col_of(f"fc{dense[1]}2_b")).then_inc(gate_ready, 1)

                def keep_y(b, s, turn):
                    act.wait_ge(turned_out, b + 1)
                    if later(b, 4):
                        act.wait_ge(y_stored[s], turn * 16)
                    act.copy(yo[:, s, :], p_o[:, :]).then_inc(y_done, 1)

                stages = [(at, take_u)]
                if gated:
                    stages.append((at + 1, keep_gate))
                if residual is None:
                    stages.append((at + 3, keep_y))
                steps(act, stages)

        block.__exit__(None, None, None)


def ffn_pass(nc, k, sum_table, x_table, store, weight, bias, target):
    with phase(nc, "ffn") as (sb, ps, sem):
        def two(name):
            return sb(name, [P, 2, BLK])

        a, xb = (sb(n, [P, 4, BLK]) for n in ("a", "xb"))
        xn, xt, yt, zn, zg, v, x3, ut, ot, yo = (two(n) for n in ("xn", "xt", "yt", "zn", "zg", "v", "x3", "ut", "ot", "yo"))
        hidden = sb("hidden", [P, 4, BLK])
        xplus = two("xplus")
        g2_block, b2_block = sb("g2_block", [P, BLK]), sb("b2_block", [P, BLK])
        stats = [sb(f"stats{i}", [P, 2, TB, 6]) for i in range(3)]
        mv = [sb(f"mv{i}", [P, 2, TB, 2]) for i in range(3)]
        shifted, rstd = [sb(f"shifted{i}", [P, 2, TB]) for i in range(3)], [sb(f"rstd{i}", [P, 2, TB]) for i in range(3)]
        p_t, p_h, p_f, p_z, p_u = ps("p_t", [P, 512]), ps("p_h", [P, 2, 512]), ps("p_f", [P, 512]), ps("p_z", [P, 2, 512]), ps("p_u", [P, 512])
        p_m = ps("p_m", [P, 512])
        a_in, x_in = ([sem(f"{n}{s}") for s in range(4)] for n in ("a_in", "x_in"))
        u_stored, y_stored = ([sem(f"{n}{s}") for s in range(2)] for n in ("u_stored", "y_stored"))
        stats_done, aggr_done, shift_done, rstd_done = ([sem(f"{n}{i}") for i in range(3)] for n in ("stats_done", "aggr_done", "shift_done", "rstd_done"))
        tiled, xn_done, turned, xt_ready, h_done, gelu_done, f_done, yt_done = (
            sem(n) for n in ("tiled", "xn_done", "turned", "xt_ready", "h_done", "gelu_done", "f_done", "yt_done"))
        z_turned, zn_done, zg_done, xplus_done, v_done, x3_done, u_turned, ut_ready = (
            sem(n) for n in ("z_turned", "zn_done", "zg_done", "xplus_done", "v_done", "x3_done", "u_turned", "ut_ready"))
        multiplied, ot_done, turned_out, y_done = (sem(n) for n in ("multiplied", "ot_done", "turned_out", "y_done"))
        last = NODE_BLOCKS - 1
        block = nc.Block()
        block.__enter__()

        @block.sync
        def _(sp):
            def load(b, s, turn):
                if later(b, 4):
                    sp.wait_ge(xn_done, b - 3)
                sp.dma_start(a[:, s, :].rearrange("p (j c) -> p j c", j=TB), block_rows(sum_table, b)).then_inc(a_in[s], 16)
                if later(b, 4):
                    sp.wait_ge(xplus_done, b - 3)
                sp.dma_start(xb[:, s, :].rearrange("p (j c) -> p j c", j=TB), block_rows(x_table, b)).then_inc(x_in[s], 16)

            def store_x3(b, s, turn):
                sp.wait_ge(x3_done, b + 1)
                sp.dma_start(block_rows(store, b), x3[:, s % 2, :].rearrange("p (j c) -> p j c", j=TB)).then_inc(u_stored[s % 2], 16)

            def store_y(b, s, turn):
                sp.wait_ge(y_done, b + 1)
                sp.dma_start(block_rows(target, b), yo[:, s % 2, :].rearrange("p (j c) -> p j c", j=TB)).then_inc(y_stored[s % 2], 16)

            steps(sp, [(0, load), (5, store_x3), (7, store_y)])
            for s in range(2):
                n = 16 * len(range(s, NODE_BLOCKS, 2))
                sp.wait_ge(u_stored[s], n)
                sp.wait_ge(y_stored[s], n)

        @block.gpsimd
        def _(pool):
            def rstd_of(i, used):
                def f(b, s, turn):
                    pool.wait_ge(aggr_done[i], b * TB + TB)
                    if later(b):
                        pool.wait_ge(used, b - 1)
                    pool.tensor_tensor(shifted[i][:, s % 2, :], mv[i][:, s % 2, :, 1], k.eps[:, :], ALU.add).then_inc(shift_done[i], 1)
                    pool.wait_ge(shift_done[i], b + 1)
                    pool.tensor_tensor(rstd[i][:, s % 2, :], shifted[i][:, s % 2, :], k.neg_half[:, :], ALU.pow).then_inc(rstd_done[i], 1)
                return f

            def x_plus_b2(b, s, turn):
                pool.wait_ge(x_in[s], turn * 16 + 16)
                if later(b):
                    pool.wait_ge(v_done, b - 1)
                pool.tensor_tensor(xplus[:, s % 2, :], xb[:, s, :], b2_block[:, :], ALU.add).then_inc(xplus_done, 1)

            pool.wait_ge(tiled, 2 * TB)
            steps(pool, [(1, x_plus_b2), (0, rstd_of(0, xn_done)), (2, rstd_of(1, zn_done)), (2, rstd_of(2, x3_done))])

        @block.vector
        def _(dve):
            for j in range(TB):
                dve.tensor_copy(g2_block[:, j * D:(j + 1) * D], k.g2[:, :]).then_inc(tiled, 1)
                dve.tensor_copy(b2_block[:, j * D:(j + 1) * D], k.b2[:, :]).then_inc(tiled, 1)
            dve.wait_ge(tiled, 2 * TB)

            def statistics(i, b, s, rows, used):
                if later(b):
                    dve.wait_ge(aggr_done[i], b * TB - TB)
                for j in range(TB):
                    dve.bn_stats(stats[i][:, s % 2, j, :], rows[:, j * D:(j + 1) * D]).then_inc(stats_done[i], 1)
                if later(b):
                    dve.wait_ge(used, b - 1)
                dve.wait_ge(stats_done[i], b * TB + TB)
                dve.nop(nofuse=True)
                for j in range(TB):
                    dve.bn_aggr(mv[i][:, s % 2, j, :], stats[i][:, s % 2, j, :]).then_inc(aggr_done[i], 1)

            def normalise(i, b, s, out_, rows, done):
                dve.wait_ge(rstd_done[i], b + 1)
                for j in range(TB):
                    ins = dve.tensor_scalar(out_[:, j * D:(j + 1) * D], rows[:, j * D:(j + 1) * D], mv[i][:, s % 2, j, 0:1], rstd[i][:, s % 2, j:j + 1],
                                            ALU.subtract, ALU.mult)
                ins.then_inc(done, 1)

            def stage_a1(b, s, turn):
                dve.wait_ge(a_in[s], turn * 16 + 16)
                statistics(0, b, s, a[:, s], xn_done)

            def stage_a2(b, s, turn):
                if later(b):
                    dve.wait_ge(turned, b - 1)
                normalise(0, b, s, xn[:, s % 2], a[:, s], xn_done)

            def stage_a3(b, s, turn):
                dve.wait_ge(f_done, b + 1)
                if later(b):
                    dve.wait_ge(z_turned, b - 1)
                dve.scalar_tensor_tensor(yt[:, s % 2, :], p_f[:, :], k.col_of("bf2"), xt[:, s % 2, :], ALU.add, ALU.add).then_inc(yt_done, 1)

            def stage_b1(b, s, turn):
                dve.wait_ge(z_turned, b + 1)
                statistics(1, b, s, p_z[:, s % 2], zn_done)

            def stage_b2(b, s, turn):
                if later(b):
                    dve.wait_ge(zg_done, b - 1)
                normalise(1, b, s, zn[:, s % 2], p_z[:, s % 2], zn_done)
                dve.wait_ge(zn_done, b + 1)
                if later(b):
                    dve.wait_ge(v_done, b - 1)
                dve.tensor_tensor(zg[:, s % 2, :], zn[:, s % 2, :], g2_block[:, :], ALU.mult).then_inc(zg_done, 1)
                dve.wait_ge(zg_done, b + 1)
                dve.wait_ge(xplus_done, b + 1)
                if later(b):
                    dve.wait_ge(x3_done, b - 1)
                dve.tensor_tensor(v[:, s % 2, :], zg[:, s % 2, :], xplus[:, s % 2, :], ALU.add).then_inc(v_done, 1)
                dve.wait_ge(v_done, b + 1)
                statistics(2, b, s, v[:, s % 2], x3_done)

            def stage_b3(b, s, turn):
                if later(b):
                    dve.wait_ge(u_stored[s % 2], turn * 32 + s // 2 * 16)
                    dve.wait_ge(u_turned, b - 1)
                normalise(2, b, s, x3[:, s % 2], v[:, s % 2], x3_done)

            steps(dve, [(2, stage_b1), (0, stage_a1), (2, stage_b2), (0, stage_a2), (2, stage_b3), (1, stage_a3)])

        @block.tensor
        def _(pe):
            def turn_in(b, s, turn):
                pe.wait_ge(xn_done, b + 1)
                if later(b, 1):
                    pe.wait_ge(xt_ready, b)
                for j in range(TB):
                    ins = pe.transpose(p_t[:, j * P:(j + 1) * P], xn[:, s % 2, j * D:(j + 1) * D], k.ident[:, :])
                ins.then_inc(turned, 1)

            def ffn(b, s, turn):
                pe.wait_ge(xt_ready, b + 1)
                for c in range(4):
                    if c >= 2 or later(b, 1):
                        pe.wait_ge(gelu_done, b * 4 + (c - 1))
                    pe.matmul(p_h[:, c % 2, :], k.W["Wf1"][:, c * D:(c + 1) * D], xt[:, s % 2, :], start=True, stop=True).then_inc(h_done, 1)
                    if c >= 1:
                        second(b, c - 1)
                second(b, 3).then_inc(f_done, 1)

            def second(b, c):
                pe.wait_ge(gelu_done, b * 4 + (c + 1))
                if c == 0 and later(b, 1):
                    pe.wait_ge(yt_done, b)
                return pe.matmul(p_f[:, :], k.W["Wf2"][:, c, :], hidden[:, c, :], start=c == 0, stop=c == 3)

            def turn_z(b, s, turn):
                pe.wait_ge(yt_done, b + 1)
                if later(b):
                    pe.wait_ge(zn_done, b - 1)
                for j in range(TB):
                    ins = pe.transpose(p_z[:, s % 2, j * D:(j + 1) * D], yt[:, s % 2, j * P:(j + 1) * P], k.ident[:, :])
                ins.then_inc(z_turned, 1)

            def turn_u(b, s, turn):
                pe.wait_ge(x3_done, b + 1)
                if later(b):
                    pe.wait_ge(y_done, b - 1)
                for j in range(TB):
                    ins = pe.transpose(p_u[:, j * P:(j + 1) * P], x3[:, s % 2, j * D:(j + 1) * D], k.ident[:, :])
                ins.then_inc(u_turned, 1)

            def last_product(b, s, turn):
                pe.wait_ge(ut_ready, b + 1)
                if later(b, 1):
                    pe.wait_ge(ot_done, b)
                pe.matmul(p_m[:, :], weight, ut[:, s % 2, :], start=True, stop=True).then_inc(multiplied, 1)

            def turn_y(b, s, turn):
                pe.wait_ge(ot_done, b + 1)
                if later(b, 1):
                    pe.wait_ge(y_done, b)
                for j in range(TB):
                    ins = pe.transpose(p_u[:, j * D:(j + 1) * D], ot[:, s % 2, j * P:(j + 1) * P], k.ident[:, :])
                ins.then_inc(turned_out, 1)

            steps(pe, [(1, ffn), (0, turn_in), (3, turn_u), (1, turn_z), (3, last_product), (4, turn_y)])

        @block.scalar
        def _(act):
            def take_x(b, s, turn):
                act.wait_ge(turned, b + 1)
                if later(b):
                    act.wait_ge(yt_done, b - 1)
                act.activation(xt[:, s % 2, :], p_t[:, :], ACT.Identity, scale=k.col_of("g1"), bias=k.col_of("b1")).then_inc(xt_ready, 1)

            def gelus(b, s, turn):
                for c in range(4):
                    act.wait_ge(h_done, b * 4 + (c + 1))
                    if later(b, 1):
                        act.wait_ge(f_done, b)
                    act.activation(hidden[:, c, :], p_h[:, c % 2, :], ACT.Gelu, bias=k.col_of(f"bf1_{c}")).then_inc(gelu_done, 1)

            def take_u(b, s, turn):
                act.wait_ge(u_turned, b + 1)
                if later(b):
                    act.wait_ge(multiplied, b - 1)
                act.copy(ut[:, s % 2, :], p_u[:, :]).then_inc(ut_ready, 1)

            def keep_y(b, s, turn):
                act.wait_ge(turned_out, b + 1)
                if later(b):
                    act.wait_ge(y_stored[s % 2], turn * 32 + s // 2 * 16)
                act.copy(yo[:, s % 2, :], p_u[:, :]).then_inc(y_done, 1)

            def add_bias(b, s, turn):
                act.wait_ge(multiplied, b + 1)
                if later(b):
                    act.wait_ge(turned_out, b - 1)
                act.activation(ot[:, s % 2, :], p_m[:, :], ACT.Identity, bias=bias).then_inc(ot_done, 1)

            steps(act, [(1, gelus), (0, take_x), (3, take_u), (3, add_bias), (4, keep_y)])

        block.__exit__(None, None, None)


VECTORS = ["fc11_b", "conv1_b", "fc12_b", "fc13_b", "fc21_b", "conv2_b", "fc22_b", "fc23_b", "bo", "bf2", "g1", "b1",
           "b0_3", "b1_3", "b2_3", "bf1_0", "bf1_1", "bf1_2", "bf1_3", "attL", "attR"]


def build(nc, a, out):
    k = Kit()
    w = {
        "fc11": a["L1_gnn_fc11_w"], "fc12": a["L1_gnn_fc12_w"], "fc13": a["L1_gnn_fc13_w"], "conv1": a["L1_gnn_conv1_w"],
        "fc21": a["L1_gnn_fc21_w"], "fc22": a["L1_gnn_fc22_w"], "fc23": a["L1_gnn_fc23_w"], "conv2": a["L1_gnn_conv2_w"],
        "Wq": a["L2_gnn_Wq"], "Wk": a["L2_gnn_Wk"], "Wv": a["L2_gnn_Wv"], "Wo": a["L2_gnn_Wo"], "Wf1": a["L2_gnn_Wf1"],
        "Wf2": a["L2_gnn_Wf2"], "W0": a["L0_gnn_W"],
        "Ws0": a["L3_gnn_Ws0"], "Wn0": a["L3_gnn_Wn0"], "Ws1": a["L3_gnn_Ws1"], "Wn1": a["L3_gnn_Wn1"],
        "Ws2": a["L3_gnn_Ws2"], "Wn2": a["L3_gnn_Wn2"], "g2": a["L2_gnn_g2"], "b2": a["L2_gnn_b2"],
        "fc11_b": a["L1_gnn_fc11_b"], "conv1_b": a["L1_gnn_conv1_b"], "fc12_b": a["L1_gnn_fc12_b"], "fc13_b": a["L1_gnn_fc13_b"],
        "fc21_b": a["L1_gnn_fc21_b"], "conv2_b": a["L1_gnn_conv2_b"], "fc22_b": a["L1_gnn_fc22_b"], "fc23_b": a["L1_gnn_fc23_b"],
        "bo": a["L2_gnn_bo"], "bf2": a["L2_gnn_bf2"], "g1": a["L2_gnn_g1"], "b1": a["L2_gnn_b1"],
        "b0_3": a["L3_gnn_b0"], "b1_3": a["L3_gnn_b1"], "b2_3": a["L3_gnn_b2"],
        "attL": a["L0_gnn_att"][:, :, 0:HID], "attR": a["L0_gnn_att"][:, :, HID:2 * HID],
    }
    for c in range(4):
        w[f"bf1_{c}"] = a["L2_gnn_bf1"][c * D:(c + 1) * D]
    k.vec_names = VECTORS

    def dram(name, shape, dt=F32):
        return nc.dram_tensor(name, shape, dt).ap()

    k.key_dram = [dram(f"keys{i}", (EPAD,), I32) for i in range(2)]
    k.oth_dram = [dram(f"others{i}", (EPAD,), I32) for i in range(2)]
    k.w_dram = dram("edge_weights", (EPAD,))
    k.sorted_dram = [dram(f"sorted{i}", (EPAD + 2, 4)) for i in range(2)]
    k.same_dram = [dram(f"same{i}", (EPAD,)) for i in range(2)]
    k.weight_dram = [dram(f"weight{i}", (EPAD,)) for i in range(2)]
    k.nv_dram = [dram(f"nv{i}", (EPAD,)) for i in range(2)]
    k.table = [dram(f"table{i}", (ROWS, D)) for i in range(2)]
    k.x1, k.x2, k.x3 = (dram(n, (NPAD, D)) for n in ("x1", "x2", "x3"))

    with ExitStack() as ctx:
        def sb(name, shape, dt=F32):
            return ctx.enter_context(nc.sbuf_tensor(name, shape, dt))

        k.W = {}
        squares = ["fc11", "fc12", "fc13", "conv1", "fc21", "fc22", "fc23", "conv2", "Wq", "Wk", "Wv", "Wo", "W0T", "Ws0T", "Wn0T",
                   "Ws1T", "Wn1T", "Ws2T", "Wn2T", "WvT", "attLW", "attRW", "Wvo"]
        all_w = sb("all_w", [P, len(squares), D])
        for i, name in enumerate(squares):
            k.W[name] = all_w[:, i, :]
        k.W["Wf1"] = sb("Wf1", [P, 4 * D])[:, :]
        k.W["Wf2"] = sb("Wf2", [P, 4, D])[:, :, :]
        k.vec = sb("vec", [P, len(VECTORS)])
        k.bsum = sb("bsum", [P, 2])
        k.g2, k.b2 = sb("g2", [P, D]), sb("b2", [P, D])
        k.ident, k.ident16 = sb("ident", [P, P]), sb("ident16", [P, P], F16)
        k.before, k.above, k.head = sb("before", [P, P]), sb("above", [P, P]), sb("head_mask", [P, P])
        k.row_iota, k.col_iota = sb("row_iota", [P, P], F16), sb("col_iota", [P, NCOL], F16)
        k.part_iota = sb("part_iota", [P, 1])
        k.neg_half, k.eps = sb("neg_half", [P, TB]), sb("eps", [P, TB])
        k.ones = sb("ones", [P, NCOL])
        k.at_key = [sb(f"at_key{i}", [P, TILES], I32) for i in range(2)]
        k.at_other = [sb(f"at_other{i}", [P, TILES], I32) for i in range(2)]
        k.at_end = [sb(f"at_end{i}", [P, TILES], I32) for i in range(2)]
        k.payload = [sb(f"payload{i}", [P, TILES, 4]) for i in range(2)]
        k.col_of = lambda name: k.vec[:, VECTORS.index(name):VECTORS.index(name) + 1]

        setup(nc, k, a["x"], a["src"], a["dst"], a["edge_weight1"], a["node_vec"], w)
        for which in range(2):
            sort_edges(nc, k, which)
            sorted_lists(nc, k, which)
        first, second = k.table
        col = k.col_of
        attend_layer0(nc, k, a["x"])
        node_pass(nc, k, "own1", first, "norm", store=k.x1, dense=("gated", 1), target=second)
        aggregate(nc, k, "conv1", k.x1, second, k.W["conv1"], relu=False, mean=False)
        node_pass(nc, k, "own2", second, "relu", dense=("gated", 2), target=first)
        aggregate(nc, k, "conv2", second, first, k.W["conv2"], relu=True, mean=False)
        node_pass(nc, k, "value", first, "norm_sum", b_table=k.x1, store=k.x2, dense=("linear", k.W["Wvo"], col("bo"), True), target=second)
        attend_layer2(nc, k, k.x2, second)
        ffn_pass(nc, k, second, k.x2, k.x3, k.W["Ws0T"], col("b0_3"), first)
        aggregate(nc, k, "sage0", k.x3, first, k.W["Wn0T"], relu=False, mean=True)
        node_pass(nc, k, "own4", first, "relu", dense=("linear", k.W["Ws1T"], col("b1_3"), True), target=second)
        aggregate(nc, k, "sage1", first, second, k.W["Wn1T"], relu=True, mean=True)
        node_pass(nc, k, "own5", second, "relu", dense=("linear", k.W["Ws2T"], col("b2_3"), False), residual=k.x3, target=first)
        aggregate(nc, k, "sage2", second, first, k.W["Wn2T"], relu=True, mean=True)
        node_pass(nc, k, "last", first, "norm", store=out)


_INS = ["x", "src", "dst", "edge_weight1", "node_vec", "L0_gnn_W", "L0_gnn_att"] \
    + [f"L1_gnn_{n}_{t}" for n in ("fc11", "fc12", "fc13", "conv1", "fc21", "fc22", "fc23", "conv2") for t in "wb"] \
    + [f"L2_gnn_{n}" for n in ("Wq", "Wk", "Wv", "Wo", "bo", "Wf1", "bf1", "Wf2", "bf2", "g1", "b1", "g2", "b2")] \
    + [f"L3_gnn_{n}{i}" for i in range(3) for n in ("Ws", "Wn", "b")]


def kernel(**inputs):
    import numpy as _np
    import concourse.bacc as _bacc
    from concourse import mybir as _mybir
    from concourse.bass_utils import run_bass_kernel_spmd as _run

    nc = _bacc.Bacc("TRN2", target_bir_lowering=False, num_devices=1)
    arrays, args = {}, {}
    for name in _INS:
        v = _np.ascontiguousarray(inputs[name])
        arrays[f"in_{name}"] = v
        args[name] = nc.dram_tensor(f"in_{name}", v.shape, _mybir.dt.from_np(v.dtype), kind="ExternalInput").ap()
    out = nc.dram_tensor("out_0", (N, D), _mybir.dt.float32, kind="ExternalOutput").ap()
    build(nc, args, out)
    r = _run(nc, [arrays], core_ids=[0])
    return r.results[0]["out_0"]
```

```python
from contextlib import ExitStack, contextmanager

import concourse.bass as bass
from concourse import mybir

ALU = mybir.AluOpType
ACT = mybir.ActivationFunctionType
F32 = mybir.dt.float32
F16 = mybir.dt.float16
I32 = mybir.dt.int32

P = 128
D = 128
N = 50000
E = 25000
TB = 4
BLK = TB * P
NODE_BLOCKS = -(-N // BLK)
NPAD = NODE_BLOCKS * BLK
TILES = -(-E // BLK) * TB
EDGE_BLOCKS = TILES // TB
EPAD = TILES * P
HALF = TILES // 2
ROWS = NPAD + EPAD
NCOL = -(-N // P)
PAD_KEY = NCOL * P - 1
HEADS, HID = 8, 16
EPS = 1e-5
BIG = 1e30
assert PAD_KEY >= N and PAD_KEY < NPAD and TILES % 2 == 0 and HALF <= P


class Kit:
    pass


@contextmanager
def phase(nc, title):
    with ExitStack() as ctx:
        sems = []

        def sb(name, shape, dt=F32):
            return ctx.enter_context(nc.sbuf_tensor(f"{title}_{name}", shape, dt))

        def ps(name, shape, dt=F32):
            return ctx.enter_context(nc.psum_tensor(f"{title}_{name}", shape, dt))

        def sem(name):
            sems.append(nc.alloc_semaphore(f"{title}_{name}"))
            return sems[-1]

        yield sb, ps, sem
        nc.clear_and_free_semaphores(sems)
        nc.all_engine_barrier()


def run_blocks(eng, blocks, body, unroll=2):
    first = 4
    for b in range(first):
        body(b, b % unroll, b // unroll)
    rounds = (blocks - first) // unroll
    with eng.Fori(0, rounds) as i:
        for s in range(unroll):
            body(i * unroll + (first + s), s, i + first // unroll)
    for b in range(first + rounds * unroll, blocks):
        body(b, b % unroll, b // unroll)


def back(lag, b, s, turn, unroll=4):
    turns_back = (lag - s + unroll - 1) // unroll
    return b - lag, (s - lag) % unroll, turn - turns_back if turns_back > 0 else turn


def later(b, lag=2):
    return not isinstance(b, int) or b >= lag


def block_rows(table, b):
    return table[bass.ds(b * BLK, BLK), :].rearrange("(p j) c -> p j c", j=TB)


def as_row(v):
    return v.rearrange("(a c) -> a c", a=1)


def setup(nc, k, src, dst, edge_w, w):
    R = len(k.vec_names)
    with phase(nc, "setup") as (sb, ps, sem):
        rc = sb("rc", [P, 2, P], I32)
        heads_of = sb("heads_of", [P, 2, P], I32)
        head = sb("head", [P, P])
        vec_rows = sb("vec_rows", [P, D])
        raw = sb("raw", [P, 9, D])
        attx = sb("attx", [P, 2, D])
        zeros = sb("zeros", [1, P])
        pads = sb("pads", [1, 2, P], I32)
        guard = sb("guard", [1, 2, 4])
        by_tile = sb("by_tile", [HALF, 4, 2, P], I32)
        by_tile_f = sb("by_tile_f", [HALF, 5, 2, P])
        pt = ps("pt", [P, 2, 512])
        pw = ps("pw", [P, 512])
        pads_set, iota_done, shifted, masks = sem("pads_set"), sem("iota_done"), sem("shifted"), sem("masks")
        weights_in, padded, lists_in, converted = sem("weights_in"), sem("padded"), sem("lists_in"), sem("converted")
        tables_in, pe_turn, copied = sem("tables_in"), sem("pe_turn"), sem("copied")
        attx_done, sums = sem("attx_done"), sem("sums")
        block = nc.Block()
        block.__enter__()

        lists = [(src, k.key_dram[0]), (dst, k.key_dram[1]), (src, k.oth_dram[0]), (dst, k.oth_dram[1])]
        direct = ["fc11", "fc12", "fc13", "conv1", "fc21", "fc22", "fc23", "conv2", "Wq", "Wk", "Wv", "Wo"]
        turned = ["W0", "Ws0", "Wn0", "Ws1", "Wn1", "Ws2", "Wn2", "Wv"]
        n_in = [0]

        @block.sync
        def _(sp):
            sp.wait_ge(pads_set, 5)
            n = 0
            for a, out in lists:
                sp.dma_start(out[0:E].rearrange("(p c) -> p c", p=8), a.rearrange("(p c) -> p c", p=8)).then_inc(padded, 16)
                sp.dma_start(as_row(out[E:EPAD]), pads[0:1, 0 if n < 2 else 1, 0:EPAD - E]).then_inc(padded, 16)
                n += 1
            sp.dma_start(k.w_dram[0:E].rearrange("(p c) -> p c", p=8), edge_w.rearrange("(p c) o -> p (c o)", p=8)).then_inc(padded, 16)
            sp.dma_start(as_row(k.w_dram[E:EPAD]), zeros[0:1, 0:EPAD - E]).then_inc(padded, 16)
            for s in range(2):
                sp.dma_start(k.sorted_dram[s][0:1, :], guard[0:1, 0, :]).then_inc(tables_in, 16)
                sp.dma_start(k.sorted_dram[s][EPAD + 1:EPAD + 2, :], guard[0:1, 1, :]).then_inc(tables_in, 16)
            sp.wait_ge(padded, 16 * 10)
            for i, a in enumerate([k.key_dram[0], k.key_dram[1], k.oth_dram[0], k.oth_dram[1]]):
                sp.dma_start(by_tile[:, i, :, :], a.rearrange("(h t p) -> t h p", h=2, p=P)).then_inc(lists_in, 16)
            sp.dma_start(by_tile_f[:, 4, :, :], k.w_dram.rearrange("(h t p) -> t h p", h=2, p=P)).then_inc(lists_in, 16)
            sp.wait_ge(tables_in, 16 * 4)

        @block.scalar
        def _(act):
            for name in direct:
                act.dma_start(k.W[name], w[name]).then_inc(weights_in, 16)
            for i, name in enumerate(turned):
                act.dma_start(raw[:, i, :], w[name]).then_inc(weights_in, 16)
            act.dma_start(k.W["Wf1"], w["Wf1"]).then_inc(weights_in, 16)
            act.dma_start(k.W["Wf2"], w["Wf2"].rearrange("(c p) n -> p c n", p=P)).then_inc(weights_in, 16)
            for r, name in enumerate(k.vec_names):
                v = w[name]
                if name in ("attL", "attR"):
                    act.dma_start(vec_rows[r:r + 1, :].rearrange("a (h d) -> a h d", h=HEADS), v).then_inc(weights_in, 16)
                else:
                    act.dma_start(vec_rows[r:r + 1, :], as_row(v)).then_inc(weights_in, 16)
            for out, v in ((k.g2, w["g2"]), (k.b2, w["b2"])):
                act.dma_start(out[:, :], as_row(v).to_broadcast([P, D])).then_inc(weights_in, 16)
            n_in[0] = len(direct) + len(turned) + 2 + R + 2
            act.wait_ge(weights_in, 16 * n_in[0])

        @block.gpsimd
        def _(pool):
            pool.memset(pads[:, 0, :], PAD_KEY).then_inc(pads_set, 1)
            pool.memset(pads[:, 1, :], 0).then_inc(pads_set, 1)
            pool.memset(guard[:, 0, :], -1.0).then_inc(pads_set, 1)
            pool.memset(guard[:, 1, :], -2.0).then_inc(pads_set, 1)
            pool.iota(rc[:, 0, :], [[0, P]], base=0, channel_multiplier=1).then_inc(iota_done, 1)
            pool.iota(rc[:, 1, :], [[1, P]], base=0, channel_multiplier=0).then_inc(iota_done, 1)
            pool.iota(k.col_iota[:, :], [[1, NCOL]], base=0, channel_multiplier=0, allow_small_or_imprecise_dtypes=True).then_inc(iota_done, 1)
            pool.memset(k.neg_half[:, :], -0.5).then_inc(iota_done, 1)
            pool.memset(k.eps[:, :], EPS).then_inc(iota_done, 1)
            pool.memset(k.ones[:, :], 1.0).then_inc(iota_done, 1)

        @block.tensor
        def _(pe):
            n = 0

            def turn(in_, width):
                nonlocal n
                if n >= 2:
                    pe.wait_ge(copied, n - 1)
                pe.transpose(pt[0:in_.shape[1], n % 2, 0:width], in_, k.ident[0:width, 0:width]).then_inc(pe_turn, 1)
                n += 1

            pe.wait_ge(masks, 5)
            pe.wait_ge(converted, 1)
            pe.wait_ge(lists_in, 16 * 5)
            for i in range(5):
                for h in range(2):
                    turn(by_tile_f[:, i, h, :], HALF)
            pe.wait_ge(weights_in, 16 * n_in[0])
            for i in range(len(turned)):
                turn(raw[:, i, :], P)
            turn(vec_rows[0:R, :], R)
            pe.wait_ge(attx_done, 2)
            for s in range(2):
                pe.matmul(pw[:, s * D:(s + 1) * D], raw[:, 0, :], attx[:, s, :], start=True, stop=True)
            pe.matmul(pw[:, 2 * D:3 * D], k.W["WvT"], k.W["Wo"], start=True, stop=True).then_inc(pe_turn, 1)

        @block.vector
        def _(dve):
            dve.memset(zeros[:, :], 0.0).then_inc(pads_set, 1)
            dve.wait_ge(iota_done, 6)
            dve.tensor_scalar(heads_of[:, :, :], rc[:, :, :], 4, None, ALU.logical_shift_right).then_inc(shifted, 1)
            dve.tensor_tensor(k.ident[:, :], rc[:, 0, :], rc[:, 1, :], ALU.is_equal).then_inc(masks, 1)
            dve.tensor_tensor(k.before[:, :], rc[:, 1, :], rc[:, 0, :], ALU.is_lt).then_inc(masks, 1)
            dve.tensor_tensor(k.above[:, :], rc[:, 0, :], rc[:, 1, :], ALU.is_lt).then_inc(masks, 1)
            dve.tensor_copy(k.row_iota[:, :], rc[:, 1, :]).then_inc(masks, 1)
            dve.wait_ge(shifted, 1)
            dve.tensor_tensor(head[:, :], heads_of[:, 0, :], heads_of[:, 1, :], ALU.is_equal).then_inc(masks, 1)
            dve.wait_ge(masks, 5)
            dve.tensor_copy(k.ident16[:, :], k.ident[:, :]).then_inc(masks, 1)
            dve.tensor_copy(k.head[:, :], head[:, :]).then_inc(masks, 1)
            dve.wait_ge(lists_in, 16 * 5)
            dve.tensor_copy(by_tile_f[:, 0:4, :, :].rearrange("t i h p -> t (i h p)"),
                            by_tile[:, :, :, :].rearrange("t i h p -> t (i h p)")).then_inc(converted, 1)
            n = 0

            def take(out, width=P, rows=P):
                nonlocal n
                dve.wait_ge(pe_turn, n + 1)
                dve.tensor_copy(out, pt[0:rows, n % 2, 0:width]).then_inc(copied, 1)
                n += 1

            slot = [(k.payload[0], 0), (k.payload[1], 0), (k.payload[1], 1), (k.payload[0], 1)]
            for i in range(5):
                for h in range(2):
                    half = slice(h * HALF, (h + 1) * HALF)
                    if i < 4:
                        take(slot[i][0][:, half, slot[i][1]], HALF)
                    else:
                        take(k.payload[0][:, half, 2], HALF)
            for name in turned:
                take(k.W[name + "T"])
            take(k.vec[:, 0:R], R)
            dve.wait_ge(copied, n)
            al, ar = k.vec_names.index("attL"), k.vec_names.index("attR")
            dve.tensor_scalar(attx[:, 0, :], head[:, :], k.vec[:, al:al + 1], None, ALU.mult).then_inc(attx_done, 1)
            dve.tensor_scalar(attx[:, 1, :], head[:, :], k.vec[:, ar:ar + 1], None, ALU.mult).then_inc(attx_done, 1)
            for i, (a, b) in enumerate((("fc11_b", "conv1_b"), ("fc21_b", "conv2_b"))):
                a, b = k.vec_names.index(a), k.vec_names.index(b)
                dve.tensor_tensor(k.bsum[:, i:i + 1], k.vec[:, a:a + 1], k.vec[:, b:b + 1], ALU.add).then_inc(sums, 1)
            dve.tensor_copy(k.payload[1][:, :, 2], k.payload[0][:, :, 2]).then_inc(sums, 1)
            dve.wait_ge(pe_turn, n + 1)
            for i, name in enumerate(("attLW", "attRW", "Wvo")):
                dve.tensor_copy(k.W[name], pw[:, i * D:(i + 1) * D]).then_inc(sums, 1)
        block.__exit__(None, None, None)


def sort_edges(nc, k, x, node_vec):
    BOTH = range(2)
    with phase(nc, "sort") as (sb, ps, sem):
        def pair(name, shape, dt=F32):
            return [sb(f"{name}{w}", shape, dt) for w in BOTH]

        key_i, bits = pair("key_i", [P, TILES], I32), pair("bits", [P, 2, TILES], I32)
        kpart, kcol = pair("kpart", [P, TILES]), pair("kcol", [P, TILES])
        oh_part, oh_col = pair("oh_part", [P, 2, TB, P], F16), pair("oh_col", [P, 2, TB, NCOL], F16)
        oh_turned = pair("oh_turned", [P, 2, P])
        counts, col_sum, start = pair("counts", [P, NCOL]), pair("col_sum", [P, NCOL + 1]), pair("start", [P, NCOL])
        base = pair("base", [P, 2, NCOL])
        key_row = pair("key_row", [P, 2, BLK], I32)
        junk, junk2 = sb("junk", [P, 2, TB, NCOL]), sb("junk2", [P, 2, TB, P])
        found, rank, place = pair("found", [P, 2, TB]), pair("rank", [P, 2, TB]), pair("place", [P, 2, TB], I32)
        cargo, key_now = pair("cargo", [P, 2, TB, 4]), pair("key_now", [P, 2, TB])
        PART = NPAD // EDGE_BLOCKS
        zeros = sb("zeros", [P, max(TB, (NPAD - N) // 16) * D])
        dst_i, dst_stage, nv = sb("dst_i", [P, TILES], I32), sb("dst_stage", [P, 2, TB], I32), sb("nv", [P, 2, TB])
        total = [ps(f"total{w}", [P, 512]) for w in BOTH]
        look = [ps(f"look{w}", [P, 2, 512]) for w in BOTH]
        turned = [ps(f"turned{w}", [P, 1024], F16) for w in BOTH]

        def two(name):
            return [sem(f"{name}{w}") for w in BOTH]

        key_split, onehots, counted, step = two("key_split"), two("onehots"), two("counted"), two("step")
        onehots2, turned_ok, turned_kept = two("onehots2"), two("turned_ok"), two("turned_kept")
        added, base_ready, looked, found_ok = two("added"), two("base_ready"), two("looked"), two("found_ok")
        rows_in = [[sem(f"rows_in{w}{s}") for s in range(2)] for w in BOTH]
        keys_staged, ranked, cargo_ready = two("keys_staged"), two("ranked"), two("cargo_ready")
        sent = [[sem(f"sent{w}{s}") for s in range(2)] for w in BOTH]
        zeros_set, tables_in = sem("zeros_set"), sem("tables_in")
        dst_ready, staged, nv_in, nv_kept = sem("dst_ready"), sem("staged"), two("nv_in"), sem("nv_kept")
        block = nc.Block()
        block.__enter__()

        @block.sync
        def _(sp):
            def load_rows(b, s, turn):
                for w in BOTH:
                    if later(b):
                        sp.wait_ge(ranked[w], b * TB - TB)
                    sp.dma_start(key_row[w][:, s, :],
                                 as_row(k.key_dram[w][bass.ds(b * BLK, BLK)]).to_broadcast([P, BLK])).then_inc(rows_in[w][s], 16)
                if isinstance(b, int) and b == EDGE_BLOCKS - 1:
                    sp.dma_start(k.table[0][b * PART:N, :].rearrange("(p r) c -> p (r c)", p=16),
                                 x[b * PART:N, :].rearrange("(p r) c -> p (r c)", p=16)).then_inc(tables_in, 16)
                    sp.dma_start(k.table[0][N:NPAD, :].rearrange("(p r) c -> p (r c)", p=16),
                                 zeros[0:16, 0:(NPAD - N) // 16 * D]).then_inc(tables_in, 16)
                else:
                    sp.dma_start(k.table[0][bass.ds(b * PART, PART), :].rearrange("(p r) c -> p (r c)", p=16),
                                 x[bass.ds(b * PART, PART), :].rearrange("(p r) c -> p (r c)", p=16)).then_inc(tables_in, 16)
                for table in k.table:
                    sp.dma_start(table[bass.ds(b * BLK + NPAD, BLK), :].rearrange("(p r) c -> p (r c)", p=P),
                                 zeros[:, 0:TB * D]).then_inc(tables_in, 16)

            sp.wait_ge(zeros_set, 1)
            run_blocks(sp, EDGE_BLOCKS, load_rows)
            sp.wait_ge(tables_in, 16 * (3 * EDGE_BLOCKS + 1))

        def make_onehots(dve, w, b, s, done):
            for j in range(TB):
                at = bass.ds(b * TB + j, 1)
                dve.tensor_scalar(oh_part[w][:, s, j, :], k.row_iota[:, :], kpart[w][:, at], None, ALU.is_equal).then_inc(done, 1)
                dve.tensor_scalar(oh_col[w][:, s, j, :], k.col_iota[:, :], kcol[w][:, at], None, ALU.is_equal).then_inc(done, 1)

        @block.vector
        def _(dve):
            dve.tensor_copy(dst_i[:, :], k.payload[0][:, :, 1]).then_inc(dst_ready, 1)
            dve.memset(zeros[:, :], 0.0).then_inc(zeros_set, 1)
            for w in BOTH:
                dve.tensor_copy(key_i[w][:, :], k.payload[w][:, :, 0]).then_inc(key_split[w], 1)
                dve.wait_ge(key_split[w], 1)
                dve.tensor_scalar(bits[w][:, 0, :], key_i[w][:, :], P - 1, None, ALU.bitwise_and).then_inc(key_split[w], 1)
                dve.tensor_scalar(bits[w][:, 1, :], key_i[w][:, :], 7, None, ALU.logical_shift_right).then_inc(key_split[w], 1)
                dve.wait_ge(key_split[w], 3)
                dve.tensor_copy(kpart[w][:, :], bits[w][:, 0, :]).then_inc(key_split[w], 1)
                dve.tensor_copy(kcol[w][:, :], bits[w][:, 1, :]).then_inc(key_split[w], 1)
                dve.wait_ge(key_split[w], 5)

            def count(b, s, turn):
                for w in BOTH:
                    if later(b):
                        dve.wait_ge(counted[w], b * TB - TB)
                    make_onehots(dve, w, b, s, onehots[w])

            run_blocks(dve, EDGE_BLOCKS, count)
            for w in BOTH:
                dve.wait_ge(counted[w], TILES)
                dve.tensor_copy(counts[w][:, :], total[w][:, 0:NCOL]).then_inc(step[w], 1)
                dve.memset(col_sum[w][:, 0:1], 0.0).then_inc(step[w], 1)
            for w in BOTH:
                dve.wait_ge(counted[w], TILES + 1)
                dve.wait_ge(step[w], 2)
                dve.tensor_tensor_scan(col_sum[w][:, 1:NCOL + 1], k.ones[:, 0:NCOL], look[w][:, 0, 0:NCOL], 0.0,
                                       ALU.mult, ALU.add).then_inc(step[w], 1)
                dve.wait_ge(step[w], 3)
                dve.tensor_tensor(start[w][:, :], look[w][:, 1, 0:NCOL], col_sum[w][:, 0:NCOL], ALU.add).then_inc(step[w], 1)
            dve.wait_ge(nv_kept, 2 * EDGE_BLOCKS)

            def prepare(w, b, s, turn):
                if later(b):
                    dve.wait_ge(looked[w], b * TB - TB)
                    dve.wait_ge(found_ok[w], b * TB - TB)
                make_onehots(dve, w, b, s, onehots2[w])
                dve.tensor_copy(key_now[w][:, s, :], k.payload[w][:, bass.ds(b * TB, TB), 0]).then_inc(keys_staged[w], 1)

            def rank_block(w, b, s, turn):
                dve.wait_ge(keys_staged[w], b + 1)
                dve.wait_ge(rows_in[w][s], turn * 16 + 16)
                if later(b, 1):
                    dve.wait_ge(ranked[w], b * TB)
                for j in range(TB):
                    dve.scalar_tensor_tensor(junk2[:, w, j, :], key_row[w][:, s, j * P:(j + 1) * P], key_now[w][:, s, j:j + 1], k.before[:, :],
                                             ALU.is_equal, ALU.mult, accum_out=rank[w][:, s, j:j + 1]).then_inc(ranked[w], 1)

            def place_block(b, s, turn):
                for w in BOTH:
                    prepare(w, b, s, turn)
                for w in BOTH:
                    rank_block(w, b, s, turn)
                    if later(b, 1):
                        dve.wait_ge(found_ok[w], b * TB)
                for j in range(TB):
                    for w in BOTH:
                        dve.wait_ge(looked[w], b * TB + (j + 1))
                        dve.scalar_tensor_tensor(junk[:, w, j, :], look[w][:, j % 2, 0:NCOL], 1.0, oh_col[w][:, s, j, :],
                                                 ALU.mult, ALU.mult, accum_out=found[w][:, s, j:j + 1]).then_inc(found_ok[w], 1)
                for w in BOTH:
                    if later(b):
                        dve.wait_ge(sent[w][s], turn * (16 * TB))
                    dve.wait_ge(found_ok[w], b * TB + TB)
                    dve.wait_ge(ranked[w], b * TB + TB)
                    dve.scalar_tensor_tensor(place[w][:, s, :], found[w][:, s, :], 1.0, rank[w][:, s, :], ALU.add, ALU.add).then_inc(cargo_ready[w], 1)
                    dve.tensor_copy(cargo[w][:, s, :, :], k.payload[w][:, bass.ds(b * TB, TB), :]).then_inc(cargo_ready[w], 1)

            run_blocks(dve, EDGE_BLOCKS, place_block)

        @block.tensor
        def _(pe):
            def count(b, s, turn):
                for w in BOTH:
                    for j in range(TB):
                        pe.wait_ge(onehots[w], b * (2 * TB) + 2 * (j + 1))
                        pe.matmul(total[w][:, 0:NCOL], oh_part[w][:, s, j, :], oh_col[w][:, s, j, :],
                                  start=isinstance(b, int) and b == 0 and j == 0, stop=False, skip_group_check=True).then_inc(counted[w], 1)

            run_blocks(pe, EDGE_BLOCKS, count)
            for w in BOTH:
                pe.wait_ge(step[w], 1)
                pe.matmul(look[w][:, 0, 0:NCOL], k.ones[:, 0:P], counts[w][:, :], start=True, stop=True)
                pe.matmul(look[w][:, 1, 0:NCOL], k.above[:, :], counts[w][:, :], start=True, stop=True).then_inc(counted[w], 1)
            for w in BOTH:
                pe.wait_ge(step[w], 4)
                pe.matmul(total[w][:, 0:NCOL], k.ident[:, :], start[w][:, :], start=True, stop=False, skip_group_check=True).then_inc(added[w], 1)

            def place_block(b, s, turn):
                for j in range(TB):
                    for w in BOTH:
                        pe.wait_ge(onehots2[w], b * (2 * TB) + 2 * (j + 1))
                        if j >= 1 or later(b, 1):
                            pe.wait_ge(turned_kept[w], b * TB + j)
                        pe.transpose(turned[w][:, 0:P], oh_part[w][:, s, j, :], k.ident16[:, :]).then_inc(turned_ok[w], 1)
                    for w in BOTH:
                        pe.wait_ge(base_ready[w], b * TB + (j + 1))
                        pe.matmul(total[w][:, 0:NCOL], oh_part[w][:, s, j, :], oh_col[w][:, s, j, :], start=False, stop=False,
                                  skip_group_check=True).then_inc(added[w], 1)
                    for w in BOTH:
                        pe.wait_ge(turned_kept[w], b * TB + (j + 1))
                        if j >= 2 or later(b, 1):
                            pe.wait_ge(found_ok[w], b * TB + (j - 1))
                        pe.matmul(look[w][:, j % 2, 0:NCOL], oh_turned[w][:, j % 2, :], base[w][:, j % 2, :], start=True, stop=True).then_inc(looked[w], 1)

            run_blocks(pe, EDGE_BLOCKS, place_block)

        @block.scalar
        def _(act):
            def keep(b, s, turn):
                for j in range(TB):
                    for w in BOTH:
                        act.wait_ge(added[w], b * TB + (j + 1))
                        if j >= 2 or later(b, 1):
                            act.wait_ge(looked[w], b * TB + (j - 1))
                        act.copy(base[w][:, j % 2, :], total[w][:, 0:NCOL]).then_inc(base_ready[w], 1)
                    for w in BOTH:
                        act.wait_ge(turned_ok[w], b * TB + (j + 1))
                        act.copy(oh_turned[w][:, j % 2, :], turned[w][:, 0:P]).then_inc(turned_kept[w], 1)

            run_blocks(act, EDGE_BLOCKS, keep)

        @block.gpsimd
        def _(pool):
            def keep_nv(b, s):
                for w in BOTH:
                    pool.tensor_copy(k.payload[w][:, bass.ds(b * TB, TB), 3], nv[:, s, :]).then_inc(nv_kept, 1)

            def gather_nv(b, s, turn):
                if later(b):
                    pool.wait_ge(nv_in[s], turn * (16 * TB))
                    keep_nv(b - 2, s)
                    pool.wait_ge(nv_kept, b * 2 - 2)
                pool.tensor_copy(dst_stage[:, s, :], dst_i[:, bass.ds(b * TB, TB)]).then_inc(staged, 1)
                pool.wait_ge(staged, b + 1)
                pool.nop(nofuse=True)
                for j in range(TB):
                    pool.indirect_dma_start(out=nv[:, s, j:j + 1], out_offset=None, in_=node_vec.rearrange("(n a) -> n a", a=1),
                                            in_offset=bass.IndirectOffsetOnAxis(ap=dst_stage[:, s, j:j + 1], axis=0)).then_inc(nv_in[s], 16)

            pool.wait_ge(dst_ready, 1)
            run_blocks(pool, EDGE_BLOCKS, gather_nv)
            for b in (EDGE_BLOCKS - 2, EDGE_BLOCKS - 1):
                pool.wait_ge(nv_in[b % 2], (b // 2 + 1) * 16 * TB)
                keep_nv(b, b % 2)

            def send(b, s, turn):
                for w in BOTH:
                    pool.wait_ge(cargo_ready[w], b * 2 + 2)
                    pool.nop(nofuse=True)
                    for j in range(TB):
                        pool.indirect_dma_start(out=k.sorted_dram[w][:, :], out_offset=bass.IndirectOffsetOnAxis(ap=place[w][:, s, j:j + 1], axis=0),
                                                in_=cargo[w][:, s, j, :], in_offset=None).then_inc(sent[w][s], 16)

            run_blocks(pool, EDGE_BLOCKS, send)
            for w in BOTH:
                for s in range(2):
                    pool.wait_ge(sent[w][s], 16 * TB * len(range(s, EDGE_BLOCKS, 2)))

        block.__exit__(None, None, None)


def sorted_lists(nc, k, which):
    table = k.sorted_dram[which]
    with phase(nc, f"lists{which}") as (sb, ps, sem):
        words = sb("words", [HALF, 3, 2, P, 4])
        same = sb("same", [HALF, 2, P])
        is_end = sb("is_end", [HALF, 2, P])
        spare = sb("spare", [HALF, 2, P])
        diff = sb("diff", [HALF, 2, P])
        idx = sb("idx", [HALF, 3, 2, P])
        pt = ps("pt", [P, 2, 512])
        loaded, spare_set, step, ready = sem("loaded"), sem("spare_set"), sem("step"), sem("ready")
        stored, pe_turn, copied = sem("stored"), sem("pe_turn"), sem("copied")
        block = nc.Block()
        block.__enter__()

        @block.sync
        def _(sp):
            for i in range(3):
                first = (1, 0, 2)[i]
                sp.dma_start(words[:, i, :, :, :].rearrange("t h p w -> t h (p w)"),
                             table[first:first + EPAD, :].rearrange("(h t p) w -> t h (p w)", h=2, p=P)).then_inc(loaded, 16)
            sp.wait_ge(ready, 3)
            for a, src in ((k.same_dram[which], same), (k.weight_dram[which], idx[:, 0]), (k.nv_dram[which], idx[:, 1])):
                sp.dma_start(a.rearrange("(h t p) -> t h p", h=2, p=P), src[:, :, :] if src is same else src).then_inc(stored, 16)
            sp.wait_ge(stored, 16 * 3)

        @block.gpsimd
        def _(pool):
            pool.iota(spare[:, :, :], [[HALF * P, 2], [1, P]], base=NPAD, channel_multiplier=P,
                      allow_small_or_imprecise_dtypes=True).then_inc(spare_set, 1)

        @block.vector
        def _(dve):
            dve.wait_ge(loaded, 16 * 3)
            key = words[:, 0, :, :, 0]
            dve.tensor_tensor(same[:, :, :], key, words[:, 1, :, :, 0], ALU.is_equal).then_inc(ready, 1)
            dve.tensor_copy(idx[:, 0], words[:, 0, :, :, 2]).then_inc(ready, 1)
            dve.tensor_copy(idx[:, 1], words[:, 0, :, :, 3]).then_inc(ready, 1)
            dve.tensor_tensor(is_end[:, :, :], key, words[:, 2, :, :, 0], ALU.not_equal).then_inc(step, 1)
            dve.wait_ge(spare_set, 1)
            dve.tensor_tensor(diff[:, :, :], key, spare[:, :, :], ALU.subtract).then_inc(step, 1)
            dve.wait_ge(step, 2)
            dve.tensor_tensor(diff[:, :, :], diff[:, :, :], is_end[:, :, :], ALU.mult).then_inc(step, 1)
            dve.wait_ge(step, 3)
            dve.wait_ge(stored, 16 * 3)
            dve.tensor_tensor(idx[:, 2], diff[:, :, :], spare[:, :, :], ALU.add).then_inc(step, 1)
            dve.tensor_copy(idx[:, 1], words[:, 0, :, :, 1]).then_inc(step, 1)
            dve.tensor_scalar(idx[:, 0], key, float(N - 1), None, ALU.min).then_inc(step, 1)
            n = 0
            for out in (k.at_key[which], k.at_other[which], k.at_end[which]):
                for h in range(2):
                    dve.wait_ge(pe_turn, n + 1)
                    dve.tensor_copy(out[:, h * HALF:(h + 1) * HALF], pt[:, n % 2, 0:HALF]).then_inc(copied, 1)
                    n += 1

        @block.tensor
        def _(pe):
            pe.wait_ge(step, 6)
            n = 0
            for i in range(3):
                for h in range(2):
                    if n >= 2:
                        pe.wait_ge(copied, n - 1)
                    pe.transpose(pt[:, n % 2, 0:HALF], idx[:, i, h, :], k.ident[0:HALF, 0:HALF]).then_inc(pe_turn, 1)
                    n += 1

        block.__exit__(None, None, None)


def gather_rows(pool, source, rows, index, done):
    for j in range(TB):
        pool.indirect_dma_start(out=rows[:, j * D:(j + 1) * D], out_offset=None, in_=source,
                                in_offset=bass.IndirectOffsetOnAxis(ap=index[:, j:j + 1], axis=0)).then_inc(done, 16)


def scatter_add_rows(pool, target, rows, index, done):
    for j in range(TB):
        pool.indirect_dma_start(out=target, out_offset=bass.IndirectOffsetOnAxis(ap=index[:, j:j + 1], axis=0),
                                in_=rows[:, j * D:(j + 1) * D], in_offset=None, bounds_check=ROWS - 1, oob_is_err=True,
                                compute_op=ALU.add).then_inc(done, 16)


def edge_pool_program(pool, gathers, end_index, target, y, stage, sems):
    index_ready, rows_used, rows_in, y_ready, sent = sems
    END = len(gathers)

    def gather(b, s, count):
        if later(b):
            pool.wait_ge(rows_used, b - 1)
        for i, (_, index, _) in enumerate(gathers):
            ins = pool.tensor_copy(stage[:, s, i, :], index[:, bass.ds(b * TB, TB)])
        ins.then_inc(index_ready, 1)
        pool.wait_ge(index_ready, count)
        pool.nop(nofuse=True)
        for i, (source, _, rows) in enumerate(gathers):
            gather_rows(pool, source, rows[:, s, :], stage[:, s, i, :], rows_in[s])

    def scatter(b, s, turn, count):
        if later(b):
            pool.wait_ge(sent[s], turn * (16 * TB))
        pool.tensor_copy(stage[:, s, END, :], end_index[:, bass.ds(b * TB, TB)]).then_inc(index_ready, 1)
        pool.wait_ge(y_ready, b + 1)
        pool.wait_ge(index_ready, count)
        pool.nop(nofuse=True)
        scatter_add_rows(pool, target, y[:, s, :], stage[:, s, END, :], sent[s])

    for b in range(3):
        gather(b, b % 2, b + 1)

    def both(b, s, turn):
        gather(b, s, b * 2 - 2)
        scatter(b - 3, 1 - s, turn - 2 + s, b * 2 - 1)

    both(3, 1, 1)
    pairs = (EDGE_BLOCKS - 4) // 2
    with pool.Fori(0, pairs) as i:
        for s in range(2):
            both(i * 2 + (4 + s), s, i + 2)
    for b in range(4 + 2 * pairs, EDGE_BLOCKS):
        both(b, b % 2, b // 2)
    for b in range(EDGE_BLOCKS - 3, EDGE_BLOCKS):
        scatter(b, b % 2, b // 2, EDGE_BLOCKS + b + 1)
    for s in range(2):
        pool.wait_ge(sent[s], 16 * TB * len(range(s, EDGE_BLOCKS, 2)))


def attend_layer0(nc, k, x):
    target = k.table[0]
    with phase(nc, "layer0") as (sb, ps, sem):
        xs_rows, xd_rows = sb("xs_rows", [P, 2, BLK]), sb("xd_rows", [P, 2, BLK])
        stage = sb("stage", [P, 2, 3, TB], I32)
        xs, xd = sb("xs", [P, 2, BLK]), sb("xd", [P, 2, BLK])
        same, nv = sb("same", [P, 2, BLK]), sb("nv", [P, 2, BLK])
        small, leaky, ex = sb("small", [P, BLK]), sb("leaky", [P, BLK]), sb("ex", [P, BLK])
        alpha, msg = sb("alpha", [P, BLK]), sb("msg", [P, BLK])
        asum, osum = sb("asum", [P, 2, BLK]), sb("osum", [P, 2, BLK])
        inv, out = sb("inv", [P, BLK]), sb("out", [P, 2, BLK])
        y = sb("y", [P, 2, BLK])
        p_s, p_d, p_z, p_h, p_o = ps("p_s", [P, 512]), ps("p_d", [P, 512]), ps("p_z", [P, 512]), ps("p_h", [P, 512]), ps("p_o", [P, 512])
        index_ready, rows_used, y_ready = sem("index_ready"), sem("rows_used"), sem("y_ready")
        rows_in, sent, lines_in = ([sem(f"{n}{s}") for s in range(2)] for n in ("rows_in", "sent", "lines_in"))
        x_ready, z_done, h_done, small_done, leaky_done = sem("x_ready"), sem("z_done"), sem("h_done"), sem("small_done"), sem("leaky_done")
        ex_done, alpha_done, msg_done, asum_done, osum_done = sem("ex_done"), sem("alpha_done"), sem("msg_done"), sem("asum_done"), sem("osum_done")
        inv_done, out_done, turned_out = sem("inv_done"), sem("out_done"), sem("turned_out")
        block = nc.Block()
        block.__enter__()

        @block.gpsimd
        def _(pool):
            edge_pool_program(pool, [(x, k.at_key[0], xs_rows), (x, k.at_other[0], xd_rows)], k.at_end[0], target, y, stage,
                              (index_ready, rows_used, rows_in, y_ready, sent))

        @block.sync
        def _(sp):
            def load(b, s, turn):
                if later(b):
                    sp.wait_ge(osum_done, b - 1)
                cols = bass.ds(b * BLK, BLK)
                sp.dma_start(same[:, s, :], as_row(k.same_dram[0][cols]).to_broadcast([P, BLK])).then_inc(lines_in[s], 16)
                sp.dma_start(nv[:, s, :], as_row(k.nv_dram[0][cols]).to_broadcast([P, BLK])).then_inc(lines_in[s], 16)

            run_blocks(sp, EDGE_BLOCKS, load)

        @block.tensor
        def _(pe):
            def products(b, s, turn):
                pe.wait_ge(rows_in[s], turn * (32 * TB) + 32 * TB)
                if later(b, 1):
                    pe.wait_ge(x_ready, b)
                for rows, out_ in ((xs_rows, p_s), (xd_rows, p_d)):
                    for j in range(TB):
                        ins = pe.transpose(out_[:, j * P:(j + 1) * P], rows[:, s, j * D:(j + 1) * D], k.ident[:, :])
                ins.then_inc(rows_used, 1)
                pe.wait_ge(x_ready, b + 1)
                if later(b, 1):
                    pe.wait_ge(leaky_done, b)
                pe.matmul(p_z[:, :], k.W["attLW"], xs[:, s, :], start=True, stop=False)
                pe.matmul(p_z[:, :], k.W["attRW"], xd[:, s, :], start=False, stop=True).then_inc(z_done, 1)
                if later(b, 1):
                    pe.wait_ge(msg_done, b)
                pe.matmul(p_h[:, :], k.W["W0T"], xd[:, s, :], start=True, stop=True).then_inc(h_done, 1)

            def turn_out(b, s):
                pe.wait_ge(out_done, b + 1)
                if later(b, 1):
                    pe.wait_ge(y_ready, b)
                for j in range(TB):
                    ins = pe.transpose(p_o[:, j * P:(j + 1) * P], out[:, s, j * P:(j + 1) * P], k.ident[:, :])
                ins.then_inc(turned_out, 1)

            def both(b, s, turn):
                products(b, s, turn)
                if later(b, 1):
                    turn_out(b - 1, 1 - s)

            run_blocks(pe, EDGE_BLOCKS, both)
            turn_out(EDGE_BLOCKS - 1, (EDGE_BLOCKS - 1) % 2)

        @block.scalar
        def _(act):
            def keep_y(b, s, turn):
                act.wait_ge(turned_out, b + 1)
                if later(b):
                    act.wait_ge(sent[s], turn * (16 * TB))
                act.copy(y[:, s, :], p_o[:, :]).then_inc(y_ready, 1)

            def body(b, s, turn):
                act.wait_ge(rows_used, b + 1)
                if later(b):
                    act.wait_ge(h_done, b - 1)
                act.copy(xs[:, s, :], p_s[:, :])
                act.copy(xd[:, s, :], p_d[:, :]).then_inc(x_ready, 1)
                act.wait_ge(leaky_done, b + 1)
                if later(b, 1):
                    act.wait_ge(alpha_done, b)
                act.activation(ex[:, :], leaky[:, :], ACT.Exp).then_inc(ex_done, 1)
                if later(b, 1):
                    keep_y(b - 1, 1 - s, turn if s else turn - 1)

            run_blocks(act, EDGE_BLOCKS, body)
            keep_y(EDGE_BLOCKS - 1, (EDGE_BLOCKS - 1) % 2, (EDGE_BLOCKS - 1) // 2)

        @block.vector
        def _(dve):
            def body(b, s, turn):
                more = later(b, 1)
                dve.wait_ge(z_done, b + 1)
                if more:
                    dve.wait_ge(leaky_done, b)
                dve.tensor_scalar(small[:, :], p_z[:, :], 0.2, None, ALU.mult).then_inc(small_done, 1)
                dve.wait_ge(small_done, b + 1)
                if more:
                    dve.wait_ge(ex_done, b)
                dve.tensor_tensor(leaky[:, :], p_z[:, :], small[:, :], ALU.max).then_inc(leaky_done, 1)
                dve.wait_ge(lines_in[s], turn * 32 + 32)
                dve.wait_ge(ex_done, b + 1)
                if more:
                    dve.wait_ge(osum_done, b)
                dve.tensor_tensor(alpha[:, :], ex[:, :], nv[:, s, :], ALU.mult).then_inc(alpha_done, 1)
                dve.wait_ge(alpha_done, b + 1)
                dve.wait_ge(h_done, b + 1)
                dve.tensor_tensor(msg[:, :], alpha[:, :], p_h[:, :], ALU.mult).then_inc(msg_done, 1)
                first = isinstance(b, int) and b == 0
                dve.tensor_tensor_scan(asum[:, s, :], same[:, s, :], alpha[:, :], 0.0 if first else asum[:, 1 - s, BLK - 1:BLK],
                                       ALU.mult, ALU.add).then_inc(asum_done, 1)
                dve.wait_ge(msg_done, b + 1)
                dve.tensor_tensor_scan(osum[:, s, :], same[:, s, :], msg[:, :], 0.0 if first else osum[:, 1 - s, BLK - 1:BLK],
                                       ALU.mult, ALU.add).then_inc(osum_done, 1)
                dve.wait_ge(asum_done, b + 1)
                if more:
                    dve.wait_ge(out_done, b)
                dve.reciprocal(inv[:, :], asum[:, s, :]).then_inc(inv_done, 1)
                dve.wait_ge(inv_done, b + 1)
                dve.wait_ge(osum_done, b + 1)
                if later(b):
                    dve.wait_ge(turned_out, b - 1)
                dve.scalar_tensor_tensor(out[:, s, :], inv[:, :], 1e-16, osum[:, s, :], ALU.add, ALU.mult).then_inc(out_done, 1)

            run_blocks(dve, EDGE_BLOCKS, body)

        block.__exit__(None, None, None)


def aggregate(nc, k, title, source, target, weight, relu, mean):
    with phase(nc, title) as (sb, ps, sem):
        rows = sb("rows", [P, 2, BLK])
        stage = sb("stage", [P, 2, 2, TB], I32)
        same, wrow = sb("same", [P, 2, BLK]), sb("wrow", [P, 2, BLK])
        ones = sb("ones_block", [P, BLK])
        msg, total = sb("msg", [P, 2, BLK]), sb("total", [P, 2, BLK])
        count, inv, avg = sb("count", [P, 2, BLK]), sb("inv", [P, BLK]), sb("avg", [P, 2, BLK])
        y = sb("y", [P, 2, BLK])
        p_x, p_y = ps("p_x", [P, 2, 512]), ps("p_y", [P, 2, 512])
        index_ready, rows_used, y_ready = sem("index_ready"), sem("rows_used"), sem("y_ready")
        rows_in, sent, lines_in = ([sem(f"{n}{s}") for s in range(2)] for n in ("rows_in", "sent", "lines_in"))
        msg_done, total_done, multiplied = sem("msg_done"), sem("total_done"), sem("multiplied")
        ones_set, count_done, inv_done, avg_done = sem("ones_set"), sem("count_done"), sem("inv_done"), sem("avg_done")
        sums, sums_done = (avg, avg_done) if mean else (total, total_done)
        lines = 1 if mean else 2
        block = nc.Block()
        block.__enter__()

        @block.gpsimd
        def _(pool):
            edge_pool_program(pool, [(source, k.at_other[1], rows)], k.at_end[1], target, y, stage,
                              (index_ready, rows_used, rows_in, y_ready, sent))

        @block.sync
        def _(sp):
            def load(b, s, turn):
                if later(b):
                    sp.wait_ge(sums_done, b - 1)
                cols = bass.ds(b * BLK, BLK)
                sp.dma_start(same[:, s, :], as_row(k.same_dram[1][cols]).to_broadcast([P, BLK])).then_inc(lines_in[s], 16)
                if not mean:
                    sp.dma_start(wrow[:, s, :], as_row(k.weight_dram[1][cols]).to_broadcast([P, BLK])).then_inc(lines_in[s], 16)

            run_blocks(sp, EDGE_BLOCKS, load)

        @block.tensor
        def _(pe):
            def turn_rows(b, s, turn):
                pe.wait_ge(rows_in[s], turn * (16 * TB) + 16 * TB)
                if later(b):
                    pe.wait_ge(msg_done, b - 1)
                for j in range(TB):
                    ins = pe.transpose(p_x[:, s, j * P:(j + 1) * P], rows[:, s, j * D:(j + 1) * D], k.ident[:, :])
                ins.then_inc(rows_used, 1)

            def multiply(b, s):
                pe.wait_ge(sums_done, b + 1)
                if later(b):
                    pe.wait_ge(y_ready, b - 1)
                for j in range(TB):
                    ins = pe.matmul(p_y[:, s, j * D:(j + 1) * D], sums[:, s, j * P:(j + 1) * P], weight, start=True, stop=True)
                ins.then_inc(multiplied, 1)

            def body(b, s, turn):
                turn_rows(b, s, turn)
                if later(b, 1):
                    multiply(b - 1, 1 - s)

            run_blocks(pe, EDGE_BLOCKS, body)
            multiply(EDGE_BLOCKS - 1, (EDGE_BLOCKS - 1) % 2)

        @block.scalar
        def _(act):
            def body(b, s, turn):
                act.wait_ge(multiplied, b + 1)
                if later(b):
                    act.wait_ge(sent[s], turn * (16 * TB))
                act.copy(y[:, s, :], p_y[:, s, :]).then_inc(y_ready, 1)

            run_blocks(act, EDGE_BLOCKS, body)

        @block.vector
        def _(dve):
            if mean:
                dve.memset(ones[:, :], 1.0).then_inc(ones_set, 1)
                dve.wait_ge(ones_set, 1)

            def body(b, s, turn):
                first = isinstance(b, int) and b == 0
                dve.wait_ge(rows_used, b + 1)
                dve.wait_ge(lines_in[s], turn * (16 * lines) + 16 * lines)
                if later(b):
                    dve.wait_ge(total_done, b - 1)
                if mean:
                    if relu:
                        dve.tensor_scalar(msg[:, s, :], p_x[:, s, :], 0.0, None, ALU.max).then_inc(msg_done, 1)
                    else:
                        dve.tensor_copy(msg[:, s, :], p_x[:, s, :]).then_inc(msg_done, 1)
                elif relu:
                    dve.scalar_tensor_tensor(msg[:, s, :], p_x[:, s, :], 0.0, wrow[:, s, :], ALU.max, ALU.mult).then_inc(msg_done, 1)
                else:
                    dve.tensor_tensor(msg[:, s, :], p_x[:, s, :], wrow[:, s, :], ALU.mult).then_inc(msg_done, 1)
                if mean:
                    if later(b, 1):
                        dve.wait_ge(inv_done, b)
                        dve.wait_ge(count_done, b)
                    dve.tensor_tensor_scan(count[:, s, :], same[:, s, :], ones[:, :], 0.0 if first else count[:, 1 - s, BLK - 1:BLK],
                                           ALU.mult, ALU.add).then_inc(count_done, 1)
                dve.wait_ge(msg_done, b + 1)
                if later(b, 1):
                    dve.wait_ge(total_done, b)
                if later(b):
                    dve.wait_ge(multiplied, b - 1)
                dve.tensor_tensor_scan(total[:, s, :], same[:, s, :], msg[:, s, :], 0.0 if first else total[:, 1 - s, BLK - 1:BLK],
                                       ALU.mult, ALU.add).then_inc(total_done, 1)
                if mean:
                    dve.wait_ge(count_done, b + 1)
                    if later(b, 1):
                        dve.wait_ge(avg_done, b)
                    dve.reciprocal(inv[:, :], count[:, s, :]).then_inc(inv_done, 1)
                    dve.wait_ge(inv_done, b + 1)
                    dve.wait_ge(total_done, b + 1)
                    dve.tensor_tensor(avg[:, s, :], total[:, s, :], inv[:, :], ALU.mult).then_inc(avg_done, 1)

            run_blocks(dve, EDGE_BLOCKS, body)

        block.__exit__(None, None, None)


def steps(eng, stages, total=NODE_BLOCKS):
    drain = max(lag for lag, _ in stages)
    first = -(-(drain + 4) // 4) * 4

    def one(n, s, turn):
        for lag, f in stages:
            if not isinstance(n, int) or 0 <= n - lag < total:
                f(*back(lag, n, s, turn))

    for n in range(first):
        one(n, n % 4, n // 4)
    rounds = (total - first) // 4
    with eng.Fori(0, rounds) as i:
        for s in range(4):
            one(i * 4 + (first + s), s, i + first // 4)
    for n in range(first + 4 * rounds, total + drain):
        one(n, n % 4, n // 4)


def attend_layer2(nc, k, source, target):
    with phase(nc, "layer2") as (sb, ps, sem):
        def two(name):
            return sb(name, [P, 2, BLK])

        xs_rows, xd_rows, xs, xd, same, y, out = (two(n) for n in ("xs_rows", "xd_rows", "xs", "xd", "same", "y", "out"))
        vs, vd, ssum, osum = (two(n) for n in ("vs", "vd", "ssum", "osum"))
        stage = sb("stage", [P, 2, 3, TB], I32)

        def one(name):
            return sb(name, [P, BLK])

        kd, dot1, dot0, self_score, reset, best = (one(n) for n in ("kd", "dot1", "dot0", "self_score", "reset", "best"))
        neg_self, weights, keep_w, pv, gv, vsum, den, inv, norm = (one(n) for n in ("neg_self", "weights", "keep_w", "pv", "gv", "vsum", "den", "inv", "norm"))
        top = sb("top", [P, 2, BLK + 1])
        gap = sb("gap", [P, 3, BLK])
        ex = sb("ex", [P, 3, BLK])
        p_s, p_d, p_qs, p_kd, p_qd, p_vs, p_vd, p_y = (ps(n, [P, 512]) for n in ("p_s", "p_d", "p_qs", "p_kd", "p_qd", "p_vs", "p_vd", "p_y"))
        index_ready, rows_used, y_ready = sem("index_ready"), sem("rows_used"), sem("y_ready")
        rows_in, sent, lines_in = ([sem(f"{n}{s}") for s in range(2)] for n in ("rows_in", "sent", "lines_in"))
        x_ready, qk_done, v_done, kd_ready, v_ready = sem("x_ready"), sem("qk_done"), sem("v_done"), sem("kd_ready"), sem("v_ready")
        dots_done, scored, self_ready = sem("dots_done"), sem("scored"), sem("self_ready")
        kd_done = sem("kd_done")
        den_done, inv_done, norm_done = sem("den_done"), sem("inv_done"), sem("norm_done")
        step, out_done, multiplied, gaps_done, ex_done = sem("step"), sem("out_done"), sem("multiplied"), sem("gaps_done"), sem("ex_done")
        p_score, p_self = p_qs, p_qd
        block = nc.Block()
        block.__enter__()

        def has_next(b):
            return not isinstance(b, int) or b + 1 < EDGE_BLOCKS

        @block.gpsimd
        def _(pool):
            edge_pool_program(pool, [(source, k.at_other[1], xs_rows), (source, k.at_key[1], xd_rows)], k.at_end[1], target, y, stage,
                              (index_ready, rows_used, rows_in, y_ready, sent))

        @block.sync
        def _(sp):
            def load(b, s, turn):
                if later(b):
                    sp.wait_ge(out_done, b - 1)
                sp.dma_start(same[:, s, :], as_row(k.same_dram[1][bass.ds(b * BLK, BLK)]).to_broadcast([P, BLK])).then_inc(lines_in[s], 16)

            run_blocks(sp, EDGE_BLOCKS, load)

        @block.tensor
        def _(pe):
            def turn_rows(b, s, turn):
                pe.wait_ge(rows_in[s], turn * (32 * TB) + 32 * TB)
                if later(b, 1):
                    pe.wait_ge(x_ready, b)
                for rows, out_ in ((xs_rows, p_s), (xd_rows, p_d)):
                    for j in range(TB):
                        ins = pe.transpose(out_[:, j * P:(j + 1) * P], rows[:, s, j * D:(j + 1) * D], k.ident[:, :])
                ins.then_inc(rows_used, 1)

            def products(b, s, turn):
                pe.wait_ge(x_ready, b + 1)
                if later(b, 1):
                    pe.wait_ge(kd_ready, b)
                pe.matmul(p_kd[:, :], k.W["Wk"], xd[:, s, :], start=True, stop=True).then_inc(kd_done, 1)
                if later(b, 1):
                    pe.wait_ge(gaps_done, b)
                pe.matmul(p_qs[:, :], k.W["Wq"], xs[:, s, :], start=True, stop=True)
                pe.matmul(p_qd[:, :], k.W["Wq"], xd[:, s, :], start=True, stop=True).then_inc(qk_done, 1)
                if later(b, 1):
                    pe.wait_ge(v_ready, b)
                pe.matmul(p_vs[:, :], k.W["Wv"], xs[:, s, :], start=True, stop=True)
                pe.matmul(p_vd[:, :], k.W["Wv"], xd[:, s, :], start=True, stop=True).then_inc(v_done, 1)
                pe.wait_ge(dots_done, b * 2 + 2)
                pe.matmul(p_score[:, :], k.head[:, :], dot1[:, :], start=True, stop=True)
                pe.matmul(p_self[:, :], k.head[:, :], dot0[:, :], start=True, stop=True).then_inc(scored, 1)

            def project(b, s):
                pe.wait_ge(out_done, b + 1)
                if later(b, 1):
                    pe.wait_ge(y_ready, b)
                for j in range(TB):
                    ins = pe.matmul(p_y[:, j * D:(j + 1) * D], out[:, s, j * P:(j + 1) * P], k.W["Wo"], start=True, stop=True)
                ins.then_inc(multiplied, 1)

            def both(b, s, turn):
                products(b, s, turn)
                if has_next(b):
                    turn_rows(b + 1, 1 - s, turn + s)
                if later(b, 1):
                    project(b - 1, 1 - s)

            turn_rows(0, 0, 0)
            run_blocks(pe, EDGE_BLOCKS, both)
            project(EDGE_BLOCKS - 1, (EDGE_BLOCKS - 1) % 2)

        @block.scalar
        def _(act):
            def keep_y(b, s, turn):
                act.wait_ge(multiplied, b + 1)
                if later(b):
                    act.wait_ge(sent[s], turn * (16 * TB))
                act.copy(y[:, s, :], p_y[:, :]).then_inc(y_ready, 1)

            def take_x(b, s):
                act.wait_ge(rows_used, b + 1)
                if later(b):
                    act.wait_ge(v_done, b - 1)
                act.copy(xs[:, s, :], p_s[:, :])
                act.copy(xd[:, s, :], p_d[:, :]).then_inc(x_ready, 1)

            def body(b, s, turn):
                act.wait_ge(kd_done, b + 1)
                if later(b, 1):
                    act.wait_ge(dots_done, b * 2)
                act.copy(kd[:, :], p_kd[:, :]).then_inc(kd_ready, 1)
                act.wait_ge(v_done, b + 1)
                if later(b):
                    act.wait_ge(out_done, b - 1)
                act.copy(vs[:, s, :], p_vs[:, :])
                act.copy(vd[:, s, :], p_vd[:, :]).then_inc(v_ready, 1)
                act.wait_ge(scored, b + 1)
                if later(b, 1):
                    act.wait_ge(gaps_done, b)
                act.mul(self_score[:, :], p_self[:, :], HID ** -0.5).then_inc(self_ready, 1)
                act.wait_ge(gaps_done, b + 1)
                if later(b, 1):
                    act.wait_ge(den_done, b)
                act.activation(ex[:, :, :].rearrange("p a c -> p (a c)"), gap[:, :, :].rearrange("p a c -> p (a c)"), ACT.Exp).then_inc(ex_done, 1)
                if has_next(b):
                    take_x(b + 1, 1 - s)
                if later(b, 1):
                    keep_y(b - 1, 1 - s, turn if s else turn - 1)

            take_x(0, 0)
            run_blocks(act, EDGE_BLOCKS, body)
            keep_y(EDGE_BLOCKS - 1, (EDGE_BLOCKS - 1) % 2, (EDGE_BLOCKS - 1) // 2)

        @block.vector
        def _(dve):
            STEPS = 15
            dve.memset(top[:, 1, BLK:BLK + 1], 0.0).then_inc(step, 1)

            def invert(b):
                dve.wait_ge(den_done, b + 1)
                if later(b, 1):
                    dve.wait_ge(norm_done, b)
                dve.reciprocal(inv[:, :], den[:, :]).then_inc(inv_done, 1)

            def finish(b, s):
                dve.wait_ge(inv_done, b + 1)
                if later(b, 1):
                    dve.wait_ge(out_done, b)
                dve.tensor_tensor(norm[:, :], osum[:, s, :], inv[:, :], ALU.mult).then_inc(norm_done, 1)
                dve.wait_ge(norm_done, b + 1)
                if later(b):
                    dve.wait_ge(multiplied, b - 1)
                dve.tensor_tensor(out[:, s, :], norm[:, :], vd[:, s, :], ALU.subtract).then_inc(out_done, 1)

            def body(b, s, turn):
                first = isinstance(b, int) and b == 0
                n = 0

                def did(ins):
                    nonlocal n
                    n += 1
                    ins.then_inc(step, 1)

                def settle():
                    dve.wait_ge(step, b * STEPS + (n + 1))

                settle()
                dve.wait_ge(kd_ready, b + 1)
                dve.wait_ge(qk_done, b + 1)
                if later(b, 1):
                    dve.wait_ge(scored, b)
                dve.tensor_tensor(dot1[:, :], p_qs[:, :], kd[:, :], ALU.mult).then_inc(dots_done, 1)
                dve.tensor_tensor(dot0[:, :], p_qd[:, :], kd[:, :], ALU.mult).then_inc(dots_done, 1)
                dve.wait_ge(lines_in[s], turn * 16 + 16)
                did(dve.tensor_scalar(reset[:, :], same[:, s, :], 1.0, BIG, ALU.subtract, ALU.mult))
                did(dve.tensor_copy(top[:, s, 0:1], top[:, 1 - s, BLK:BLK + 1]))
                if not first:
                    invert(b - 1)
                dve.wait_ge(self_ready, b + 1)
                did(dve.scalar_tensor_tensor(best[:, :], p_score[:, :], HID ** -0.5, self_score[:, :], ALU.mult, ALU.max))
                settle()
                did(dve.tensor_tensor_scan(top[:, s, 1:BLK + 1], reset[:, :], best[:, :], top[:, s, 0:1], ALU.add, ALU.max))
                settle()
                if later(b, 1):
                    dve.wait_ge(ex_done, b)
                did(dve.tensor_tensor(reset[:, :], top[:, s, 0:BLK], top[:, s, 1:BLK + 1], ALU.subtract))
                settle()
                did(dve.tensor_tensor(gap[:, 2, :], reset[:, :], same[:, s, :], ALU.mult))
                did(dve.scalar_tensor_tensor(gap[:, 0, :], p_score[:, :], HID ** -0.5, top[:, s, 1:BLK + 1], ALU.mult, ALU.subtract))
                settle()
                dve.tensor_tensor(gap[:, 1, :], self_score[:, :], top[:, s, 1:BLK + 1], ALU.subtract).then_inc(gaps_done, 1)
                if not first:
                    finish(b - 1, 1 - s)
                dve.wait_ge(ex_done, b + 1)
                did(dve.scalar_tensor_tensor(neg_self[:, :], same[:, s, :], 1.0, ex[:, 1, :], ALU.subtract, ALU.mult))
                did(dve.tensor_tensor(keep_w[:, :], ex[:, 2, :], same[:, s, :], ALU.mult))
                dve.wait_ge(v_ready, b + 1)
                did(dve.tensor_tensor(pv[:, :], ex[:, 0, :], vs[:, s, :], ALU.mult))
                settle()
                did(dve.tensor_tensor(gv[:, :], neg_self[:, :], vd[:, s, :], ALU.mult))
                did(dve.tensor_tensor(weights[:, :], ex[:, 0, :], neg_self[:, :], ALU.subtract))
                settle()
                did(dve.tensor_tensor(vsum[:, :], pv[:, :], gv[:, :], ALU.subtract))
                did(dve.tensor_tensor_scan(ssum[:, s, :], keep_w[:, :], weights[:, :], 0.0 if first else ssum[:, 1 - s, BLK - 1:BLK],
                                           ALU.mult, ALU.add))
                settle()
                did(dve.tensor_tensor_scan(osum[:, s, :], keep_w[:, :], vsum[:, :], 0.0 if first else osum[:, 1 - s, BLK - 1:BLK],
                                           ALU.mult, ALU.add))
                dve.tensor_scalar(den[:, :], ssum[:, s, :], 1e-8, None, ALU.add).then_inc(den_done, 1)
                assert n == STEPS, n
            run_blocks(dve, EDGE_BLOCKS, body)
            last = EDGE_BLOCKS - 1
            invert(last)
            finish(last, last % 2)

        block.__exit__(None, None, None)


def node_pass(nc, k, title, a_table, u, b_table=None, store=None, dense=None, residual=None, target=None):
    norm = u != "relu"
    b_table = residual if residual is not None else b_table
    gated = dense is not None and dense[0] == "gated"
    with phase(nc, title) as (sb, ps, sem):
        a, bb, v, xn, ut, yo = (sb(n, [P, 4, BLK]) for n in ("a", "b", "v", "xn", "ut", "yo"))
        stats, mv = sb("stats", [P, 4, TB, 6]), sb("mv", [P, 4, TB, 2])
        shifted, rstd, offset = (sb(n, [P, 4, TB]) for n in ("shifted", "rstd", "offset"))
        gate, prod, ot = (sb(n, [P, 2, BLK]) for n in ("gate", "prod", "ot"))
        p_t = ps("p_t", [P, 512])
        p_m = [ps(f"p_m{i}", [P, 2, 512]) for i in range(3 if gated else 1)]
        p_o = ps("p_o", [P, 512])
        a_in, b_in, u_stored, y_stored = ([sem(f"{n}{s}") for s in range(4)] for n in ("a_in", "b_in", "u_stored", "y_stored"))
        v_done, stats_done, aggr_done, shift_done, rstd_done, u_done = (sem(n) for n in ("v_done", "stats_done", "aggr_done", "shift_done", "rstd_done", "u_done"))
        offset_done = sem("offset_done")
        turned, ut_ready, multiplied, gate_ready, prod_done, ot_done, turned_out, y_done = (
            sem(n) for n in ("turned", "ut_ready", "multiplied", "gate_ready", "prod_done", "ot_done", "turned_out", "y_done"))
        v = v if u == "norm_sum" else a
        a_used = {"norm": u_done, "norm_sum": v_done, "relu": turned}[u]
        last = NODE_BLOCKS - 1
        at = 2 if norm else 0
        full = (N - last * BLK) // TB
        block = nc.Block()
        block.__enter__()

        @block.sync
        def _(sp):
            def load_a(b, s, turn):
                if later(b, 4):
                    sp.wait_ge(a_used, b - 3)
                sp.dma_start(a[:, s, :].rearrange("p (j c) -> p j c", j=TB), block_rows(a_table, b)).then_inc(a_in[s], 16)

            def load_b(b, s, turn):
                if later(b, 4):
                    sp.wait_ge(y_done if residual is not None else v_done, b - 3)
                sp.dma_start(bb[:, s, :].rearrange("p (j c) -> p j c", j=TB), block_rows(b_table, b)).then_inc(b_in[s], 16)

            def store_block(b, s, table, rows, done):
                if table.shape[0] == N and isinstance(b, int) and b == last:
                    sp.dma_start(table[b * BLK:N, :].rearrange("(p j) c -> p j c", j=TB),
                                 rows[0:full, s, :].rearrange("p (j c) -> p j c", j=TB)).then_inc(done[s], 16)
                else:
                    sp.dma_start(block_rows(table, b), rows[:, s, :].rearrange("p (j c) -> p j c", j=TB)).then_inc(done[s], 16)

            def store_u(b, s, turn):
                sp.wait_ge(u_done, b + 1)
                store_block(b, s, store, xn, u_stored)

            def store_y(b, s, turn):
                sp.wait_ge(y_done, b + 1)
                store_block(b, s, target, yo, y_stored)

            stages = [(0, load_a)]
            if b_table is not None:
                stages.append((4 if residual is not None else 0, load_b))
            if store is not None:
                stages.append((5, store_u))
            if dense is not None:
                stages.append((at + 8, store_y))
            steps(sp, stages)
            for s in range(4):
                if store is not None:
                    sp.wait_ge(u_stored[s], 16 * len(range(s, NODE_BLOCKS, 4)))
                if dense is not None:
                    sp.wait_ge(y_stored[s], 16 * len(range(s, NODE_BLOCKS, 4)))

        if norm:
            @block.gpsimd
            def _(pool):
                def rstd_of(b, s, turn):
                    pool.wait_ge(aggr_done, b * TB + TB)
                    if later(b, 4):
                        pool.wait_ge(u_done, b - 3)
                    pool.tensor_tensor(shifted[:, s, :], mv[:, s, :, 1], k.eps[:, :], ALU.add).then_inc(shift_done, 1)
                    pool.wait_ge(shift_done, b + 1)
                    pool.tensor_tensor(rstd[:, s, :], shifted[:, s, :], k.neg_half[:, :], ALU.pow).then_inc(rstd_done, 1)

                steps(pool, [(0, rstd_of)])

        @block.vector
        def _(dve):
            def statistics(b, s, turn):
                dve.wait_ge(a_in[s], turn * 16 + 16)
                if u == "norm_sum":
                    dve.wait_ge(b_in[s], turn * 16 + 16)
                    if later(b, 4):
                        dve.wait_ge(u_done, b - 3)
                    dve.scalar_tensor_tensor(v[:, s, :], a[:, s, :], 0.0, bb[:, s, :], ALU.max, ALU.add).then_inc(v_done, 1)
                    dve.wait_ge(v_done, b + 1)
                if later(b, 4):
                    dve.wait_ge(aggr_done, b * TB - 3 * TB)
                for j in range(TB):
                    dve.bn_stats(stats[:, s, j, :], v[:, s, j * D:(j + 1) * D]).then_inc(stats_done, 1)
                if later(b, 4):
                    dve.wait_ge(u_done, b - 3)
                dve.wait_ge(stats_done, b * TB + TB)
                dve.nop(nofuse=True)
                for j in range(TB):
                    dve.bn_aggr(mv[:, s, j, :], stats[:, s, j, :]).then_inc(aggr_done, 1)

            def find_offset(b, s, turn):
                dve.wait_ge(rstd_done, b + 1)
                if later(b, 4):
                    dve.wait_ge(u_done, b - 3)
                dve.scalar_tensor_tensor(offset[:, s, :], mv[:, s, :, 0], -1.0, rstd[:, s, :], ALU.mult, ALU.mult).then_inc(offset_done, 1)

            def combine(b, s, turn):
                h = s % 2
                dve.wait_ge(multiplied, b + 1)
                if later(b):
                    dve.wait_ge(turned_out, b - 1)
                if gated:
                    i = dense[1]
                    dve.wait_ge(gate_ready, b + 1)
                    if later(b):
                        dve.wait_ge(ot_done, b - 1)
                    dve.scalar_tensor_tensor(prod[:, h, :], p_m[2][:, h, :], k.col_of(f"fc{i}3_b"), gate[:, h, :], ALU.add, ALU.mult).then_inc(prod_done, 1)
                    dve.wait_ge(prod_done, b + 1)
                    dve.scalar_tensor_tensor(ot[:, h, :], p_m[0][:, h, :], k.bsum[:, i - 1:i], prod[:, h, :], ALU.add, ALU.add).then_inc(ot_done, 1)
                elif dense[3]:
                    dve.scalar_tensor_tensor(ot[:, h, :], p_m[0][:, h, :], dense[2], ut[:, s, :], ALU.add, ALU.add).then_inc(ot_done, 1)
                else:
                    dve.tensor_scalar(ot[:, h, :], p_m[0][:, h, :], dense[2], None, ALU.add).then_inc(ot_done, 1)

            def add_residual(b, s, turn):
                dve.wait_ge(turned_out, b + 1)
                dve.wait_ge(b_in[s], turn * 16 + 16)
                if later(b, 4):
                    dve.wait_ge(y_stored[s], turn * 16)
                dve.tensor_tensor(yo[:, s, :], p_o[:, :], bb[:, s, :], ALU.add).then_inc(y_done, 1)

            stages = [(0, statistics)] if norm else []
            if dense is not None:
                stages.append((at + 2, combine))
            if norm:
                stages.insert(0 if gated else len(stages), (1, find_offset))
            if residual is not None:
                stages.insert(0, (at + 4, add_residual))
            steps(dve, stages)

        @block.scalar
        def _(act):
            def normalise(b, s, turn):
                act.wait_ge(offset_done, b + 1)
                if later(b, 4):
                    if store is not None:
                        act.wait_ge(u_stored[s], turn * 16)
                    if dense is not None:
                        act.wait_ge(turned, b - 3)
                for j in range(TB):
                    ins = act.activation(xn[:, s, j * D:(j + 1) * D], v[:, s, j * D:(j + 1) * D], ACT.Identity,
                                         bias=offset[:, s, j:j + 1], scale=rstd[:, s, j:j + 1])
                ins.then_inc(u_done, 1)

            def take_u(b, s, turn):
                act.wait_ge(turned, b + 1)
                if later(b, 4):
                    act.wait_ge(multiplied, b - 3)
                    act.wait_ge(ot_done, b - 3)
                if norm:
                    act.copy(ut[:, s, :], p_t[:, :]).then_inc(ut_ready, 1)
                else:
                    act.activation(ut[:, s, :], p_t[:, :], ACT.Relu).then_inc(ut_ready, 1)

            def keep_gate(b, s, turn):
                h = s % 2
                act.wait_ge(multiplied, b + 1)
                if later(b):
                    act.wait_ge(prod_done, b - 1)
                act.activation(gate[:, h, :], p_m[1][:, h, :], ACT.Identity, bias=k.col_of(f"fc{dense[1]}2_b")).then_inc(gate_ready, 1)

            def keep_y(b, s, turn):
                act.wait_ge(turned_out, b + 1)
                if later(b, 4):
                    act.wait_ge(y_stored[s], turn * 16)
                act.copy(yo[:, s, :], p_o[:, :]).then_inc(y_done, 1)

            stages = [(at, take_u)] if dense is not None else []
            if gated:
                stages.append((at + 1, keep_gate))
            if norm:
                stages.insert(0, (1, normalise))
            if dense is not None and residual is None:
                stages.append((at + 3, keep_y))
            steps(act, stages)

        if dense is not None:
            @block.tensor
            def _(pe):
                def turn_in(b, s, turn):
                    if norm:
                        pe.wait_ge(u_done, b + 1)
                    else:
                        pe.wait_ge(a_in[s], turn * 16 + 16)
                    if later(b, 1):
                        pe.wait_ge(ut_ready, b)
                    rows = xn if norm else a
                    for j in range(TB):
                        ins = pe.transpose(p_t[:, j * P:(j + 1) * P], rows[:, s, j * D:(j + 1) * D], k.ident[:, :])
                    ins.then_inc(turned, 1)

                def multiply(b, s, turn):
                    h = s % 2
                    pe.wait_ge(ut_ready, b + 1)
                    if later(b):
                        pe.wait_ge(ot_done, b - 1)
                    if gated:
                        for m in (1, 2, 0):
                            ins = pe.matmul(p_m[m][:, h, :], k.W[f"fc{dense[1]}{m + 1}"], ut[:, s, :], start=True, stop=True)
                    else:
                        ins = pe.matmul(p_m[0][:, h, :], dense[1], ut[:, s, :], start=True, stop=True)
                    ins.then_inc(multiplied, 1)

                def turn_out(b, s, turn):
                    h = s % 2
                    pe.wait_ge(ot_done, b + 1)
                    if later(b, 1):
                        pe.wait_ge(y_done, b)
                    for j in range(TB):
                        ins = pe.transpose(p_o[:, j * D:(j + 1) * D], ot[:, h, j * P:(j + 1) * P], k.ident[:, :])
                    ins.then_inc(turned_out, 1)

                steps(pe, [(at, turn_in), (at + 1, multiply), (at + 3, turn_out)])

        block.__exit__(None, None, None)


def ffn_pass(nc, k, sum_table, x_table, store, weight, bias, target):
    with phase(nc, "ffn") as (sb, ps, sem):
        def two(name):
            return sb(name, [P, 2, BLK])

        a, xb = (sb(n, [P, 4, BLK]) for n in ("a", "xb"))
        xn, xt, yt, zn, zg, v, x3, ut, ot, yo = (two(n) for n in ("xn", "xt", "yt", "zn", "zg", "v", "x3", "ut", "ot", "yo"))
        hidden = sb("hidden", [P, 4, BLK])
        xplus = two("xplus")
        g2_block, b2_block = sb("g2_block", [P, BLK]), sb("b2_block", [P, BLK])
        stats = [sb(f"stats{i}", [P, 2, TB, 6]) for i in range(3)]
        mv = [sb(f"mv{i}", [P, 2, TB, 2]) for i in range(3)]
        shifted, rstd = [sb(f"shifted{i}", [P, 2, TB]) for i in range(3)], [sb(f"rstd{i}", [P, 2, TB]) for i in range(3)]
        p_t, p_h, p_f, p_z, p_u = ps("p_t", [P, 512]), ps("p_h", [P, 2, 512]), ps("p_f", [P, 512]), ps("p_z", [P, 2, 512]), ps("p_u", [P, 512])
        p_m = ps("p_m", [P, 512])
        a_in, x_in = ([sem(f"{n}{s}") for s in range(4)] for n in ("a_in", "x_in"))
        u_stored, y_stored = ([sem(f"{n}{s}") for s in range(2)] for n in ("u_stored", "y_stored"))
        stats_done, aggr_done, shift_done, rstd_done = ([sem(f"{n}{i}") for i in range(3)] for n in ("stats_done", "aggr_done", "shift_done", "rstd_done"))
        tiled, xn_done, turned, xt_ready, h_done, gelu_done, f_done, yt_done = (
            sem(n) for n in ("tiled", "xn_done", "turned", "xt_ready", "h_done", "gelu_done", "f_done", "yt_done"))
        z_turned, zn_done, zg_done, xplus_done, v_done, x3_done, u_turned, ut_ready = (
            sem(n) for n in ("z_turned", "zn_done", "zg_done", "xplus_done", "v_done", "x3_done", "u_turned", "ut_ready"))
        multiplied, ot_done, turned_out, y_done = (sem(n) for n in ("multiplied", "ot_done", "turned_out", "y_done"))
        last = NODE_BLOCKS - 1
        block = nc.Block()
        block.__enter__()

        @block.sync
        def _(sp):
            def load(b, s, turn):
                if later(b, 4):
                    sp.wait_ge(xn_done, b - 3)
                sp.dma_start(a[:, s, :].rearrange("p (j c) -> p j c", j=TB), block_rows(sum_table, b)).then_inc(a_in[s], 16)
                if later(b, 4):
                    sp.wait_ge(xplus_done, b - 3)
                sp.dma_start(xb[:, s, :].rearrange("p (j c) -> p j c", j=TB), block_rows(x_table, b)).then_inc(x_in[s], 16)

            def store_x3(b, s, turn):
                sp.wait_ge(x3_done, b + 1)
                sp.dma_start(block_rows(store, b), x3[:, s % 2, :].rearrange("p (j c) -> p j c", j=TB)).then_inc(u_stored[s % 2], 16)

            def store_y(b, s, turn):
                sp.wait_ge(y_done, b + 1)
                sp.dma_start(block_rows(target, b), yo[:, s % 2, :].rearrange("p (j c) -> p j c", j=TB)).then_inc(y_stored[s % 2], 16)

            steps(sp, [(0, load), (6, store_x3), (7, store_y)])
            for s in range(2):
                n = 16 * len(range(s, NODE_BLOCKS, 2))
                sp.wait_ge(u_stored[s], n)
                sp.wait_ge(y_stored[s], n)

        @block.gpsimd
        def _(pool):
            def rstd_of(i, used):
                def f(b, s, turn):
                    pool.wait_ge(aggr_done[i], b * TB + TB)
                    if later(b):
                        pool.wait_ge(used, b - 1)
                    pool.tensor_tensor(shifted[i][:, s % 2, :], mv[i][:, s % 2, :, 1], k.eps[:, :], ALU.add).then_inc(shift_done[i], 1)
                    pool.wait_ge(shift_done[i], b + 1)
                    pool.tensor_tensor(rstd[i][:, s % 2, :], shifted[i][:, s % 2, :], k.neg_half[:, :], ALU.pow).then_inc(rstd_done[i], 1)
                return f

            def x_plus_b2(b, s, turn):
                pool.wait_ge(x_in[s], turn * 16 + 16)
                if later(b):
                    pool.wait_ge(v_done, b - 1)
                pool.tensor_tensor(xplus[:, s % 2, :], xb[:, s, :], b2_block[:, :], ALU.add).then_inc(xplus_done, 1)

            pool.wait_ge(tiled, 2 * TB)
            steps(pool, [(1, x_plus_b2), (0, rstd_of(0, xn_done)), (2, rstd_of(1, zn_done)), (2, rstd_of(2, x3_done))])

        @block.vector
        def _(dve):
            for j in range(TB):
                dve.tensor_copy(g2_block[:, j * D:(j + 1) * D], k.g2[:, :]).then_inc(tiled, 1)
                dve.tensor_copy(b2_block[:, j * D:(j + 1) * D], k.b2[:, :]).then_inc(tiled, 1)
            dve.wait_ge(tiled, 2 * TB)

            def statistics(i, b, s, rows, used):
                if later(b):
                    dve.wait_ge(aggr_done[i], b * TB - TB)
                for j in range(TB):
                    dve.bn_stats(stats[i][:, s % 2, j, :], rows[:, j * D:(j + 1) * D]).then_inc(stats_done[i], 1)
                if later(b):
                    dve.wait_ge(used, b - 1)
                dve.wait_ge(stats_done[i], b * TB + TB)
                dve.nop(nofuse=True)
                for j in range(TB):
                    dve.bn_aggr(mv[i][:, s % 2, j, :], stats[i][:, s % 2, j, :]).then_inc(aggr_done[i], 1)

            def normalise(i, b, s, out_, rows, done):
                dve.wait_ge(rstd_done[i], b + 1)
                for j in range(TB):
                    ins = dve.tensor_scalar(out_[:, j * D:(j + 1) * D], rows[:, j * D:(j + 1) * D], mv[i][:, s % 2, j, 0:1], rstd[i][:, s % 2, j:j + 1],
                                            ALU.subtract, ALU.mult)
                ins.then_inc(done, 1)

            def stage_a1(b, s, turn):
                dve.wait_ge(a_in[s], turn * 16 + 16)
                statistics(0, b, s, a[:, s], xn_done)

            def stage_a2(b, s, turn):
                if later(b):
                    dve.wait_ge(turned, b - 1)
                normalise(0, b, s, xn[:, s % 2], a[:, s], xn_done)

            def stage_a3(b, s, turn):
                dve.wait_ge(f_done, b + 1)
                if later(b):
                    dve.wait_ge(z_turned, b - 1)
                dve.scalar_tensor_tensor(yt[:, s % 2, :], p_f[:, :], k.col_of("bf2"), xt[:, s % 2, :], ALU.add, ALU.add).then_inc(yt_done, 1)

            def stage_b1(b, s, turn):
                dve.wait_ge(z_turned, b + 1)
                statistics(1, b, s, p_z[:, s % 2], zn_done)

            def stage_b2(b, s, turn):
                if later(b):
                    dve.wait_ge(zg_done, b - 1)
                normalise(1, b, s, zn[:, s % 2], p_z[:, s % 2], zn_done)
                dve.wait_ge(zn_done, b + 1)
                if later(b):
                    dve.wait_ge(v_done, b - 1)
                dve.tensor_tensor(zg[:, s % 2, :], zn[:, s % 2, :], g2_block[:, :], ALU.mult).then_inc(zg_done, 1)
                dve.wait_ge(zg_done, b + 1)
                dve.wait_ge(xplus_done, b + 1)
                if later(b):
                    dve.wait_ge(x3_done, b - 1)
                dve.tensor_tensor(v[:, s % 2, :], zg[:, s % 2, :], xplus[:, s % 2, :], ALU.add).then_inc(v_done, 1)
                dve.wait_ge(v_done, b + 1)
                statistics(2, b, s, v[:, s % 2], x3_done)

            def stage_b3(b, s, turn):
                if later(b):
                    dve.wait_ge(u_stored[s % 2], turn * 32 + s // 2 * 16)
                    dve.wait_ge(u_turned, b - 1)
                normalise(2, b, s, x3[:, s % 2], v[:, s % 2], x3_done)

            steps(dve, [(0, stage_a1), (3, stage_b3), (2, stage_b1), (0, stage_a2), (2, stage_b2), (1, stage_a3)])

        @block.tensor
        def _(pe):
            def turn_in(b, s, turn):
                pe.wait_ge(xn_done, b + 1)
                if later(b, 1):
                    pe.wait_ge(xt_ready, b)
                for j in range(TB):
                    ins = pe.transpose(p_t[:, j * P:(j + 1) * P], xn[:, s % 2, j * D:(j + 1) * D], k.ident[:, :])
                ins.then_inc(turned, 1)

            def ffn(b, s, turn):
                pe.wait_ge(xt_ready, b + 1)
                for c in range(4):
                    if c >= 2 or later(b, 1):
                        pe.wait_ge(gelu_done, b * 4 + (c - 1))
                    pe.matmul(p_h[:, c % 2, :], k.W["Wf1"][:, c * D:(c + 1) * D], xt[:, s % 2, :], start=True, stop=True).then_inc(h_done, 1)
                    if c >= 1:
                        second(b, c - 1)
                second(b, 3).then_inc(f_done, 1)

            def second(b, c):
                pe.wait_ge(gelu_done, b * 4 + (c + 1))
                if c == 0 and later(b, 1):
                    pe.wait_ge(yt_done, b)
                return pe.matmul(p_f[:, :], k.W["Wf2"][:, c, :], hidden[:, c, :], start=c == 0, stop=c == 3)

            def turn_z(b, s, turn):
                pe.wait_ge(yt_done, b + 1)
                if later(b):
                    pe.wait_ge(zn_done, b - 1)
                for j in range(TB):
                    ins = pe.transpose(p_z[:, s % 2, j * D:(j + 1) * D], yt[:, s % 2, j * P:(j + 1) * P], k.ident[:, :])
                ins.then_inc(z_turned, 1)

            def turn_u(b, s, turn):
                pe.wait_ge(x3_done, b + 1)
                if later(b):
                    pe.wait_ge(y_done, b - 1)
                for j in range(TB):
                    ins = pe.transpose(p_u[:, j * P:(j + 1) * P], x3[:, s % 2, j * D:(j + 1) * D], k.ident[:, :])
                ins.then_inc(u_turned, 1)

            def last_product(b, s, turn):
                pe.wait_ge(ut_ready, b + 1)
                if later(b, 1):
                    pe.wait_ge(ot_done, b)
                pe.matmul(p_m[:, :], weight, ut[:, s % 2, :], start=True, stop=True).then_inc(multiplied, 1)

            def turn_y(b, s, turn):
                pe.wait_ge(ot_done, b + 1)
                if later(b, 1):
                    pe.wait_ge(y_done, b)
                for j in range(TB):
                    ins = pe.transpose(p_u[:, j * D:(j + 1) * D], ot[:, s % 2, j * P:(j + 1) * P], k.ident[:, :])
                ins.then_inc(turned_out, 1)

            steps(pe, [(1, ffn), (0, turn_in), (3, turn_u), (1, turn_z), (3, last_product), (4, turn_y)])

        @block.scalar
        def _(act):
            def take_x(b, s, turn):
                act.wait_ge(turned, b + 1)
                if later(b):
                    act.wait_ge(yt_done, b - 1)
                act.activation(xt[:, s % 2, :], p_t[:, :], ACT.Identity, scale=k.col_of("g1"), bias=k.col_of("b1")).then_inc(xt_ready, 1)

            def gelus(b, s, turn):
                for c in range(4):
                    act.wait_ge(h_done, b * 4 + (c + 1))
                    if later(b, 1):
                        act.wait_ge(f_done, b)
                    act.activation(hidden[:, c, :], p_h[:, c % 2, :], ACT.Gelu, bias=k.col_of(f"bf1_{c}")).then_inc(gelu_done, 1)

            def take_u(b, s, turn):
                act.wait_ge(u_turned, b + 1)
                if later(b):
                    act.wait_ge(multiplied, b - 1)
                act.copy(ut[:, s % 2, :], p_u[:, :]).then_inc(ut_ready, 1)

            def keep_y(b, s, turn):
                act.wait_ge(turned_out, b + 1)
                if later(b):
                    act.wait_ge(y_stored[s % 2], turn * 32 + s // 2 * 16)
                act.copy(yo[:, s % 2, :], p_u[:, :]).then_inc(y_done, 1)

            def add_bias(b, s, turn):
                act.wait_ge(multiplied, b + 1)
                if later(b):
                    act.wait_ge(turned_out, b - 1)
                act.activation(ot[:, s % 2, :], p_m[:, :], ACT.Identity, bias=bias).then_inc(ot_done, 1)

            steps(act, [(1, gelus), (0, take_x), (3, take_u), (3, add_bias), (4, keep_y)])

        block.__exit__(None, None, None)


VECTORS = ["fc11_b", "conv1_b", "fc12_b", "fc13_b", "fc21_b", "conv2_b", "fc22_b", "fc23_b", "bo", "bf2", "g1", "b1",
           "b0_3", "b1_3", "b2_3", "bf1_0", "bf1_1", "bf1_2", "bf1_3", "attL", "attR"]


def build(nc, a, out):
    k = Kit()
    w = {
        "fc11": a["L1_gnn_fc11_w"], "fc12": a["L1_gnn_fc12_w"], "fc13": a["L1_gnn_fc13_w"], "conv1": a["L1_gnn_conv1_w"],
        "fc21": a["L1_gnn_fc21_w"], "fc22": a["L1_gnn_fc22_w"], "fc23": a["L1_gnn_fc23_w"], "conv2": a["L1_gnn_conv2_w"],
        "Wq": a["L2_gnn_Wq"], "Wk": a["L2_gnn_Wk"], "Wv": a["L2_gnn_Wv"], "Wo": a["L2_gnn_Wo"], "Wf1": a["L2_gnn_Wf1"],
        "Wf2": a["L2_gnn_Wf2"], "W0": a["L0_gnn_W"],
        "Ws0": a["L3_gnn_Ws0"], "Wn0": a["L3_gnn_Wn0"], "Ws1": a["L3_gnn_Ws1"], "Wn1": a["L3_gnn_Wn1"],
        "Ws2": a["L3_gnn_Ws2"], "Wn2": a["L3_gnn_Wn2"], "g2": a["L2_gnn_g2"], "b2": a["L2_gnn_b2"],
        "fc11_b": a["L1_gnn_fc11_b"], "conv1_b": a["L1_gnn_conv1_b"], "fc12_b": a["L1_gnn_fc12_b"], "fc13_b": a["L1_gnn_fc13_b"],
        "fc21_b": a["L1_gnn_fc21_b"], "conv2_b": a["L1_gnn_conv2_b"], "fc22_b": a["L1_gnn_fc22_b"], "fc23_b": a["L1_gnn_fc23_b"],
        "bo": a["L2_gnn_bo"], "bf2": a["L2_gnn_bf2"], "g1": a["L2_gnn_g1"], "b1": a["L2_gnn_b1"],
        "b0_3": a["L3_gnn_b0"], "b1_3": a["L3_gnn_b1"], "b2_3": a["L3_gnn_b2"],
        "attL": a["L0_gnn_att"][:, :, 0:HID], "attR": a["L0_gnn_att"][:, :, HID:2 * HID],
    }
    for c in range(4):
        w[f"bf1_{c}"] = a["L2_gnn_bf1"][c * D:(c + 1) * D]
    k.vec_names = VECTORS

    def dram(name, shape, dt=F32):
        return nc.dram_tensor(name, shape, dt).ap()

    k.key_dram = [dram(f"keys{i}", (EPAD,), I32) for i in range(2)]
    k.oth_dram = [dram(f"others{i}", (EPAD,), I32) for i in range(2)]
    k.w_dram = dram("edge_weights", (EPAD,))
    k.sorted_dram = [dram(f"sorted{i}", (EPAD + 2, 4)) for i in range(2)]
    k.same_dram = [dram(f"same{i}", (EPAD,)) for i in range(2)]
    k.weight_dram = [dram(f"weight{i}", (EPAD,)) for i in range(2)]
    k.nv_dram = [dram(f"nv{i}", (EPAD,)) for i in range(2)]
    k.table = [dram(f"table{i}", (ROWS, D)) for i in range(2)]
    k.x1, k.x2, k.x3 = (dram(n, (NPAD, D)) for n in ("x1", "x2", "x3"))

    with ExitStack() as ctx:
        def sb(name, shape, dt=F32):
            return ctx.enter_context(nc.sbuf_tensor(name, shape, dt))

        k.W = {}
        squares = ["fc11", "fc12", "fc13", "conv1", "fc21", "fc22", "fc23", "conv2", "Wq", "Wk", "Wv", "Wo", "W0T", "Ws0T", "Wn0T",
                   "Ws1T", "Wn1T", "Ws2T", "Wn2T", "WvT", "attLW", "attRW", "Wvo"]
        all_w = sb("all_w", [P, len(squares), D])
        for i, name in enumerate(squares):
            k.W[name] = all_w[:, i, :]
        k.W["Wf1"] = sb("Wf1", [P, 4 * D])[:, :]
        k.W["Wf2"] = sb("Wf2", [P, 4, D])[:, :, :]
        k.vec = sb("vec", [P, len(VECTORS)])
        k.bsum = sb("bsum", [P, 2])
        k.g2, k.b2 = sb("g2", [P, D]), sb("b2", [P, D])
        k.ident, k.ident16 = sb("ident", [P, P]), sb("ident16", [P, P], F16)
        k.before, k.above, k.head = sb("before", [P, P]), sb("above", [P, P]), sb("head_mask", [P, P])
        k.row_iota, k.col_iota = sb("row_iota", [P, P], F16), sb("col_iota", [P, NCOL], F16)
        k.neg_half, k.eps = sb("neg_half", [P, TB]), sb("eps", [P, TB])
        k.ones = sb("ones", [P, NCOL])
        k.at_key = [sb(f"at_key{i}", [P, TILES], I32) for i in range(2)]
        k.at_other = [sb(f"at_other{i}", [P, TILES], I32) for i in range(2)]
        k.at_end = [sb(f"at_end{i}", [P, TILES], I32) for i in range(2)]
        k.payload = [sb(f"payload{i}", [P, TILES, 4]) for i in range(2)]
        k.col_of = lambda name: k.vec[:, VECTORS.index(name):VECTORS.index(name) + 1]

        setup(nc, k, a["src"], a["dst"], a["edge_weight1"], w)
        sort_edges(nc, k, a["x"], a["node_vec"])
        for which in range(2):
            sorted_lists(nc, k, which)
        first, second = k.table
        col = k.col_of
        attend_layer0(nc, k, a["x"])
        node_pass(nc, k, "own1", first, "norm", store=k.x1, dense=("gated", 1), target=second)
        aggregate(nc, k, "conv1", k.x1, second, k.W["conv1"], relu=False, mean=False)
        node_pass(nc, k, "own2", second, "relu", dense=("gated", 2), target=first)
        aggregate(nc, k, "conv2", second, first, k.W["conv2"], relu=True, mean=False)
        node_pass(nc, k, "value", first, "norm_sum", b_table=k.x1, store=k.x2, dense=("linear", k.W["Wvo"], col("bo"), True), target=second)
        attend_layer2(nc, k, k.x2, second)
        ffn_pass(nc, k, second, k.x2, k.x3, k.W["Ws0T"], col("b0_3"), first)
        aggregate(nc, k, "sage0", k.x3, first, k.W["Wn0T"], relu=False, mean=True)
        node_pass(nc, k, "own4", first, "relu", dense=("linear", k.W["Ws1T"], col("b1_3"), True), target=second)
        aggregate(nc, k, "sage1", first, second, k.W["Wn1T"], relu=True, mean=True)
        node_pass(nc, k, "own5", second, "relu", dense=("linear", k.W["Ws2T"], col("b2_3"), False), residual=k.x3, target=first)
        aggregate(nc, k, "sage2", second, first, k.W["Wn2T"], relu=True, mean=True)
        node_pass(nc, k, "last", first, "norm", store=out)


_INS = ["x", "src", "dst", "edge_weight1", "node_vec", "L0_gnn_W", "L0_gnn_att"] \
    + [f"L1_gnn_{n}_{t}" for n in ("fc11", "fc12", "fc13", "conv1", "fc21", "fc22", "fc23", "conv2") for t in "wb"] \
    + [f"L2_gnn_{n}" for n in ("Wq", "Wk", "Wv", "Wo", "bo", "Wf1", "bf1", "Wf2", "bf2", "g1", "b1", "g2", "b2")] \
    + [f"L3_gnn_{n}{i}" for i in range(3) for n in ("Ws", "Wn", "b")]


def kernel(**inputs):
    import numpy as _np
    import concourse.bacc as _bacc
    from concourse import mybir as _mybir
    from concourse.bass_utils import run_bass_kernel_spmd as _run

    nc = _bacc.Bacc("TRN2", target_bir_lowering=False, num_devices=1)
    arrays, args = {}, {}
    for name in _INS:
        v = _np.ascontiguousarray(inputs[name])
        arrays[f"in_{name}"] = v
        args[name] = nc.dram_tensor(f"in_{name}", v.shape, _mybir.dt.from_np(v.dtype), kind="ExternalInput").ap()
    out = nc.dram_tensor("out_0", (N, D), _mybir.dt.float32, kind="ExternalOutput").ap()
    build(nc, args, out)
    r = _run(nc, [arrays], core_ids=[0])
    return r.results[0]["out_0"]
```
